# Optimizing a Trainium2 kernel written in Bass

```python
import numpy as np
import jax
import jax.numpy as jnp

def _softmax(x, axis=-1):
    return jax.nn.softmax(x, axis=axis)

def _gelu(x):
    return jax.nn.gelu(x, approximate=True)

def _silu(x):
    return jax.nn.silu(x)

def _sigmoid(x):
    return jax.nn.sigmoid(x)

def _layernorm(x, axis=-1, eps=1e-05):
    m = jnp.mean(x, axis=axis, keepdims=True)
    v = jnp.var(x, axis=axis, keepdims=True)
    return (x - m) / jnp.sqrt(v + eps)

def _scatter_add(tgt, idx, src, axis=0):
    return tgt.at[idx].add(src)

def _segment_sum(src, seg, n):
    return jax.ops.segment_sum(src, seg, n)
kernel_name = 'mk_adj_ffn_d2_adj_r2_9a37ca'

def setup_inputs(seed: int=0):
    np.random.seed(seed)
    _w = jnp.asarray

    def _rec_inputs():
        import jax
        import jax.numpy as jnp
        _gk = jax.random.key(seed)
        x = -0.0005207 + 1.001 * jax.random.normal(jax.random.fold_in(_gk, 1), (4096, 128), jnp.float32)
        _w = (1.0 + jnp.arange(4096, dtype=jnp.float32)) ** (-0.5)
        _w = _w / _w.mean()
        _pij = jnp.clip(0.00195312 * _w[:, None] * _w[None, :], 0.0, 1.0)
        _a = jax.random.uniform(jax.random.fold_in(_gk, 2), (4096, 4096)) < _pij
        _a = jnp.logical_or(_a, jnp.eye(4096, dtype=bool))
        _af = _a.astype(jnp.float32)
        _af = _af * jax.random.uniform(jax.random.fold_in(_gk, 3), (4096, 4096), jnp.float32, 0.05, 1)
        adj = _af
        return (x, adj)
    x, adj = _rec_inputs()

    def _L0_gnn_setup():
        import jax, jax.numpy as jnp
        import numpy as np
        N = 4096
        D = 128
        L = 3

        def _cxin_conv(x, a, eps, W, b):
            ax = a @ x
            h = ax + (1.0 + eps[0]) * ax
            for i in range(L):
                h = jax.nn.relu(h @ W[i].T + b[i])
            return h
        key = jax.random.key(seed)
        ks = jax.random.split(key, 8)
        s = 1.0 / np.sqrt(D)
        return {'x1': jax.random.normal(ks[0], (N, D), jnp.float32), 'x2': jax.random.normal(ks[1], (N, D), jnp.float32), 'G1': jax.random.uniform(ks[2], (N, N), jnp.float32), 'G2': jax.random.uniform(ks[3], (N, N), jnp.float32), 'eps1': jnp.zeros((1,), jnp.float32), 'eps2': jnp.zeros((1,), jnp.float32), 'W1': jax.random.normal(ks[4], (L, D, D), jnp.float32) * s, 'b1': jnp.zeros((L, D), jnp.float32), 'W2': jax.random.normal(ks[5], (L, D, D), jnp.float32) * s, 'b2': jnp.zeros((L, D), jnp.float32), 'Wm': jax.random.normal(ks[6], (D, 2 * D), jnp.float32) * (1.0 / np.sqrt(2 * D)), 'bm': jnp.zeros((D,), jnp.float32)}
    _L0_gnn_all = _L0_gnn_setup()
    _L0_gnn_in = {k: v for k, v in _L0_gnn_all.items() if k in ('x2', 'eps1', 'eps2', 'W1', 'b1', 'W2', 'b2', 'Wm', 'bm')}
    del _L0_gnn_all

    def _L0_ffn_setup():
        import jax, jax.numpy as jnp
        import numpy as np
        D_MODEL = 128
        N_EXPERTS = 16
        HIDDEN = 256
        SCALE = 0.02
        key = jax.random.key(seed)
        ks = jax.random.split(key, 5)
        x = jax.random.normal(ks[0], (4, 4096, D_MODEL), dtype=jnp.float32)
        gate_w = jax.random.normal(ks[1], (D_MODEL, N_EXPERTS), dtype=jnp.float32) * SCALE
        gate_b = jnp.zeros((N_EXPERTS,), dtype=jnp.float32)
        w1 = jax.random.normal(ks[2], (N_EXPERTS, D_MODEL, HIDDEN), dtype=jnp.float32) * SCALE
        w2 = jax.random.normal(ks[3], (N_EXPERTS, D_MODEL, HIDDEN), dtype=jnp.float32) * SCALE
        w3 = jax.random.normal(ks[4], (N_EXPERTS, HIDDEN, D_MODEL), dtype=jnp.float32) * SCALE
        return {'x': x, 'gate_w': gate_w, 'gate_b': gate_b, 'w1': w1, 'w2': w2, 'w3': w3}
    _L0_ffn_all = _L0_ffn_setup()
    _L0_ffn_in = {k: v for k, v in _L0_ffn_all.items() if k in ('gate_w', 'gate_b', 'w1', 'w2', 'w3')}
    del _L0_ffn_all

    def _L1_gnn_setup():
        import jax, jax.numpy as jnp
        import numpy as np
        N = 4096
        F = 128
        NEG_INF = -9000000000000000.0
        ALPHA = 0.2
        THRESH = 1e-06
        key = jax.random.key(seed)
        k1, k2, k3, k4 = jax.random.split(key, 4)
        x = jax.random.normal(k1, (N, F), jnp.float32)
        h0 = jax.random.normal(k2, (N, F), jnp.float32)
        limit = float(np.sqrt(6.0 / (2 * F + 1)) * 1.414)
        a = jax.random.uniform(k3, (2 * F, 1), jnp.float32, -limit, limit)
        temp = jnp.zeros((5,), jnp.float32)
        adj = jax.random.bernoulli(k4, 0.005, (N, N)).astype(jnp.float32)
        adj = jnp.maximum(adj, jnp.eye(N, dtype=jnp.float32))
        return {'x': x, 'h0': h0, 'a': a, 'temp': temp, 'adj': adj, 'l': 1}
    _L1_gnn_all = _L1_gnn_setup()
    _L1_gnn_in = {k: v for k, v in _L1_gnn_all.items() if k in ('h0', 'a', 'temp')}
    del _L1_gnn_all

    def _L1_ffn_setup():
        import jax, jax.numpy as jnp
        import numpy as np
        B, S, H, F, E, K = (8, 2048, 128, 256, 16, 2)
        EPS = 1e-05
        key = jax.random.key(seed)
        ks = jax.random.split(key, 9)
        sc = 0.02
        return {'x': jax.random.normal(ks[0], (B, S, H), dtype=jnp.float32), 'gate_w': jax.random.normal(ks[1], (H, E), dtype=jnp.float32) * sc, 'gate_b': jnp.zeros((E,), dtype=jnp.float32), 'w1': jax.random.normal(ks[2], (E, H, F), dtype=jnp.float32) * sc, 'b1': jnp.zeros((E, F), dtype=jnp.float32), 'w2': jax.random.normal(ks[3], (E, F, H), dtype=jnp.float32) * sc, 'b2': jnp.zeros((E, H), dtype=jnp.float32), 'gamma': jnp.ones((H,), dtype=jnp.float32), 'beta': jnp.zeros((H,), dtype=jnp.float32)}
    _L1_ffn_all = _L1_ffn_setup()
    _L1_ffn_in = {k: v for k, v in _L1_ffn_all.items() if k in ('gate_w', 'gate_b', 'w1', 'b1', 'w2', 'b2', 'gamma', 'beta')}
    del _L1_ffn_all
    return {'x': x, 'adj': adj, 'L0_gnn_x2': _L0_gnn_in['x2'], 'L0_gnn_eps1': _L0_gnn_in['eps1'], 'L0_gnn_eps2': _L0_gnn_in['eps2'], 'L0_gnn_W1': _L0_gnn_in['W1'], 'L0_gnn_b1': _L0_gnn_in['b1'], 'L0_gnn_W2': _L0_gnn_in['W2'], 'L0_gnn_b2': _L0_gnn_in['b2'], 'L0_gnn_Wm': _L0_gnn_in['Wm'], 'L0_gnn_bm': _L0_gnn_in['bm'], 'L0_ffn_gate_w': _L0_ffn_in['gate_w'], 'L0_ffn_gate_b': _L0_ffn_in['gate_b'], 'L0_ffn_w1': _L0_ffn_in['w1'], 'L0_ffn_w2': _L0_ffn_in['w2'], 'L0_ffn_w3': _L0_ffn_in['w3'], 'L1_gnn_h0': _L1_gnn_in['h0'], 'L1_gnn_a': _L1_gnn_in['a'], 'L1_gnn_temp': _L1_gnn_in['temp'], 'L1_ffn_gate_w': _L1_ffn_in['gate_w'], 'L1_ffn_gate_b': _L1_ffn_in['gate_b'], 'L1_ffn_w1': _L1_ffn_in['w1'], 'L1_ffn_b1': _L1_ffn_in['b1'], 'L1_ffn_w2': _L1_ffn_in['w2'], 'L1_ffn_b2': _L1_ffn_in['b2'], 'L1_ffn_gamma': _L1_ffn_in['gamma'], 'L1_ffn_beta': _L1_ffn_in['beta']}

def reference(x, adj, L0_gnn_x2, L0_gnn_eps1, L0_gnn_eps2, L0_gnn_W1, L0_gnn_b1, L0_gnn_W2, L0_gnn_b2, L0_gnn_Wm, L0_gnn_bm, L0_ffn_gate_w, L0_ffn_gate_b, L0_ffn_w1, L0_ffn_w2, L0_ffn_w3, L1_gnn_h0, L1_gnn_a, L1_gnn_temp, L1_ffn_gate_w, L1_ffn_gate_b, L1_ffn_w1, L1_ffn_b1, L1_ffn_w2, L1_ffn_b2, L1_ffn_gamma, L1_ffn_beta):
    import jax
    import jax.numpy as jnp

    def _L0_gnn_ref(x1, x2, G1, G2, eps1, eps2, W1, b1, W2, b2, Wm, bm):
        import jax, jax.numpy as jnp
        import numpy as np
        N = 4096
        D = 128
        L = 3

        def _cxin_conv(x, a, eps, W, b):
            ax = a @ x
            h = ax + (1.0 + eps[0]) * ax
            for i in range(L):
                h = jax.nn.relu(h @ W[i].T + b[i])
            return h
        out1 = _cxin_conv(x1, G1, eps1, W1, b1)
        out2 = _cxin_conv(x2, G2, eps2, W2, b2)
        merged = jnp.concatenate((out1, out2), axis=1)
        return merged @ Wm.T + bm

    def _L0_ffn_ref(x, gate_w, gate_b, w1, w2, w3):
        import jax, jax.numpy as jnp
        import numpy as np
        D_MODEL = 128
        N_EXPERTS = 16
        HIDDEN = 256
        SCALE = 0.02
        n_experts = w1.shape[0]
        logits = jnp.einsum('bsd,de->bse', x, gate_w) + gate_b
        probs = jax.nn.softmax(logits, axis=-1)
        top_probs, top_idx = jax.lax.top_k(probs, 2)
        top_probs = top_probs / jnp.sum(top_probs, axis=-1, keepdims=True)
        dispatch = jnp.sum(jax.nn.one_hot(top_idx, n_experts, dtype=x.dtype) * top_probs[..., None], axis=-2)
        h1 = jnp.einsum('bsd,edh->bseh', x, w1)
        h2 = jnp.einsum('bsd,edh->bseh', x, w2)
        hidden = jax.nn.silu(h1) * h2
        expert_out = jnp.einsum('bseh,eho->bseo', hidden, w3)
        return jnp.einsum('bseo,bse->bso', expert_out, dispatch)

    def _L1_gnn_ref(x, h0, a, temp, adj, l):
        import jax, jax.numpy as jnp
        import numpy as np
        N = 4096
        F = 128
        NEG_INF = -9000000000000000.0
        ALPHA = 0.2
        THRESH = 1e-06
        Fdim = x.shape[1]
        feat_1 = x @ a[:Fdim]
        feat_2 = x @ a[Fdim:]
        e = jax.nn.leaky_relu(feat_1 + feat_2.T, ALPHA)
        att = jnp.where(adj > 0, e, NEG_INF)
        U = jax.nn.softmax(att, axis=1)
        P = 0.5 * U
        prop_u = U @ x
        rowsum = jnp.sum(U * P, axis=1)
        coe = jax.nn.sigmoid(temp)
        xi = x * rowsum[:, None]
        feat_odd = prop_u - xi
        feat_even = x + prop_u - xi
        feat = coe[2] * feat_odd + (1.0 - coe[2]) * feat_even
        sgn = jnp.sign(feat)
        mod = jnp.abs(feat)
        mod = jnp.where(mod > THRESH, mod - THRESH, 0.0)
        feat = mod * sgn
        pu = U @ feat
        feat_odd2 = feat - coe[3] * pu
        feat_even2 = pu + feat_odd2 * rowsum[:, None]
        feat_odd2 = coe[0] * feat_odd2 + (1.0 - coe[0]) * h0
        out = coe[1] * feat_even2 + (1.0 - coe[1]) * feat_odd2
        return out

    def _L1_ffn_ref(x, gate_w, gate_b, w1, b1, w2, b2, gamma, beta):
        import jax, jax.numpy as jnp
        import numpy as np
        B, S, H, F, E, K = (8, 2048, 128, 256, 16, 2)
        EPS = 1e-05
        gate_logits = x @ gate_w + gate_b
        topk_vals, topk_idx = jax.lax.top_k(gate_logits, K)
        topk_w = jax.nn.softmax(topk_vals, axis=-1)
        h = jax.nn.relu(jnp.einsum('bsh,ehf->bsef', x, w1) + b1)
        expert_out = jnp.einsum('bsef,efh->bseh', h, w2) + b2
        sel = jnp.take_along_axis(expert_out, topk_idx[:, :, :, None], axis=2)
        moe = jnp.sum(topk_w[..., None] * sel, axis=2)
        y = x + moe
        mu = jnp.mean(y, axis=-1, keepdims=True)
        var = jnp.var(y, axis=-1, keepdims=True)
        return (y - mu) / jnp.sqrt(var + EPS) * gamma + beta
    x = x + _L0_gnn_ref(_layernorm(x, axis=-1), L0_gnn_x2, adj, adj, L0_gnn_eps1, L0_gnn_eps2, L0_gnn_W1, L0_gnn_b1, L0_gnn_W2, L0_gnn_b2, L0_gnn_Wm, L0_gnn_bm)
    x = x + _L0_ffn_ref(_layernorm(x, axis=-1)[None], L0_ffn_gate_w, L0_ffn_gate_b, L0_ffn_w1, L0_ffn_w2, L0_ffn_w3)[0]
    x = x + _L1_gnn_ref(_layernorm(x, axis=-1), L1_gnn_h0, L1_gnn_a, L1_gnn_temp, adj, 1)
    x = x + _L1_ffn_ref(_layernorm(x, axis=-1)[None], L1_ffn_gate_w, L1_ffn_gate_b, L1_ffn_w1, L1_ffn_b1, L1_ffn_w2, L1_ffn_b2, L1_ffn_gamma, L1_ffn_beta)[0]
    return x

_drawn_inputs = setup_inputs


def setup_inputs(seed=0):
    import zlib

    import numpy as np

    out = dict(_drawn_inputs(seed))
    spreads = {'L0_gnn_b1': (0.0, 0.1),
     'L0_gnn_b2': (0.0, 0.1),
     'L0_gnn_bm': (0.0, 0.1),
     'L0_ffn_gate_b': (0.0, 0.8),
     'L1_gnn_temp': (0.0, 0.8),
     'L1_ffn_gate_b': (0.0, 0.575),
     'L1_ffn_b1': (0.0, 0.8),
     'L1_ffn_b2': (0.0, 1.081),
     'L1_ffn_gamma': (1.0, 0.2),
     'L1_ffn_beta': (0.0, 0.272)}
    factors = {'L0_ffn_gate_w': 8.0,
     'L0_ffn_w1': 8.0,
     'L0_ffn_w2': 8.0,
     'L0_ffn_w3': 8.0,
     'L1_ffn_w1': 6.122,
     'L1_ffn_w2': 4.921}
    for name, (base, spread) in spreads.items():
        noise = np.random.default_rng([zlib.crc32(name.encode()), seed]).standard_normal(out[name].shape)
        drawn = base * np.exp(spread * noise) if base else spread * noise
        out[name] = jnp.asarray(drawn.astype(out[name].dtype))
    for name, factor in factors.items():
        out[name] = (out[name] * factor).astype(out[name].dtype)
    return out
```

```python
from contextlib import ExitStack, contextmanager

import numpy as np
import concourse.bass as bass
from concourse import mybir

ALU = mybir.AluOpType
ACT = mybir.ActivationFunctionType
AX = mybir.AxisListType
F32 = mybir.dt.float32
F32R = mybir.dt.float32r
U32 = mybir.dt.uint32
U8 = mybir.dt.uint8

P = 128
N = 4096
NT = N // P
CT = 4
CW = CT * P
NC = N // CW
NG = NT // CT
E = 16
H = 256
CAP = N + P
ROW = P + 1
ST = 80
RS = 8
EPS = 1e-5
THRESH = 1e-6
SLOPE = 0.2


def wait_alone(eng, need, sem, value):
    if isinstance(value, int):
        eng.wait_ge(sem, value)
    else:
        eng.reg_mov(need, value)
        eng.wait_ge(sem, 1)
        eng.wait_ge(sem, need)


class Steps:

    def __init__(self, eng, sem, need):
        self.eng, self.sem, self.need, self.base, self.n = eng, sem, need, 0, 0

    def __call__(self, instruction):
        instruction.then_inc(self.sem, 1)
        self.n += 1

    def wait(self):
        self.eng.wait_ge(self.sem, self.base + self.n)

    def wait_alone(self):
        wait_alone(self.eng, self.need, self.sem, self.base + self.n)

    @contextmanager
    def loop(self, trips, each):
        start = self.base + self.n
        with self.eng.Fori(0, trips) as lap:
            self.base, self.n = lap * each + start, 0
            yield lap
            assert self.n == each, f"a lap counts {self.n}"
        self.base, self.n = start + trips * each, 0


def bass_gnn_moe_kernel(nc, x, adjT, x2, eps, WT, bT, WmT, bm, gate_w, gate_b, w12, w3, h0, a, temp,
                        ew1, eb1, ew2, eb2, gamma, beta, out):
    mask_d = nc.dram_tensor("mask_d", [NC * NG, P, CT * CW], U8).ap()
    code_d = nc.dram_tensor("code_d", [NC * NG, P, CT * CW], U8).ap()
    sorted_d = [nc.dram_tensor(f"sorted_d{L}", [E * CAP + P, ROW], F32).ap() for L in range(2)]
    expert_d = [nc.dram_tensor(f"expert_d{L}", [2 * N, P], F32).ap() for L in range(2)]
    nf1_d = nc.dram_tensor("nf1_d", [NC, CW], F32).ap()

    x_v = x.rearrange("(t p) d -> p t d", p=P)
    x2_v = x2.rearrange("(t p) d -> p t d", p=P)
    h0_v = h0.rearrange("(t p) d -> p t d", p=P)
    out_v = out.rearrange("(t p) d -> p t d", p=P)

    with ExitStack() as ctx:
        def sb(name, shape, dt=F32):
            return ctx.enter_context(nc.sbuf_tensor(name, shape, dt))

        def sem(name):
            return ctx.enter_context(nc.semaphore(name))

        xs = sb("xs", [P, NT, P])
        xh = sb("xh", [P, NT, P])
        ident = sb("ident", [P, P])
        ones = sb("ones", [P, P])
        upper = sb("upper", [P, P])
        bTs = sb("bTs", [P, 6])
        gws = sb("gws", [P, 2, E])
        gbs = sb("gbs", [P, 2, E])
        a_s = sb("a_s", [P, 2])
        gam = sb("gam", [P, P])
        bet = sb("bet", [P, P])
        eps1 = sb("eps1", [P, 2])
        ls = sb("ls", [P, 5])
        lsc = sb("lsc", [P, 5])
        nc3 = sb("nc3", [P, 1])
        iota_e = sb("iota_e", [P, E])
        ecap = sb("ecap", [P, E])
        kcol = sb("kcol", [P, 1])
        tok = sb("tok", [P, 2, NT], U32)
        fill = sb("fill", [P, ROW])
        minus2 = sb("minus2", [P, 1])
        run = sb("run", [P, CT + 1, E])
        cnt = sb("cnt", [P, 4, E])
        tcol = sb("tcol", [P, 4])
        endu = sb("endu", [P, E], U32)
        nuu = sb("nuu", [P, E], U32)
        tiles = sb("tiles", [1, 2, P], U32)
        stat = sb("stat", [P, CT, 6])
        mv = sb("mv", [P, CT, 2])
        rs4 = sb("rs4", [P, 4, CT])
        lg = sb("lg", [P, CT, E])
        top = sb("top", [P, CT, 8])
        topi = sb("topi", [P, CT, 8], U32)
        topf = sb("topf", [P, CT, 8])
        oh = sb("oh", [P, 3, CT, E])
        posf = sb("posf", [P, 2, CT, E])
        posr = sb("posr", [P, 2, CT])
        pos = sb("pos", [P, 2, CT], U32)
        dl = sb("dl", [P, NT])
        wt = sb("wt", [P, 2, NT])
        f12 = sb("f12", [P, NT, 2])
        ext = sb("ext", [P, 2])
        extr = sb("extr", [P, 2])
        mid = sb("mid", [P, 1])
        zc = sb("zc", [P, 3, NT])
        fB = sb("fB", [P, 2, NT])
        fD = sb("fD", [P, 2, NT])
        fA = sb("fA", [P, NT])
        fC = sb("fC", [P, NT])
        al = sb("al", [P, NT])
        ga = sb("ga", [P, NT])
        ep = sb("ep", [P, NT])
        rsu = sb("rsu", [P, NT])
        q8 = sb("q8", [P, 8, CT])
        csr = sb("csr", [P, P])
        cs = sb("cs", [P, P])
        b1c = sb("b1c", [P, E, 2])

        R1_SIZE, R2_SIZE = NT * 4 * 130 * 4, 100544
        base1 = (nc.sbuf_base + 31) // 32 * 32
        assert base1 + R1_SIZE + R2_SIZE <= nc.sbuf_usable_end, (base1 + R1_SIZE + R2_SIZE, nc.sbuf_usable_end)
        base2 = base1 + R1_SIZE

        def at(region, offset, name, shape, dt=F32):
            size = int(np.prod(shape[1:])) * (1 if dt == U8 else 4)
            start, limit = (base1, R1_SIZE) if region == 1 else (base2, R2_SIZE)
            assert offset + size <= limit, (name, offset + size, limit)
            return nc.alloc_sbuf_tensor_at(name, shape, dt, offset=start + offset)

        XHI = at(1, 0, "XHI", [P, NT, 2 * P], F32R)
        XLO = at(1, 32768, "XLO", [P, NT, 2 * P], F32R)
        W12s = at(2, 0, "W12s", [P, E, 2 * H])
        W3s = at(2, 32768, "W3s", [P, E, 2, P])
        Abuf = at(2, 49152, "Abuf", [P, 2, CT, CW])
        HI = at(2, 65536, "HI", [P, 4, CW], F32R)
        LO = at(2, 73728, "LO", [P, 4, CW], F32R)
        Mbuf = at(2, 81920, "Mbuf", [P, 2, CT * CW], U8)
        hT = at(2, 86016, "hT", [P, 2, CW])
        stg = at(2, 86016, "stg", [P, CT, 2 * P])
        WTs = at(2, 96320, "WTs", [P, 6, P])
        WmTs = at(2, 99392, "WmTs", [P, 2, P])
        XB = at(1, 0, "XB", [P, NT, 2, 130], F32R)
        XD = at(1, 33280, "XD", [P, NT, 2, 130], F32R)
        XB2 = at(2, 0, "XB2", [P, NT, 2, P], F32R)
        XD2 = at(2, 32768, "XD2", [P, NT, 2, P], F32R)
        MP = at(2, 65536, "MP", [P, 4, CW], F32R)
        MM = at(2, 73728, "MM", [P, 4, CW], F32R)
        Cbuf = at(2, 81920, "Cbuf", [P, 2, CT * CW], U8)
        nfrow = at(2, 0, "nfrow", [1, N])
        nf1 = at(2, 86016, "nf1", [P, 2, CW])
        ev = at(2, 90112, "ev", [P, CT, 2, 2, 130])
        ev2 = at(2, 90112, "ev2", [P, CT, 2, 2, P])
        tmpb = at(2, 98432, "tmpb", [P, CT, 130])
        V1s = at(1, 0, "V1s", [P, E, H])
        V2s = at(1, 16384, "V2s", [P, E, 2, P])
        C2s = at(1, 32768, "C2s", [P, E, P])
        h0b = at(1, 58368, "h0b", [P, CT, P])
        tmo = at(1, 60416, "tmo", [P, 2, CT, P])
        pay, xTb, xin, exT, eg, ehid, ehT, ey, yb = [], [], [], [], [], [], [], [], []
        for L, (r, o, o2) in enumerate(((2, 90112, 49152), (1, 40960, 47360))):
            pay.append(at(r, o, f"pay{L}", [P, 2, CT, ROW]))
            xTb.append(at(r, o + 4160, f"xT{L}", [P, CW]))
            xin.append(at(r if L else 2, o2, f"xin{L}", [P, RS, ROW]))
            o2 += 4160
            exT.append(at(r if L else 2, o2, f"exT{L}", [P, 2, P]))
            eg.append(at(r if L else 2, o2 + 1024, f"eg{L}", [P, 2, H]))
            ehid.append(at(r if L else 2, o2 + 3072, f"ehid{L}", [P, 2, H]))
            ehT.append(at(r if L else 2, o2 + 5120, f"ehT{L}", [P, 2, 2, P]))
            ey.append(at(r if L else 2, o2 + 7168, f"ey{L}", [P, RS, P]))
            yb.append(at(2, 65536, f"yb{L}", [P, 2, 2, CT, P]))
        B = [ctx.enter_context(nc.psum_tensor(f"B{i}", [P, 512], F32)) for i in range(8)]

        s_x, s_x2, s_cst, s_w, s_w1 = sem("s_x"), sem("s_x2"), sem("s_cst"), sem("s_w"), sem("s_w1")
        s_pool = sem("s_pool")
        s_const = sem("s_const")
        s_dve = sem("s_dve")
        s_fillin = sem("s_fillin")
        s_bmr = sem("s_bmr")
        s_ad = [sem(f"s_ad{i}") for i in range(2)]
        s_mst = [sem(f"s_mst{i}") for i in range(2)]
        s_hi, s_lo, s_used, s_mk, s_xp = sem("s_hi"), sem("s_lo"), sem("s_used"), sem("s_mk"), sem("s_xp")
        s_h0, s_h1, s_m, s_r, s_g = sem("s_h0"), sem("s_h1"), sem("s_m"), sem("s_r"), sem("s_g")
        s_var, s_root = sem("s_var"), sem("s_root")
        s_xn = [sem(f"s_xn{L}") for L in range(2)]
        s_p2 = [sem(f"s_p2{L}") for L in range(2)]
        s_tr = [sem(f"s_tr{L}") for L in range(2)]
        s_xT = [sem(f"s_xT{L}") for L in range(2)]
        s_gt = [sem(f"s_gt{L}") for L in range(2)]
        s_oh = [sem(f"s_oh{L}") for L in range(2)]
        s_pp = [sem(f"s_pp{L}") for L in range(2)]
        s_pos = [sem(f"s_pos{L}") for L in range(2)]
        s_sc = [sem(f"s_sc{L}") for L in range(2)]
        s_pfree = [sem(f"s_pfree{L}") for L in range(2)]
        s_cn = [sem(f"s_cn{L}") for L in range(2)]
        s_end = [sem(f"s_end{L}") for L in range(2)]
        s_tl = [sem(f"s_tl{L}") for L in range(2)]
        s_tt = [sem(f"s_tt{L}") for L in range(2)]
        s_tu = [sem(f"s_tu{L}") for L in range(2)]
        s_tail = [sem(f"s_tail{L}") for L in range(2)]
        s_ld = [sem(f"s_ld{i}") for i in range(RS)]
        s_etx = sem("s_etx")
        s_exT = sem("s_exT")
        s_eh = sem("s_eh")
        s_eg = sem("s_eg")
        s_ehid = sem("s_ehid")
        s_eth = sem("s_eth")
        s_ehT = sem("s_ehT")
        s_eo = sem("s_eo")
        s_ey = sem("s_ey")
        s_est = [sem(f"s_est{i}") for i in range(CT)]
        s_efree = [sem(f"s_efree{L}") for L in range(2)]
        s_eall = [sem(f"s_eall{L}") for L in range(2)]
        s_yl = [[sem(f"s_yl{L}{i}") for i in range(2)] for L in range(2)]
        s_wd = [sem(f"s_wd{L}") for L in range(2)]
        s_we = [sem(f"s_we{L}") for L in range(2)]
        s_cb = [sem(f"s_cb{L}") for L in range(2)]
        s_cx, s_ct, s_cxT, s_cf, s_cr, s_crow = (sem(n) for n in ("s_cx", "s_ct", "s_cxT", "s_cf", "s_cr", "s_crow"))
        s_nfst = sem("s_nfst")
        s_cxh, s_cfr, s_cs = sem("s_cxh"), sem("s_cfr"), sem("s_cs")
        s_ext, s_extr, s_zc, s_exps, s_ls = (sem(n) for n in ("s_ext", "s_extr", "s_zc", "s_exps", "s_ls"))
        s_xb = sem("s_xb")
        s_csr, s_csp = sem("s_csr"), sem("s_csp")
        s_cl = [[sem(f"s_cl{U}{i}") for i in range(2)] for U in range(2)]
        s_cst2 = [sem(f"s_cst2{i}") for i in range(2)]
        s_nfl = [sem(f"s_nfl{i}") for i in range(2)]
        s_code = sem("s_code")
        s_mp = [sem(f"s_mp{U}") for U in range(2)]
        s_mm = [sem(f"s_mm{U}") for U in range(2)]
        s_mu = [sem(f"s_mu{U}") for U in range(2)]
        s_evp = [sem(f"s_evp{U}") for U in range(2)]
        s_evm = [sem(f"s_evm{U}") for U in range(2)]
        s_post = [sem(f"s_post{U}") for U in range(2)]
        s_h0l = sem("s_h0l")
        s_fin, s_out = sem("s_fin"), [sem("s_out0"), sem("s_out1")]

        ACC, PM, PG, PT, PGT, PPX = B[0:2], B[2:4], B[4], B[5], B[6], B[7]

        block = ctx.enter_context(nc.Block())

        @block.sync
        def _(sp):
            need = sp.alloc_register("need_sp")
            sp.dma_start(xs[:], x_v).then_inc(s_x, 16)
            sp.dma_start(xh[:], x2_v).then_inc(s_x2, 16)

            def load_adjacency(c, g):
                G = c * NG + g
                if not (isinstance(G, int) and G < 2):
                    wait_alone(sp, need, s_hi, CT * (G - 1))
                    wait_alone(sp, need, s_mk, G - 1)
                sp.dma_start(Abuf[:, g % 2], adjT[bass.ds(G, 1)].rearrange("a p n -> p (a n)")
                             .rearrange("p (t n) -> p t n", t=CT)).then_inc(s_ad[g % 2], 16)

            def store_mask(G, slot):
                wait_alone(sp, need, s_mk, G + 1)
                sp.dma_start(mask_d[bass.ds(G, 1)].rearrange("a p n -> p (a n)"), Mbuf[:, slot]).then_inc(s_mst[slot], 16)

            for g in range(NG):
                load_adjacency(0, g)
                if g == 1:
                    for dst, src in ((WTs[:], WT), (WmTs[:], WmT), (bTs[:], bT), (gws[:], gate_w), (a_s[:], a),
                                     (gbs[:], gate_b.partition_broadcast(P)),
                                     (gam[:], gamma.partition_broadcast(P)), (bet[:], beta.partition_broadcast(P)),
                                     (eps1[:], eps.partition_broadcast(P)), (ls[:], temp.partition_broadcast(P)),
                                     (b1c[:], eb1)):
                        sp.dma_start(dst, src).then_inc(s_cst, 16)
                    sp.dma_start(csr[:], bm.partition_broadcast(P)).then_inc(s_bmr, 16)
                if g == 3:
                    sp.dma_start(W12s[:], w12).then_inc(s_w, 16)
                    sp.dma_start(W3s[:], w3).then_inc(s_w, 16)
                    wait_alone(sp, need, s_const, 1)
                    for L in range(2):
                        sp.dma_start(sorted_d[L][E * CAP:E * CAP + P, :], fill[:]).then_inc(s_fillin, 16)
                if g:
                    store_mask(g - 1, (g - 1) % 2)
            with sp.Fori(1, NC) as c:
                for g in range(NG):
                    load_adjacency(c, g)
                    store_mask(c * NG + g - 1, (g - 1) % 2)
            store_mask(NC * NG - 1, 1)

            def moe_loads(L):
                wait_alone(sp, need, s_end[L], 1)
                r = sp.alloc_register(f"row{L}")
                for e in range(E):
                    sp.reg_load(r, endu[0:1, e:e + 1])
                    row = sp.snap(r, min_val=0, max_val=E * CAP - P)
                    sp.dma_start(sorted_d[L][bass.ds(row, P), :], fill[:]).then_inc(s_tail[L], 16)
                wait_alone(sp, need, s_tu[L], 1)
                wait_alone(sp, need, s_tail[L], 16 * E)
                wait_alone(sp, need, s_sc[L], 16 * 2 * NT)
                wait_alone(sp, need, s_fillin, 32)
                with sp.Fori(0, ST // RS) as lap:
                    for u in range(RS):
                        k = lap * RS + u
                        sp.reg_load(r, tiles[0:1, 1, bass.ds(k, 1)])
                        row = sp.snap(r, min_val=0, max_val=E * CAP)
                        wait_alone(sp, need, s_efree[L], k + 1)
                        sp.dma_start(xin[L][:, u], sorted_d[L][bass.ds(row, P), :]).then_inc(s_ld[u], 16)
                wait_alone(sp, need, s_eall[L], 1)
                y_v = expert_d[L].rearrange("(k t p) d -> k p t d", k=2, p=P)
                for c in range(NC):
                    if c >= 2:
                        wait_alone(sp, need, s_cb[L], c - 1)
                    for k in range(2):
                        sp.dma_start(yb[L][:, c % 2, k], y_v[k, :, c * CT:(c + 1) * CT, :]).then_inc(s_yl[L][c % 2], 16)
                    if L and c:
                        store_out(c - 1)
                if L:
                    store_out(NC - 1)

            def store_out(c):
                wait_alone(sp, need, s_fin, c + 1)
                sp.dma_start(out_v[:, c * CT:(c + 1) * CT, :], xs[:, c * CT:(c + 1) * CT, :]).then_inc(s_out[c % 2], 16)

            moe_loads(0)

            sp.wait_ge(s_crow, NC)
            sp.dma_start(nf1_d.rearrange("c n -> (c n)").unsqueeze(0), nfrow[:]).then_inc(s_nfst, 16)
            sp.wait_ge(s_nfst, 16)

            def load_codes(U, G, slot):
                src = (mask_d, code_d)[U]
                sp.dma_start(Cbuf[:, slot], src[bass.ds(G, 1)].rearrange("a p n -> p (a n)")).then_inc(s_cl[U][slot], 16)

            def load_nf1(c, slot):
                sp.dma_start(nf1[:, slot], nf1_d[bass.ds(c, 1), :].rearrange("a n -> (a n)").partition_broadcast(P)).then_inc(s_nfl[slot], 16)

            def codes_done(U, G):
                wait_alone(sp, need, s_mp[U], CT * (G + 1))
                wait_alone(sp, need, s_mm[U], CT * (G + 1))

            for i in range(2):
                wait_alone(sp, need, s_mst[i], 16 * NC * NG // 2)
            wait_alone(sp, need, s_cb[0], NC)
            for i in range(2):
                load_codes(0, i, i)
            load_nf1(0, 0)

            def group_d(c, g, last):
                G = c * NG + g
                wait_alone(sp, need, s_code, CT * (G + 1))
                sp.dma_start(code_d[bass.ds(G, 1)].rearrange("a p n -> p (a n)"), Cbuf[:, g % 2]).then_inc(s_cst2[g % 2], 16)
                codes_done(0, G)
                wait_alone(sp, need, s_cst2[g % 2], 16 * (c * (NG // 2) + g // 2 + 1))
                if not (last and g >= NG - 2):
                    load_codes(0, G + 2, g % 2)

            with sp.Fori(0, (NC - 2) // 2) as c2:
                for d in range(2):
                    load_nf1(c2 * 2 + d + 1, (d + 1) % 2)
                    for g in range(NG):
                        group_d(c2 * 2 + d, g, False)
            load_nf1(NC - 1, 1)
            for g in range(NG):
                group_d(NC - 2, g, False)
            for g in range(NG):
                group_d(NC - 1, g, True)
            for i in range(2):
                load_codes(1, i, i)
            wait_alone(sp, need, s_mu[0], NC * NT)
            for dst, src in ((V1s[:], ew1), (V2s[:], ew2), (C2s[:], eb2.partition_broadcast(P))):
                sp.dma_start(dst, src).then_inc(s_w1, 16)

            def group_e(c, g, last):
                codes_done(1, c * NG + g)
                if not (last and g >= NG - 2):
                    load_codes(1, c * NG + g + 2, g % 2)

            sp.dma_start(h0b[:], h0_v[:, 0:CT, :]).then_inc(s_h0l, 16)
            with sp.Fori(0, NC - 1) as c:
                for g in range(NG):
                    group_e(c, g, False)
                wait_alone(sp, need, s_post[1], c + 1)
                sp.dma_start(h0b[:], h0_v[:, bass.ds(c * CT + CT, CT), :]).then_inc(s_h0l, 16)
            for g in range(NG):
                group_e(NC - 1, g, True)
            moe_loads(1)
            for i in range(2):
                wait_alone(sp, need, s_out[i], 16 * NC // 2)

        @block.gpsimd
        def _(pool):
            need = pool.alloc_register("need_pool")
            S = Steps(pool, s_pool, need)
            S(pool.memset(ident[:], 0.0))
            S(pool.memset(ones[:], 1.0))
            S(pool.memset(fill[:, 0:P], 0.0))
            S(pool.memset(minus2[:], -2.0))
            S(pool.iota(fill[:, P:P + 1].bitcast(U32), pattern=[[1, 1]], base=2 * N, channel_multiplier=1))
            S(pool.iota(tok[:], pattern=[[N, 2], [P, NT]], base=0, channel_multiplier=1))
            S(pool.iota(iota_e[:], pattern=[[1, E]], base=0, channel_multiplier=0, allow_small_or_imprecise_dtypes=True))
            S(pool.iota(ecap[:], pattern=[[CAP, E]], base=0, channel_multiplier=0, allow_small_or_imprecise_dtypes=True))
            S(pool.iota(kcol[:], pattern=[[1, 1]], base=0, channel_multiplier=1, allow_small_or_imprecise_dtypes=True))
            S.wait()
            S(pool.affine_select(out=ident[:], in_=ident[:], compare_op=ALU.not_equal, fill=1.0, base=0,
                                 pattern=[[-1, P]], channel_multiplier=1))
            S(pool.affine_select(out=upper[:], in_=ones[:], compare_op=ALU.is_gt, fill=0.0, base=0,
                                 pattern=[[1, P]], channel_multiplier=-1))
            S.wait()
            pool.sem_inc(s_const, 1)

            def scatter_chunk(L, c):
                wait_alone(pool, need, s_p2[L], c + 1)
                pool.wait_ge(s_pos[L], c + 1)
                for q in range(CT):
                    for k in range(2):
                        pool.indirect_dma_start(
                            out=sorted_d[L], out_offset=bass.IndirectOffsetOnAxis(ap=pos[:, k, q:q + 1], axis=0),
                            in_=pay[L][:, k, q, :], in_offset=None,
                            bounds_check=E * CAP - 1, oob_is_err=False).then_inc(s_sc[L], 16)
                pool.wait_ge(s_sc[L], c * (16 * 2 * CT) + 16 * 2 * CT)
                pool.sem_inc(s_pfree[L], 1)

            def scatter_results(L):
                def scattered(lap, u):
                    done = lap * (RS // CT) + (u // CT + 1) + L * (ST // CT)
                    pool.wait_ge(s_est[u % CT], done * 16)
                    pool.sem_inc(s_efree[L], 1)

                pool.sem_inc(s_efree[L], RS)
                with pool.Fori(0, ST // RS) as lap:
                    for u in range(RS):
                        wait_alone(pool, need, s_ey, lap * RS + u + 1 + L * ST)
                        pool.indirect_dma_start(
                            out=expert_d[L], out_offset=bass.IndirectOffsetOnAxis(ap=xin[L][:, u, P:P + 1].bitcast(U32), axis=0),
                            in_=ey[L][:, u], in_offset=None,
                            bounds_check=2 * N - 1, oob_is_err=False).then_inc(s_est[u % CT], 16)
                        if u:
                            scattered(lap, u - 1)
                    scattered(lap, RS - 1)
                pool.sem_inc(s_eall[L], 1)

            for L in range(2):
                pool.sem_inc(s_pfree[L], 1)
                with pool.Fori(0, NC) as c:
                    scatter_chunk(L, c)
                scatter_results(L)
                if L == 0:
                    pool.wait_ge(s_ext, 1)
                    pool.partition_all_reduce(extr[:], ext[:], P, bass.bass_isa.ReduceOp.max).then_inc(s_extr, 1)

        A_ACT = {2: "in", 5: "relu0", 8: "relu1", 11: "relu2", 15: "root", 17: "copy", 19: "xT"}
        A_DVE = {2: "in", 13: "add", 16: "norm", 21: "top", 25: "pos"}
        A_PE = {1: "mlp0", 4: "mlp1", 7: "mlp2", 10: "merge", 15: "turn", 18: "gate", 22: "prefix"}
        E_ACT = {2: "out", 17: "root", 20: "copy", 22: "xT"}
        E_DVE = {2: "out", 6: "post", 18: "norm", 25: "top", 30: "pos"}
        E_PE = {19: "turn", 22: "gate", 26: "prefix"}

        @block.scalar
        def _(act):
            def leading_part(c, jt, first):
                g, j = jt // CT, jt % CT
                if j == 0:
                    act.wait_ge(s_ad[g % 2], (c * (NG // 2) + g // 2) * 16 + 16)
                if not (first and jt < 4):
                    act.wait_ge(s_used, c * NT + jt - 3)
                act.activation(HI[:, jt % 4], Abuf[:, g % 2, j], ACT.Copy).then_inc(s_hi, 1)

            def mlp_in(c):
                act.wait_ge(s_used, c * NT + NT)
                act.activation(hT[:, 0], ACC[0][:], ACT.Identity, scale=eps1[:, 0:1]).then_inc(s_h0, 1)

            def relu(c, layer):
                act.wait_ge(s_m, c * 3 + layer + 1)
                for v in range(2):
                    bias = bTs[:, 3 * v + layer:3 * v + layer + 1]
                    act.activation(hT[:, v], PM[v][:], ACT.Relu, bias=bias).then_inc(s_r, 1)

            def root(n):
                act.wait_ge(s_var, n + 1)
                act.activation(rs4[:, 1], rs4[:, 0], ACT.Sqrt).then_inc(s_root, 1)

            def second_copy(L, c):
                act.wait_ge(s_xn[L], c + 1)
                if L:
                    act.activation(xh[:, bass.ds(c * CT, CT), :], pay[L][:, 0, :, 0:P], ACT.Copy).then_inc(s_cxh, 1)
                act.activation(pay[L][:, 1, :, 0:P], pay[L][:, 0, :, 0:P], ACT.Copy).then_inc(s_p2[L], 1)

            def xT_out(L, c):
                act.wait_ge(s_tr[L], c + 1)
                act.activation(xTb[L][:], PT[:], ACT.Copy).then_inc(s_xT[L], 1)

            def tail_a(what, c):
                if what == "in":
                    mlp_in(c)
                elif what in ("relu0", "relu1", "relu2"):
                    relu(c, int(what[4]))
                elif what == "root":
                    root(c + NG)
                elif what == "copy":
                    second_copy(0, c)
                elif what == "xT":
                    xT_out(0, c)

            act.wait_ge(s_ls, 1)
            for jt in range(NT):
                if jt % CT == 0:
                    root(jt // CT)
                leading_part(0, jt, True)
            with act.Fori(0, NC - 1) as t:
                for jt in range(NT):
                    leading_part(t + 1, jt, False)
                    tail_a(A_ACT.get(jt), t)
            for what in A_ACT.values():
                tail_a(what, NC - 1)

            def experts(L):
                def x_out(k, u):
                    act.wait_ge(s_etx, k + 1 + L * ST)
                    act.activation(exT[L][:, u % 2], (B[2], B[5])[u % 2][:, 0:P], ACT.Copy).then_inc(s_exT, 1)

                def h_out(k, u):
                    act.wait_ge(s_eh, k + 1 + L * ST)
                    act.activation(eg[L][:, u % 2], B[u % 2][:, 0:H], (ACT.Silu, ACT.Copy)[L]).then_inc(s_eg, 1)

                for k in range(RS):
                    x_out(k, k)
                    if k:
                        h_out(k - 1, k - 1)
                with act.Fori(1, ST // RS) as lap:
                    for u in range(RS):
                        x_out(lap * RS + u, u)
                        h_out(lap * RS + (u - 1), (u - 1) % RS)
                h_out(ST - 1, RS - 1)

            def weights(L):
                act.wait_ge(s_wd[L], 1)
                act.activation(wt[:, 1], dl[:], ACT.Exp).then_inc(s_we[L], 1)

            weights(0)
            experts(0)

            act.sem_inc(s_cxh, 1)
            with act.Fori(0, NC) as c:
                root(c + (NG + NC))
                act.wait_ge(s_cx, c + 1)
                act.activation(xh[:, bass.ds(c * CT, CT), :], pay[0][:, 0, :, 0:P], ACT.Copy).then_inc(s_cxh, 1)
                act.wait_ge(s_ct, c + 1)
                act.activation(xTb[0][:], PT[:], ACT.Copy).then_inc(s_cxT, 1)
                act.wait_ge(s_cr, c + 1)
                act.activation(nfrow[:, bass.ds(c * CW, CW)], PG[0:1, :], ACT.Copy, scale=-1.0).then_inc(s_crow, 1)
            act.wait_ge(s_zc, 1)
            act.activation(fB[:, 0], zc[:, 0], ACT.Exp).then_inc(s_exps, 1)
            act.activation(fD[:, 0], zc[:, 0], ACT.Exp, scale=SLOPE).then_inc(s_exps, 1)
            act.activation(fA[:], zc[:, 1], ACT.Exp).then_inc(s_exps, 1)
            act.activation(fC[:], zc[:, 2], ACT.Exp).then_inc(s_exps, 1)
            act.activation(lsc[:], ls[:], ACT.Exp, scale=-1.0).then_inc(s_exps, 1)

            def positive(U, c, jt, first):
                g, j = jt // CT, jt % CT
                if U == 0:
                    act.wait_ge(s_code, c * NT + jt + 1)
                elif j == 0:
                    act.wait_ge(s_cl[1][g % 2], (c * (NG // 2) + g // 2) * 16 + 16)
                if not (first and jt < 4):
                    act.wait_ge(s_mu[U], c * NT + jt - 3)
                act.activation(MP[:, jt % 4], Cbuf[:, g % 2, j * CW:(j + 1) * CW], ACT.Relu, bias=minus2[:]).then_inc(s_mp[U], 1)

            def products_out(U, c, first):
                act.wait_ge(s_mu[U], c * NT + NT)
                if not first:
                    act.wait_ge(s_post[U], c)
                for q in range((4, 2)[U]):
                    if U == 0:
                        act.activation(ev[:, q, 0].rearrange("p h n -> p (h n)"), B[q][:, 0:260], ACT.Copy).then_inc(s_evp[U], 1)
                    else:
                        act.activation(ev2[:, q].rearrange("p s h n -> p (s h n)"), B[q][:], ACT.Copy).then_inc(s_evp[U], 1)

            def tail_u(U, what, c, first):
                if what == "out":
                    products_out(U, c, first)
                elif U and what == "root":
                    root(c + (NG + 2 * NC))
                elif U and what == "copy":
                    second_copy(1, c)
                elif U and what == "xT":
                    xT_out(1, c)

            for U in range(2):
                for jt in range(NT):
                    positive(U, 0, jt, True)
                for jt in range(NT):
                    positive(U, 1, jt, False)
                    tail_u(U, E_ACT.get(jt), 0, True)
                with act.Fori(1, NC - 1) as t:
                    for jt in range(NT):
                        positive(U, t + 1, jt, False)
                        tail_u(U, E_ACT.get(jt), t, False)
                for what in E_ACT.values():
                    tail_u(U, what, NC - 1, False)
            weights(1)
            experts(1)
            with act.Fori(0, NC) as c:
                root(c + (NG + 3 * NC))

        @block.tensor
        def _(pe):
            pe.wait_ge(s_const, 1)
            pe.wait_ge(s_ls, 1)

            def aggregate(c, jt, first):
                if first and jt % CT == 0:
                    pe.wait_ge(s_xp, jt // CT + 1)
                if jt == 0 and not first:
                    pe.wait_ge(s_h0, c)
                    pe.wait_ge(s_h1, c)
                pe.wait_ge(s_hi, c * NT + jt + 1)
                for X, start in ((XHI, jt == 0), (XLO, False)):
                    for v in range(2):
                        pe.matmul(ACC[v][:], X[:, jt, v * P:(v + 1) * P], HI[:, jt % 4], start=start, stop=False)
                pe.wait_ge(s_lo, c * NT + jt + 1)
                for v in range(2):
                    last = pe.matmul(ACC[v][:], XHI[:, jt, v * P:(v + 1) * P], LO[:, jt % 4], start=False, stop=jt == NT - 1)
                last.then_inc(s_used, 1)

            def mlp(c, layer):
                if layer == 0:
                    pe.wait_ge(s_h0, c + 1)
                    pe.wait_ge(s_h1, c + 1)
                else:
                    pe.wait_ge(s_r, c * 6 + 2 * layer)
                for v in range(2):
                    last = pe.matmul(PM[v][:], WTs[:, 3 * v + layer], hT[:, v], start=True, stop=True)
                last.then_inc(s_m, 1)

            def merge(c):
                pe.wait_ge(s_r, c * 6 + 6)
                for q in range(CT):
                    for v in range(2):
                        last = pe.matmul(PG[:, q * P:(q + 1) * P], hT[:, v, q * P:(q + 1) * P], WmTs[:, v],
                                         start=v == 0, stop=v == 1)
                last.then_inc(s_g, 1)

            def turn(L, c):
                pe.wait_ge(s_xn[L], c + 1)
                for q in range(CT):
                    last = pe.transpose(PT[:, q * P:(q + 1) * P], pay[L][:, 0, q, 0:P], ident[:])
                last.then_inc(s_tr[L], 1)

            def gate(L, c):
                pe.wait_ge(s_xT[L], c + 1)
                for q in range(CT):
                    last = pe.matmul(PGT[:, q * E:(q + 1) * E], xTb[L][:, q * P:(q + 1) * P], gws[:, L], start=True, stop=True)
                last.then_inc(s_gt[L], 1)

            def prefix(L, c):
                pe.wait_ge(s_oh[L], c + 1)
                pe.matmul(PPX[:, 0:CT * E], upper[:], oh[:, 2].rearrange("p q e -> p (q e)"), start=True, stop=False)
                pe.matmul(PPX[:, 0:CT * E], ones[:], run[:, 0:CT].rearrange("p q e -> p (q e)"),
                          start=False, stop=True).then_inc(s_pp[L], 1)

            def tail(L, what, c):
                if what in ("mlp0", "mlp1", "mlp2"):
                    mlp(c, int(what[3]))
                elif what == "merge":
                    merge(c)
                elif what == "turn":
                    turn(L, c)
                elif what == "gate":
                    gate(L, c)
                elif what == "prefix":
                    prefix(L, c)

            for jt in range(NT):
                aggregate(0, jt, True)
            with pe.Fori(0, NC - 1) as t:
                for jt in range(NT):
                    aggregate(t + 1, jt, False)
                    tail(0, A_PE.get(jt), t)
            for what in A_PE.values():
                tail(0, what, NC - 1)

            def tile_table(L):
                pe.matmul(PGT[:, 0:E], ones[:], run[:, CT], start=True, stop=True).then_inc(s_cn[L], 1)
                pe.wait_ge(s_tl[L], 1)
                pe.matmul(PPX[0:1, 0:P], tcol[:, 0:1], ident[:], start=True, stop=True)
                pe.matmul(PPX[0:1, P:2 * P], tcol[:, 2:3], ident[:], start=True, stop=True).then_inc(s_tt[L], 1)

            def experts(L):
                W1, W2, width = ((W12s, W3s, 2 * H), (V1s, V2s, H))[L]
                r = pe.alloc_register(f"expert{L}")

                def expert(k):
                    pe.reg_load(r, tiles[0:1, 0, bass.ds(k, 1)])
                    return pe.snap(r, min_val=0, max_val=E - 1)

                def x_in(k, lap, u):
                    pe.wait_ge(s_ld[u], lap * 16 + 16 + L * 16 * (ST // RS))
                    pe.transpose((B[2], B[5])[u % 2][:, 0:P], xin[L][:, u, 0:P], ident[:]).then_inc(s_etx, 1)

                def hidden(k, u):
                    e = expert(k)
                    pe.wait_ge(s_exT, k + 1 + L * ST)
                    pe.matmul(B[u % 2][:, 0:width], exT[L][:, u % 2], W1[:, bass.ds(e, 1), :].rearrange("p a n -> p (a n)"),
                              start=True, stop=True).then_inc(s_eh, 1)

                def result(k, u, first):
                    e = expert(k)
                    pe.wait_ge(s_ehT, k + 1 + L * ST)
                    if not first:
                        pe.wait_ge(s_ey, k - 1 + L * ST)
                    for h in range(2):
                        last = pe.matmul((B[4], B[6])[u % 2][:, 0:P], ehT[L][:, u % 2, h],
                                         W2[:, bass.ds(e, 1), h, :].rearrange("p a n -> p (a n)"), start=h == 0, stop=h == 1)
                    last.then_inc(s_eo, 1)

                def hidden_turn(k, u):
                    pe.wait_ge((s_ehid, s_eg)[L], k + 1 + L * ST)
                    for h in range(2):
                        src = (ehid, eg)[L][L][:, u % 2, h * P:(h + 1) * P]
                        last = pe.transpose(B[3][:, h * P:(h + 1) * P], src, ident[:])
                    last.then_inc(s_eth, 1)

                pe.wait_ge(s_tu[L], 1)
                pe.wait_ge((s_w, s_w1)[L], (32, 48)[L])
                for k in range(ST + 3):
                    if k == RS:
                        with pe.Fori(1, ST // RS) as lap:
                            for u in range(RS):
                                x_in(lap * RS + u, lap, u)
                                hidden(lap * RS + (u - 1), (u - 1) % RS)
                                result(lap * RS + (u - 3), (u - 3) % RS, False)
                                hidden_turn(lap * RS + (u - 2), (u - 2) % RS)
                    if RS <= k < ST:
                        continue
                    if k < ST:
                        x_in(k, 0, k % RS)
                    if 0 <= k - 1 < ST:
                        hidden(k - 1, (k - 1) % RS)
                    if 0 <= k - 3 < ST:
                        result(k - 3, (k - 3) % RS, k - 3 < 2)
                    if 0 <= k - 2 < ST:
                        hidden_turn(k - 2, (k - 2) % RS)

            tile_table(0)
            experts(0)

            with pe.Fori(0, NC) as c:
                pe.wait_ge(s_cx, c + 1)
                for q in range(CT):
                    last = pe.transpose(PT[:, q * P:(q + 1) * P], pay[0][:, 0, q, 0:P], ident[:])
                last.then_inc(s_ct, 1)
                pe.wait_ge(s_cxT, c + 1)
                pe.matmul(PG[0:1, :], a_s[:, 0:1], xTb[0][:], start=True, stop=True).then_inc(s_cr, 1)
                pe.wait_ge(s_cfr, c + 1)
                for q in range(CT):
                    last = pe.matmul(PGT[:, 2 * q:2 * q + 2], xTb[0][:, q * P:(q + 1) * P], a_s[:], start=True, stop=True)
                last.then_inc(s_cf, 1)

            def column_sums(U):
                if U == 0:
                    pe.wait_ge(s_crow, NC)
                pe.wait_ge(s_csr, U + 1)
                pe.matmul(PG[:, 0:P], ones[:], csr[:], start=True, stop=True).then_inc(s_csp, 1)
                pe.wait_ge(s_cs, U + 1)

            def multiply(U, c, jt, first):
                operands = ((XB, XD), (XB2, XD2))[U]
                if U == 0 and first and jt % CT == 0:
                    pe.wait_ge(s_xb, jt // CT + 1)
                for kind, (ring, made) in enumerate(((MP, s_mp[U]), (MM, s_mm[U]))):
                    pe.wait_ge(made, c * NT + jt + 1)
                    rhs = operands[kind][:, jt].rearrange("p h n -> p (h n)")
                    for q in range(CT):
                        if jt == 0 and not first:
                            if U == 0:
                                pe.wait_ge((s_evp, s_evm)[kind][0], c * 4 + (q - 3))
                            elif kind == 0:
                                pe.wait_ge((s_evp, s_evp, s_evm, s_evm)[q][1], c * 2 + (q % 2 - 1))
                        if U == 0:
                            dst = B[4 * kind + q][:, 0:260]
                        else:
                            dst = B[q][:, kind * 2 * P:(kind + 1) * 2 * P]
                        last = pe.matmul(dst, ring[:, jt % 4, q * P:(q + 1) * P], rhs,
                                         start=jt == 0 and (U == 0 or kind == 0), stop=jt == NT - 1,
                                         skip_group_check=U == 1)
                last.then_inc(s_mu[U], 1)

            for U in range(2):
                column_sums(U)
                if U:
                    pe.wait_ge(s_post[0], NC)
                for jt in range(NT):
                    multiply(U, 0, jt, True)
                with pe.Fori(0, NC - 1) as t:
                    for jt in range(NT):
                        multiply(U, t + 1, jt, False)
                        if U:
                            tail(1, E_PE.get(jt), t)
            for what in E_PE.values():
                tail(1, what, NC - 1)
            tile_table(1)
            experts(1)

        @block.vector
        def _(dve):
            need = dve.alloc_register("need_dve")
            D = Steps(dve, s_dve, need)

            def rest(c, jt, first):
                g, j = jt // CT, jt % CT
                dve.wait_ge(s_hi, c * NT + jt + 1)
                if not (first and jt < 4):
                    dve.wait_ge(s_used, c * NT + jt - 3)
                dve.tensor_tensor(LO[:, jt % 4], Abuf[:, g % 2, j], HI[:, jt % 4].bitcast(F32), ALU.subtract).then_inc(s_lo, 1)
                if j == CT - 1:
                    if not (first and g < 2):
                        dve.wait_ge(s_mst[g % 2], (c * (NG // 2) + g // 2) * 16)
                    dve.tensor_scalar(Mbuf[:, g % 2], Abuf[:, g % 2].rearrange("p t n -> p (t n)"), 0.0, 2.0,
                                      ALU.is_gt, ALU.mult).then_inc(s_mk, 1)

            def statistics(src):
                for q in range(CT):
                    D(dve.bn_stats(stat[:, q], src[:, q]))
                D.wait_alone()
                for q in range(CT):
                    D(dve.bn_aggr(mv[:, q], stat[:, q]))
                D.wait()
                dve.tensor_scalar(rs4[:, 0], mv[:, :, 1], EPS, None, ALU.add).then_inc(s_var, 1)

            def inverse_root(n):
                v, r, t = rs4[:, 0], rs4[:, 2], rs4[:, 3]
                dve.wait_ge(s_root, n + 1)
                D(dve.reciprocal(r, rs4[:, 1]))
                D.wait()
                D(dve.tensor_tensor(t, r, r, ALU.mult))
                D.wait()
                D(dve.tensor_tensor(t, t, v, ALU.mult))
                D.wait()
                D(dve.tensor_scalar(t, t, -0.5, 1.5, ALU.mult, ALU.add))
                D.wait()
                D(dve.tensor_tensor(r, r, t, ALU.mult))
                D.wait()

            def normalize(dst, src, q):
                return dve.tensor_scalar(dst, src, mv[:, q, 0:1], rs4[:, 2, q:q + 1], ALU.subtract, ALU.mult)

            def chunk_of(c):
                return xs[:, bass.ds(c * CT, CT), :]

            def split(hi, lo, src):
                D(dve.tensor_copy(hi, src))
                D.wait()
                return dve.tensor_tensor(lo, src, hi.bitcast(F32), ALU.subtract)

            def operands_a(g):
                t = slice(g * CT, (g + 1) * CT)
                statistics(xs[:, t])
                inverse_root(g)
                for q in range(CT):
                    D(normalize(stg[:, q, 0:P], xs[:, g * CT + q], q))
                D(dve.tensor_copy(stg[:, :, P:], xh[:, t]))
                D.wait()
                D(dve.tensor_tensor(xs[:, t], xs[:, t], csr[:].unsqueeze(1).broadcast_to([P, CT, P]), ALU.add))
                split(XHI[:, t], XLO[:, t], stg[:]).then_inc(s_xp, 1)

            def mlp_in(c):
                dve.wait_ge(s_used, c * NT + NT)
                dve.tensor_scalar(hT[:, 1], ACC[1][:], eps1[:, 1:2], None, ALU.mult).then_inc(s_h1, 1)

            def add_gnn(c):
                dve.wait_ge(s_g, c + 1)
                D(dve.tensor_tensor(chunk_of(c), PG[:].rearrange("p (t n) -> p t n", t=CT), chunk_of(c), ALU.add))
                D.wait_alone()
                statistics(chunk_of(c))

            def payload(L, c, n):
                inverse_root(n)
                dve.wait_ge(s_pfree[L], c + 1)
                for k in range(2):
                    D(dve.tensor_copy(pay[L][:, k, :, P].bitcast(U32), tok[:, k, bass.ds(c * CT, CT)]))
                for q in range(CT):
                    last = normalize(pay[L][:, 0, q, 0:P], xs[:, bass.ds(c * CT + q, 1), :].rearrange("p a d -> p (a d)"), q)
                    if q < CT - 1:
                        D(last)
                last.then_inc(s_xn[L], 1)

            def top_two(L, c):
                dve.wait_ge(s_gt[L], c + 1)
                D(dve.tensor_tensor(lg[:], PGT[:, 0:CT * E].rearrange("p (q e) -> p q e", q=CT),
                                    gbs[:, L].unsqueeze(1).broadcast_to([P, CT, E]), ALU.add))
                D.wait_alone()
                for q in range(CT):
                    D(dve.max(top[:, q], lg[:, q]))
                D.wait_alone()
                for q in range(CT):
                    D(dve.max_index(topi[:, q], top[:, q], lg[:, q]))
                D(dve.tensor_tensor(dl[:, bass.ds(c * CT, CT)], top[:, :, 1], top[:, :, 0], ALU.subtract))
                D(dve.tensor_copy(run[:, 0], run[:, CT]))
                D.wait()
                D(dve.tensor_copy(topf[:], topi[:]))
                D.wait()
                for k in range(2):
                    D(dve.tensor_tensor(oh[:, k], iota_e[:].unsqueeze(1).broadcast_to([P, CT, E]),
                                        topf[:, :, k:k + 1].broadcast_to([P, CT, E]), ALU.is_equal))
                D.wait()
                D(dve.tensor_tensor(oh[:, 2], oh[:, 0], oh[:, 1], ALU.add))
                for q in range(CT):
                    D.wait()
                    last = dve.tensor_tensor(run[:, q + 1], run[:, q], oh[:, 2, q], ALU.add)
                    if q < CT - 1:
                        D(last)
                last.then_inc(s_oh[L], 1)

            def positions(L, c):
                dve.wait_ge(s_pp[L], c + 1)
                free = PPX[:, 0:CT * E].rearrange("p (q e) -> p q e", q=CT)
                for k in range(2):
                    D(dve.tensor_tensor(posf[:, k], oh[:, k], free, ALU.mult))
                D.wait()
                D(dve.tensor_reduce(posr[:], posf[:], AX.X, ALU.add))
                D.wait()
                dve.tensor_copy(pos[:], posr[:]).then_inc(s_pos[L], 1)

            def first_rows():
                D(dve.memset(run[:], 0.0))
                D.wait()
                D(dve.tensor_copy(run[0:1, CT], ecap[0:1, :]))
                D.wait()

            def tail_a(what, c):
                if what == "in":
                    mlp_in(c)
                elif what == "add":
                    add_gnn(c)
                elif what == "norm":
                    payload(0, c, c + NG)
                elif what == "top":
                    top_two(0, c)
                elif what == "pos":
                    positions(0, c)

            dve.wait_ge(s_const, 1)
            first_rows()
            dve.wait_ge(s_cst, 16 * 11)
            dve.tensor_scalar(eps1[:], eps1[:], 2.0, None, ALU.add).then_inc(s_ls, 1)
            dve.wait_ge(s_bmr, 16)
            dve.wait_ge(s_x, 16)
            dve.wait_ge(s_x2, 16)
            for jt in range(NT):
                if jt % CT == 0:
                    operands_a(jt // CT)
                rest(0, jt, True)
            with D.loop(NC - 1, 40) as t:
                for jt in range(NT):
                    rest(t + 1, jt, False)
                    tail_a(A_DVE.get(jt), t)
            for what in A_DVE.values():
                tail_a(what, NC - 1)

            def tile_table(L):
                end, need, upto, tmp = (cnt[:, i] for i in range(4))
                dve.wait_ge(s_cn[L], 1)
                D(dve.tensor_copy(end, PGT[:, 0:E]))
                D.wait()
                dve.tensor_copy(endu[:], end).then_inc(s_end[L], 1)
                D(dve.tensor_tensor(tmp, end, ecap[:], ALU.subtract))
                D.wait()
                D(dve.tensor_scalar(nuu[:], tmp, float(P - 1), None, ALU.add))
                D.wait()
                D(dve.tensor_scalar(nuu[:], nuu[:], 7, None, ALU.logical_shift_right))
                D.wait()
                D(dve.tensor_copy(need, nuu[:]))
                D.wait()
                D(dve.tensor_tensor_scan(upto, ones[:, 0:E], need, 0.0, ALU.mult, ALU.add))
                D.wait()
                D(dve.tensor_scalar(tmp, upto, kcol[:, 0:1], None, ALU.is_le))
                D.wait()
                D(dve.tensor_reduce(tcol[:, 0:1], tmp, AX.X, ALU.add))
                D(dve.tensor_tensor(need, need, tmp, ALU.mult))
                D.wait()
                D(dve.tensor_reduce(tcol[:, 1:2], need, AX.X, ALU.add))
                D.wait()
                D(dve.tensor_tensor(tcol[:, 2:3], kcol[:], tcol[:, 1:2], ALU.subtract))
                D(dve.tensor_scalar(tcol[:, 3:4], tcol[:, 0:1], float(CAP), None, ALU.mult))
                D.wait()
                D(dve.scalar_tensor_tensor(out=tcol[:, 2:3], in0=tcol[:, 2:3], scalar=float(P), in1=tcol[:, 3:4],
                                           op0=ALU.mult, op1=ALU.add))
                D.wait()
                D(dve.tensor_scalar(tcol[:, 2:3], tcol[:, 2:3], float(E * CAP), None, ALU.min))
                dve.tensor_scalar(tcol[:, 0:1], tcol[:, 0:1], float(E - 1), None, ALU.min).then_inc(s_tl[L], 1)
                dve.wait_ge(s_tt[L], 1)
                dve.tensor_copy(tiles[:], PPX[0:1, 0:2 * P].rearrange("p (a n) -> p a n", a=2)).then_inc(s_tu[L], 1)
                dve.wait_ge(s_tu[L], 1)
                if L == 0:
                    first_rows()
                dve.sem_inc(s_wd[L], 1)

            def weights(L):
                dve.wait_ge(s_we[L], 1)
                D(dve.tensor_scalar(wt[:, 0], wt[:, 1], 1.0, None, ALU.add))
                D.wait()
                D(dve.reciprocal(wt[:, 0], wt[:, 0]))
                D.wait()
                D(dve.tensor_tensor(wt[:, 1], wt[:, 1], wt[:, 0], ALU.mult))

            def experts(L):
                r = dve.alloc_register(f"bias{L}")

                def expert(k):
                    dve.reg_load(r, tiles[0:1, 0, bass.ds(k, 1)])
                    return dve.snap(r, min_val=0, max_val=E - 1)

                def gated(k, u):
                    if L == 0:
                        dve.wait_ge(s_eg, k + 1 + L * ST)
                        dve.tensor_tensor(ehid[L][:, u % 2], B[u % 2][:, H:2 * H], eg[L][:, u % 2], ALU.mult).then_inc(s_ehid, 1)

                def hidden_out(k, u):
                    src = B[3][:, 0:H].rearrange("p (h n) -> p h n", h=2)
                    if L == 0:
                        dve.wait_ge(s_eth, k + 1 + L * ST)
                        dve.tensor_copy(ehT[L][:, u % 2], src).then_inc(s_ehT, 1)
                        return
                    e = expert(k)
                    dve.wait_ge(s_eth, k + 1 + L * ST)
                    for h in range(2):
                        last = dve.tensor_scalar(ehT[L][:, u % 2, h], src[:, h], b1c[:, bass.ds(e, 1), h], 0.0, ALU.add, ALU.max)
                        if h == 0:
                            D(last)
                    last.then_inc(s_ehT, 1)

                def result_out(k, u):
                    if L:
                        e = expert(k)
                    dve.wait_ge(s_eo, k + 1 + L * ST)
                    dve.wait_ge(s_efree[L], k + 1)
                    src = (B[4], B[6])[u % 2][:, 0:P]
                    if L == 0:
                        dve.tensor_copy(ey[L][:, u], src).then_inc(s_ey, 1)
                    else:
                        bias = C2s[:, bass.ds(e, 1), :].rearrange("p a n -> p (a n)")
                        dve.tensor_tensor(ey[L][:, u], src, bias, ALU.add).then_inc(s_ey, 1)

                if L:
                    dve.wait_ge(s_w1, 48)
                for k in range(ST + 3):
                    if k == RS:
                        with D.loop(ST // RS - 1, RS * L) as lap:
                            for u in range(RS):
                                gated(lap * RS + (u + RS - 1), (u - 1) % RS)
                                hidden_out(lap * RS + (u + RS - 2), (u - 2) % RS)
                                result_out(lap * RS + (u + RS - 3), (u - 3) % RS)
                    if RS <= k < ST:
                        continue
                    if 0 <= k - 1 < ST:
                        gated(k - 1, (k - 1) % RS)
                    if 0 <= k - 2 < ST:
                        hidden_out(k - 2, (k - 2) % RS)
                    if 0 <= k - 3 < ST:
                        result_out(k - 3, (k - 3) % RS)

            def combine(L, c, c2, slot):
                dve.wait_ge(s_yl[L][slot], c2 * 32 + 32)
                for k in range(2):
                    for q in range(CT):
                        t = bass.ds(c * CT + q, 1)
                        row = (xs, xh)[L][:, t, :].rearrange("p a d -> p (a d)")
                        D(dve.scalar_tensor_tensor(out=row, in0=yb[L][:, slot, k, q], scalar=wt[:, k, t],
                                                   in1=row, op0=ALU.mult, op1=ALU.add))
                    D.wait()
                dve.sem_inc(s_cb[L], 1)

            tile_table(0)
            weights(0)
            experts(0)

            dve.sem_inc(s_cfr, 1)
            dve.wait_ge(s_pfree[0], NC + 1)
            with D.loop(NC // 2, 50) as c2:
                for slot in range(2):
                    c = c2 * 2 + slot
                    combine(0, c, c2, slot)
                    statistics(chunk_of(c))
                    inverse_root(c + (NG + NC))
                    dve.wait_ge(s_cxh, c + 1)
                    for q in range(CT):
                        last = normalize(pay[0][:, 0, q, 0:P], xs[:, bass.ds(c * CT + q, 1), :].rearrange("p a d -> p (a d)"), q)
                        if q < CT - 1:
                            D(last)
                    last.then_inc(s_cx, 1)
                    dve.wait_ge(s_cf, c + 1)
                    D(dve.tensor_copy(f12[:, bass.ds(c * CT, CT), :], PGT[:, 0:2 * CT].rearrange("p (t n) -> p t n", t=CT)))
                    D.wait()
                    dve.sem_inc(s_cfr, 1)

            def column_sums(U):
                dve.tensor_reduce(csr[:], xh[:].rearrange("p t d -> p d t"), AX.X, ALU.add).then_inc(s_csr, 1)
                dve.wait_ge(s_csp, U + 1)
                dve.tensor_copy(cs[:], PG[:, 0:P]).then_inc(s_cs, 1)
                dve.wait_ge(s_cs, U + 1)

            D(dve.tensor_reduce(ext[:, 0:1], f12[:, :, 1], AX.X, ALU.max))
            D(dve.tensor_reduce(ext[:, 1:2], f12[:, :, 1], AX.X, ALU.min))
            D.wait()
            dve.tensor_scalar(ext[:, 1:2], ext[:, 1:2], -1.0, None, ALU.mult).then_inc(s_ext, 1)
            dve.wait_ge(s_cxh, NC + 1)
            column_sums(0)
            dve.wait_ge(s_extr, 1)
            D(dve.tensor_tensor(mid[:], extr[:, 0:1], extr[:, 1:2], ALU.subtract))
            D.wait()
            D(dve.tensor_scalar(mid[:], mid[:], 0.5, None, ALU.mult))
            D.wait()
            D(dve.tensor_scalar(zc[:, 1], f12[:, :, 0], mid[:, 0:1], None, ALU.add))
            D(dve.tensor_scalar(zc[:, 0], f12[:, :, 1], mid[:, 0:1], None, ALU.subtract))
            D.wait()
            D(dve.scalar_tensor_tensor(out=al[:], in0=zc[:, 1], scalar=SLOPE, in1=zc[:, 1], op0=ALU.mult, op1=ALU.max))
            D.wait()
            D(dve.scalar_tensor_tensor(out=zc[:, 2], in0=zc[:, 1], scalar=SLOPE, in1=al[:], op0=ALU.mult, op1=ALU.subtract))
            dve.tensor_tensor(zc[:, 1], zc[:, 1], al[:], ALU.subtract).then_inc(s_zc, 1)
            dve.wait_ge(s_exps, 5)
            D(dve.tensor_tensor(fB[:, 1], fB[:, 0], fB[:, 0], ALU.mult))
            D(dve.tensor_tensor(fD[:, 1], fD[:, 0], fD[:, 0], ALU.mult))
            D(dve.tensor_scalar(ls[:], lsc[:], 1.0, None, ALU.add))
            D.wait()
            D(dve.reciprocal(ls[:], ls[:]))
            D.wait()
            D(dve.tensor_scalar(lsc[:], ls[:], -1.0, 1.0, ALU.mult, ALU.add))
            D(dve.tensor_scalar(nc3[:], ls[:, 3:4], -1.0, None, ALU.mult))
            D.wait()

            def operands_d(g):
                t = slice(g * CT, (g + 1) * CT)
                for n, (f, X) in enumerate(((fB, XB), (fD, XD))):
                    D(dve.tensor_tensor(tmpb[:, :, 0:P], xh[:, t], f[:, 0, t].unsqueeze(2).broadcast_to([P, CT, P]), ALU.mult))
                    for k in range(2):
                        D(dve.tensor_copy(tmpb[:, :, P + k], f[:, k, t]))
                    D.wait()
                    last = split(X[:, t, 0], X[:, t, 1], tmpb[:])
                    if n == 0:
                        D(last)
                        D.wait()
                last.then_inc(s_xb, 1)

            def code(c, jt, slot):
                g, j = jt // CT, jt % CT
                if j == 0:
                    dve.wait_ge(s_cl[0][g % 2], (c * (NG // 2) + g // 2) * 16 + 16)
                part = Cbuf[:, g % 2, j * CW:(j + 1) * CW]
                dve.scalar_tensor_tensor(out=part, in0=nf1[:, slot], scalar=f12[:, jt, 1:2], in1=part,
                                         op0=ALU.is_lt, op1=ALU.add).then_inc(s_code, 1)

            def other(U, c, jt, first):
                g, j = jt // CT, jt % CT
                if U == 0:
                    dve.wait_ge(s_code, c * NT + jt + 1)
                elif j == 0:
                    dve.wait_ge(s_cl[1][g % 2], (c * (NG // 2) + g // 2) * 16 + 16)
                if not (first and jt < 4):
                    dve.wait_ge(s_mu[U], c * NT + jt - 3)
                dve.tensor_scalar(MM[:, jt % 4], Cbuf[:, g % 2, j * CW:(j + 1) * CW], 2.0, None, ALU.is_equal).then_inc(s_mm[U], 1)

            def products_out(U, c):
                dve.wait_ge(s_mu[U], c * NT + NT)
                for q in range((4, 2)[U]):
                    if U == 0:
                        dve.tensor_copy(ev[:, q, 1].rearrange("p h n -> p (h n)"), B[4 + q][:, 0:260]).then_inc(s_evm[U], 1)
                    else:
                        dve.tensor_copy(ev2[:, 2 + q].rearrange("p s h n -> p (s h n)"), B[2 + q][:]).then_inc(s_evm[U], 1)

            def sum_parts(U, c):
                dve.wait_ge(s_evp[U], c * (4, 2)[U] + (4, 2)[U])
                dve.wait_ge(s_evm[U], c * (4, 2)[U] + (4, 2)[U])
                both = (ev, ev2)[U][:].rearrange("p q s h n -> p (q s) h n")
                D(dve.tensor_tensor(both[:, :, 0], both[:, :, 0], both[:, :, 1], ALU.add))
                D.wait()

            def scaled_rows(U, c):
                y = (ev, ev2)[U]
                rows = [y[:, q, 0, 0, 0:P] for q in range(CT)]
                for q in range(CT):
                    D(dve.tensor_scalar(rows[q], rows[q], al[:, bass.ds(c * CT + q, 1)], None, ALU.mult))
                D.wait()
                for q in range(CT):
                    D(dve.scalar_tensor_tensor(out=rows[q], in0=y[:, q, 1, 0, 0:P], scalar=ga[:, bass.ds(c * CT + q, 1)],
                                               in1=rows[q], op0=ALU.mult, op1=ALU.add))
                D.wait()
                for q in range(CT):
                    D(dve.scalar_tensor_tensor(out=rows[q], in0=cs[:], scalar=ep[:, bass.ds(c * CT + q, 1)],
                                               in1=rows[q], op0=ALU.mult, op1=ALU.add))
                D.wait()

            def post_d(c):
                t = bass.ds(c * CT, CT)
                A4, C4, a4, g4, e4 = fA[:, t], fC[:, t], al[:, t], ga[:, t], ep[:, t]
                z = [q8[:, i] for i in range(8)]
                sum_parts(0, c)
                sp_, sm, qp, qm = (ev[:, :, k, 0, P + n] for n in range(2) for k in range(2))
                D(dve.tensor_tensor(z[0], A4, sp_, ALU.mult))
                D(dve.tensor_tensor(z[1], C4, sm, ALU.mult))
                D.wait()
                D(dve.tensor_tensor(z[2], z[0], z[1], ALU.add))
                D.wait()
                D(dve.tensor_scalar(z[3], z[2], 0.0, None, ALU.is_equal))
                D.wait()
                D(dve.scalar_tensor_tensor(out=z[2], in0=z[3], scalar=float(N), in1=z[2], op0=ALU.mult, op1=ALU.add))
                D.wait()
                D(dve.reciprocal(z[4], z[2]))
                D.wait()
                D(dve.tensor_tensor(a4, A4, z[4], ALU.mult))
                D(dve.tensor_tensor(g4, C4, z[4], ALU.mult))
                D(dve.tensor_tensor(e4, z[3], z[4], ALU.mult))
                D.wait()
                D(dve.tensor_tensor(z[5], a4, a4, ALU.mult))
                D(dve.tensor_tensor(z[6], g4, g4, ALU.mult))
                D.wait()
                D(dve.tensor_tensor(z[5], z[5], qp, ALU.mult))
                D(dve.tensor_tensor(z[6], z[6], qm, ALU.mult))
                D.wait()
                D(dve.tensor_tensor(z[5], z[5], z[6], ALU.add))
                D.wait()
                D(dve.tensor_tensor(z[5], z[5], e4, ALU.add))
                D.wait()
                D(dve.tensor_scalar(rsu[:, t], z[5], 0.5, None, ALU.mult))
                D.wait()
                D(dve.tensor_scalar(z[7], rsu[:, t], -1.0, lsc[:, 2:3], ALU.mult, ALU.add))
                scaled_rows(0, c)
                for q in range(CT):
                    row = ev[:, q, 0, 0, 0:P]
                    xrow = xh[:, bass.ds(c * CT + q, 1), :].rearrange("p a d -> p (a d)")
                    D(dve.scalar_tensor_tensor(out=row, in0=xrow, scalar=z[7][:, q:q + 1], in1=row, op0=ALU.mult, op1=ALU.add))
                D.wait()
                rows, clip = ev[:, :, 0, 0, 0:P], ev[:, :, 1, 0, 0:P]
                D(dve.tensor_scalar(clip, rows, -THRESH, THRESH, ALU.max, ALU.min))
                D.wait()
                D(dve.tensor_tensor(xh[:, t, :], rows, clip, ALU.subtract))
                D.wait()
                for n, (f, X) in enumerate(((fB, XB2), (fD, XD2))):
                    D(dve.tensor_tensor(tmpb[:, :, 0:P], xh[:, t, :], f[:, 0, t].unsqueeze(2).broadcast_to([P, CT, P]), ALU.mult))
                    D.wait()
                    last = split(X[:, t, 0, :], X[:, t, 1, :], tmpb[:, :, 0:P])
                    if n == 0:
                        D(last)
                        D.wait()
                last.then_inc(s_post[0], 1)

            def post_e(c):
                t = bass.ds(c * CT, CT)
                sum_parts(1, c)
                scaled_rows(1, c)
                pu, m = ev2[:, :, 0, 0, :], ev2[:, :, 1, 0, :]
                odd, h = tmo[:, 0], tmo[:, 1]
                dve.wait_ge(s_h0l, c * 16 + 16)
                D(dve.scalar_tensor_tensor(out=odd, in0=pu, scalar=nc3[:, 0:1], in1=xh[:, t, :], op0=ALU.mult, op1=ALU.add))
                D(dve.tensor_scalar(h, h0b[:], lsc[:, 0:1], None, ALU.mult))
                D.wait()
                for q in range(CT):
                    D(dve.scalar_tensor_tensor(out=m[:, q], in0=odd[:, q], scalar=rsu[:, bass.ds(c * CT + q, 1)],
                                               in1=pu[:, q], op0=ALU.mult, op1=ALU.add))
                D(dve.scalar_tensor_tensor(out=h, in0=odd, scalar=ls[:, 0:1], in1=h, op0=ALU.mult, op1=ALU.add))
                D.wait()
                D(dve.tensor_scalar(h, h, lsc[:, 1:2], None, ALU.mult))
                D.wait()
                D(dve.scalar_tensor_tensor(out=h, in0=m, scalar=ls[:, 1:2], in1=h, op0=ALU.mult, op1=ALU.add))
                D.wait()
                dve.tensor_tensor(chunk_of(c), chunk_of(c), h, ALU.add).then_inc(s_post[1], 1)
                wait_alone(dve, need, s_post[1], c + 1)
                statistics(chunk_of(c))

            def tail_u(U, what, c):
                if what == "out":
                    products_out(U, c)
                elif what == "post":
                    (post_d, post_e)[U](c)
                elif U and what == "norm":
                    payload(1, c, c + (NG + 2 * NC))
                elif U and what == "top":
                    top_two(1, c)
                elif U and what == "pos":
                    positions(1, c)

            def chunk_d(c, slot, tail, first, waited):
                dve.wait_ge(s_nfl[slot], waited)
                for g in range(NG):
                    if first:
                        operands_d(g)
                    for j in range(CT):
                        code(c, g * CT + j, slot)
                    for j in range(CT):
                        jt = g * CT + j
                        other(0, c, jt, first)
                        if tail is not None:
                            tail_u(0, E_DVE.get(jt), tail)

            chunk_d(0, 0, None, True, 16)
            with D.loop((NC - 2) // 2, 82) as p2:
                chunk_d(p2 * 2 + 1, 1, p2 * 2, False, p2 * 16 + 16)
                chunk_d(p2 * 2 + 2, 0, p2 * 2 + 1, False, p2 * 16 + 32)
            chunk_d(NC - 1, 1, NC - 2, False, 16 * NC // 2)
            for what in E_DVE.values():
                tail_u(0, what, NC - 1)
            dve.wait_ge(s_post[0], NC)
            column_sums(1)
            for jt in range(NT):
                other(1, 0, jt, True)
            with D.loop(NC - 1, 61) as t:
                for jt in range(NT):
                    other(1, t + 1, jt, False)
                    tail_u(1, E_DVE.get(jt), t)
            for what in E_DVE.values():
                tail_u(1, what, NC - 1)
            tile_table(1)
            weights(1)
            experts(1)
            dve.wait_ge(s_cxh, 2 * NC + 1)
            with D.loop(NC // 2, 54) as c2:
                for slot in range(2):
                    c = c2 * 2 + slot
                    combine(1, c, c2, slot)
                    y = xh[:, bass.ds(c * CT, CT), :]
                    statistics(y)
                    inverse_root(c + (NG + 3 * NC))
                    for q in range(CT):
                        row = xh[:, bass.ds(c * CT + q, 1), :].rearrange("p a d -> p (a d)")
                        D(normalize(row, row, q))
                    D.wait()
                    D(dve.tensor_tensor(y, y, gam[:].unsqueeze(1).broadcast_to([P, CT, P]), ALU.mult))
                    D.wait()
                    D(dve.tensor_tensor(y, y, bet[:].unsqueeze(1).broadcast_to([P, CT, P]), ALU.add))
                    D.wait()
                    dve.tensor_tensor(chunk_of(c), chunk_of(c), y, ALU.add).then_inc(s_fin, 1)


def kernel(**inputs):
    import concourse.bacc as bacc
    from concourse.bass_utils import run_bass_kernel_spmd

    v = {k: np.asarray(w) for k, w in inputs.items()}

    def split_tiles(w):
        return w.reshape(E, 2, P, P).transpose(2, 0, 1, 3)

    adj = v["adj"].T.reshape(NG, CT, P, NC, CW).transpose(3, 0, 2, 1, 4).reshape(NC * NG, P, CT * CW)
    arrays = {
        "x": v["x"],
        "adjT": adj,
        "x2": v["L0_gnn_x2"],
        "eps": np.concatenate([v["L0_gnn_eps1"], v["L0_gnn_eps2"]]),
        "WT": np.concatenate([v["L0_gnn_W1"], v["L0_gnn_W2"]]).transpose(2, 0, 1),
        "bT": np.concatenate([v["L0_gnn_b1"], v["L0_gnn_b2"]]).T,
        "WmT": v["L0_gnn_Wm"].T.reshape(2, P, P).transpose(1, 0, 2),
        "bm": v["L0_gnn_bm"],
        "gate_w": np.stack([v["L0_ffn_gate_w"], v["L1_ffn_gate_w"]], axis=1),
        "gate_b": np.stack([v["L0_ffn_gate_b"], v["L1_ffn_gate_b"]]),
        "w12": np.concatenate([v["L0_ffn_w1"], v["L0_ffn_w2"]], axis=2).transpose(1, 0, 2),
        "w3": split_tiles(v["L0_ffn_w3"]),
        "h0": v["L1_gnn_h0"],
        "a": v["L1_gnn_a"].reshape(2, P).T,
        "temp": v["L1_gnn_temp"],
        "ew1": v["L1_ffn_w1"].transpose(1, 0, 2),
        "eb1": v["L1_ffn_b1"].reshape(E, 2, P).transpose(2, 0, 1),
        "ew2": split_tiles(v["L1_ffn_w2"]),
        "eb2": v["L1_ffn_b2"],
        "gamma": v["L1_ffn_gamma"],
        "beta": v["L1_ffn_beta"],
    }
    arrays = {f"in_{k}": np.ascontiguousarray(w) for k, w in arrays.items()}
    nc = bacc.Bacc("TRN2", target_bir_lowering=False, num_devices=1)
    args = [nc.dram_tensor(k, w.shape, mybir.dt.from_np(w.dtype), kind="ExternalInput").ap() for k, w in arrays.items()]
    out = nc.dram_tensor("out_dram", (N, P), F32, kind="ExternalOutput").ap()
    bass_gnn_moe_kernel(nc, *args, out)
    return run_bass_kernel_spmd(nc, [arrays], core_ids=[0]).results[0]["out_dram"]
```

```python
from contextlib import ExitStack, contextmanager

import numpy as np
import concourse.bass as bass
from concourse import mybir

ALU = mybir.AluOpType
ACT = mybir.ActivationFunctionType
AX = mybir.AxisListType
F32 = mybir.dt.float32
F32R = mybir.dt.float32r
U32 = mybir.dt.uint32
U8 = mybir.dt.uint8

P = 128
N = 4096
NT = N // P
CT = 4
CW = CT * P
NC = N // CW
NG = NT // CT
E = 16
H = 256
CAP = N + P
ROW = P + 1
ST = 80
RS = 10
AHEAD = 4
RF = 5
EPS = 1e-5
THRESH = 1e-6
SLOPE = 0.2


def wait_alone(eng, need, sem, value):
    if isinstance(value, int):
        eng.wait_ge(sem, value)
    else:
        eng.reg_mov(need, value)
        eng.wait_ge(sem, 1)
        eng.wait_ge(sem, need)


class Steps:

    def __init__(self, eng, sem, need):
        self.eng, self.sem, self.need, self.base, self.n = eng, sem, need, 0, 0

    def __call__(self, instruction):
        instruction.then_inc(self.sem, 1)
        self.n += 1

    def wait(self):
        self.eng.wait_ge(self.sem, self.base + self.n)

    def wait_alone(self):
        wait_alone(self.eng, self.need, self.sem, self.base + self.n)

    @contextmanager
    def loop(self, trips, each):
        start = self.base + self.n
        with self.eng.Fori(0, trips) as lap:
            self.base, self.n = lap * each + start, 0
            yield lap
            assert self.n == each, f"a lap counts {self.n}"
        self.base, self.n = start + trips * each, 0


def bass_gnn_moe_kernel(nc, x, adjT, x2, eps, WT, bT, WmT, bm, gate_w, gate_b, w12, w3, h0, a, temp,
                        ew1, eb1, ew2, eb2, gamma, beta, out):
    mask_d = nc.dram_tensor("mask_d", [NC * NG, P, CT * CW], U8).ap()
    code_d = nc.dram_tensor("code_d", [NC * NG, P, CT * CW], U8).ap()
    sorted_d = [nc.dram_tensor(f"sorted_d{L}", [E * CAP + P, ROW], F32).ap() for L in range(2)]
    expert_d = [nc.dram_tensor(f"expert_d{L}", [2 * N, P], F32).ap() for L in range(2)]
    nf1_d = nc.dram_tensor("nf1_d", [NC, CW], F32).ap()

    x_v = x.rearrange("(t p) d -> p t d", p=P)
    x2_v = x2.rearrange("(t p) d -> p t d", p=P)
    h0_v = h0.rearrange("(t p) d -> p t d", p=P)
    out_v = out.rearrange("(t p) d -> p t d", p=P)

    with ExitStack() as ctx:
        def sb(name, shape, dt=F32):
            return ctx.enter_context(nc.sbuf_tensor(name, shape, dt))

        def sem(name):
            return ctx.enter_context(nc.semaphore(name))

        xs = sb("xs", [P, NT, P])
        xh = sb("xh", [P, NT, P])
        ident = sb("ident", [P, P])
        ones = sb("ones", [P, P])
        upper = sb("upper", [P, P])
        bTs = sb("bTs", [P, 6])
        gws = sb("gws", [P, 2, E])
        gbs = sb("gbs", [P, 2, E])
        a_s = sb("a_s", [P, 2])
        gam = sb("gam", [P, P])
        bet = sb("bet", [P, P])
        eps1 = sb("eps1", [P, 2])
        ls = sb("ls", [P, 5])
        lsc = sb("lsc", [P, 5])
        k12 = sb("k12", [P, 2])
        nc3 = sb("nc3", [P, 1])
        iota_e = sb("iota_e", [P, E])
        ecap = sb("ecap", [P, E])
        kcol = sb("kcol", [P, 1])
        tok = sb("tok", [P, 2, NT], U32)
        fill = sb("fill", [P, ROW])
        minus2 = sb("minus2", [P, 1])
        run = sb("run", [P, E])
        cnt = sb("cnt", [P, 4, E])
        tcol = sb("tcol", [P, 4])
        endu = sb("endu", [P, E], U32)
        nuu = sb("nuu", [P, E], U32)
        tiles = sb("tiles", [1, 2, P], U32)
        stat = sb("stat", [P, 2, CT, 6])
        mv = sb("mv", [P, 2, CT, 2])
        zero4 = sb("zero4", [P, CT])
        nmr = sb("nmr", [P, 2, CT])
        varE = sb("varE", [P, 2, CT])
        epsc = sb("epsc", [P, 2, CT])
        rstd = sb("rstd", [P, 2, CT])
        lg = sb("lg", [P, CT, E])
        top = sb("top", [P, CT, 8])
        topi = sb("topi", [P, CT, 8], U32)
        topf = sb("topf", [P, CT, 8])
        oh = sb("oh", [P, 3, CT, E])
        posf = sb("posf", [P, 2, CT, E])
        posr = sb("posr", [P, 2, CT])
        pos = sb("pos", [P, 2, CT], U32)
        dl = sb("dl", [P, NT])
        wt = sb("wt", [P, 2, NT])
        f12 = sb("f12", [P, NT, 2])
        ext = sb("ext", [P, 2])
        extr = sb("extr", [P, 2])
        mid = sb("mid", [P, 1])
        zc = sb("zc", [P, 3, NT])
        fB = sb("fB", [P, 2, NT])
        fD = sb("fD", [P, 2, NT])
        fA = sb("fA", [P, NT])
        fC = sb("fC", [P, NT])
        al = sb("al", [P, NT])
        ga = sb("ga", [P, NT])
        ep = sb("ep", [P, NT])
        rsu = sb("rsu", [P, NT])
        q8 = sb("q8", [P, 8, CT])
        csr = sb("csr", [P, P])
        cs = sb("cs", [P, P])
        b1c = sb("b1c", [P, E, 2])

        R1_SIZE, R2_SIZE = NT * 4 * 130 * 4, 100544
        base1 = (nc.sbuf_base + 31) // 32 * 32
        assert base1 + R1_SIZE + R2_SIZE <= nc.sbuf_usable_end, (base1 + R1_SIZE + R2_SIZE, nc.sbuf_usable_end)
        base2 = base1 + R1_SIZE

        def at(region, offset, name, shape, dt=F32):
            size = int(np.prod(shape[1:])) * (1 if dt == U8 else 4)
            start, limit = (base1, R1_SIZE) if region == 1 else (base2, R2_SIZE)
            assert offset + size <= limit, (name, offset + size, limit)
            return nc.alloc_sbuf_tensor_at(name, shape, dt, offset=start + offset)

        XHI = at(1, 0, "XHI", [P, NT, 2 * P], F32R)
        XLO = at(1, 32768, "XLO", [P, NT, 2 * P], F32R)
        W12s = at(2, 0, "W12s", [P, E, 2 * H])
        W3s = at(2, 32768, "W3s", [P, E, 2, P])
        Abuf = at(2, 49152, "Abuf", [P, 2, CT, CW])
        HI = at(2, 65536, "HI", [P, 4, CW], F32R)
        LO = at(2, 73728, "LO", [P, 4, CW], F32R)
        Mbuf = at(2, 81920, "Mbuf", [P, 2, CT * CW], U8)
        hT = at(2, 86016, "hT", [P, 2, CW])
        stg = at(2, 86016, "stg", [P, CT, P])
        WTs = at(2, 96320, "WTs", [P, 6, P])
        WmTs = at(2, 99392, "WmTs", [P, 2, P])
        XB = at(1, 0, "XB", [P, NT, 2, 130], F32R)
        XD = at(1, 33280, "XD", [P, NT, 2, 130], F32R)
        XB2 = at(2, 0, "XB2", [P, NT, 2, P], F32R)
        XD2 = at(2, 32768, "XD2", [P, NT, 2, P], F32R)
        MP = at(2, 65536, "MP", [P, 4, CW], F32R)
        MM = at(2, 73728, "MM", [P, 4, CW], F32R)
        Cbuf = at(2, 81920, "Cbuf", [P, 4, CT * CW], U8)
        nfrow = at(2, 0, "nfrow", [1, N])
        nf1 = at(2, 90112, "nf1", [P, 2, CW])
        ev = at(2, 94208, "ev", [P, CT, 2, 130])
        ev2 = at(2, 94208, "ev2", [P, CT, 2, P])
        tmpx = at(2, 94208, "tmpx", [P, CT, 130])
        tmpb = at(2, 98400, "tmpb", [P, CT, 130])
        V1s = at(1, 0, "V1s", [P, E, H])
        V2s = at(1, 16384, "V2s", [P, E, 2, P])
        C2s = at(1, 32768, "C2s", [P, E, P])
        h0b = at(1, 58368, "h0b", [P, CT, P])
        odd = at(1, 60416, "odd", [P, CT, P])
        h0s = at(1, 62464, "h0s", [P, CT, P])
        pay = [at(r, o, f"pay{L}", [P, 2, CT, ROW]) for L, (r, o) in enumerate(((2, 90112), (1, 40960)))]
        xTb = [at(r, o + 4160, f"xT{L}", [P, CW]) for L, (r, o) in enumerate(((2, 90112), (1, 40960)))]
        xTc = at(2, 96320, "xTc", [P, CW])
        xin = at(2, 49152, "xin", [P, RS, ROW])
        ey = at(2, 54400, "ey", [P, RS, P])
        exT = at(2, 59520, "exT", [P, 2, P])
        eg = at(2, 60544, "eg", [P, 2, H])
        ehid = at(2, 62592, "ehid", [P, 2, H])
        ehT = at(2, 64640, "ehT", [P, 2, 2, P])
        yb = at(2, 69632, "yb", [P, 4, 2, CT, P])
        B = [ctx.enter_context(nc.psum_tensor(f"B{i}", [P, 512], F32)) for i in range(8)]

        s_x, s_x2 = [sem(f"s_x{i}") for i in range(2)], [sem(f"s_x2{i}") for i in range(2)]
        s_xh, s_cst, s_w, s_w1 = sem("s_xh"), sem("s_cst"), sem("s_w"), sem("s_w1")
        s_pool = sem("s_pool")
        s_const = sem("s_const")
        s_dve = sem("s_dve")
        s_fillin = sem("s_fillin")
        s_bmr = sem("s_bmr")
        s_ad = [sem(f"s_ad{i}") for i in range(2)]
        s_mst = [sem(f"s_mst{i}") for i in range(2)]
        s_hi, s_lo, s_used, s_mk, s_xp = sem("s_hi"), sem("s_lo"), sem("s_used"), sem("s_mk"), sem("s_xp")
        s_h0, s_h1, s_m, s_r, s_g = sem("s_h0"), sem("s_h1"), sem("s_m"), sem("s_r"), sem("s_g")
        s_var, s_root = sem("s_var"), sem("s_root")
        s_xn = [sem(f"s_xn{L}") for L in range(2)]
        s_p2 = [sem(f"s_p2{L}") for L in range(2)]
        s_tr = [sem(f"s_tr{L}") for L in range(2)]
        s_xT = [sem(f"s_xT{L}") for L in range(2)]
        s_gt = [sem(f"s_gt{L}") for L in range(2)]
        s_oh = [sem(f"s_oh{L}") for L in range(2)]
        s_pp = [sem(f"s_pp{L}") for L in range(2)]
        s_pos = [sem(f"s_pos{L}") for L in range(2)]
        s_sc = [sem(f"s_sc{L}") for L in range(2)]
        s_pfree = [sem(f"s_pfree{L}") for L in range(2)]
        s_cn = [sem(f"s_cn{L}") for L in range(2)]
        s_end = [sem(f"s_end{L}") for L in range(2)]
        s_tl = [sem(f"s_tl{L}") for L in range(2)]
        s_tt = [sem(f"s_tt{L}") for L in range(2)]
        s_tu = [sem(f"s_tu{L}") for L in range(2)]
        s_tail = [[sem(f"s_tail{L}{i}") for i in range(2)] for L in range(2)]
        s_ld = [sem(f"s_ld{i}") for i in range(RS)]
        s_etx = sem("s_etx")
        s_exT = sem("s_exT")
        s_eh = sem("s_eh")
        s_eg = sem("s_eg")
        s_ehid = sem("s_ehid")
        s_eth = sem("s_eth")
        s_ehT = sem("s_ehT")
        s_eo = sem("s_eo")
        s_ey = sem("s_ey")
        s_est = [sem(f"s_est{i}") for i in range(RF)]
        s_efree = [sem(f"s_efree{L}") for L in range(2)]
        s_eall = [sem(f"s_eall{L}") for L in range(2)]
        s_yl = [sem(f"s_yl{i}") for i in range(4)]
        s_wd = [sem(f"s_wd{L}") for L in range(2)]
        s_we = [sem(f"s_we{L}") for L in range(2)]
        s_cb = [sem(f"s_cb{L}") for L in range(2)]
        s_cx, s_ct, s_cxT, s_cf, s_cr, s_crow = (sem(n) for n in ("s_cx", "s_ct", "s_cxT", "s_cf", "s_cr", "s_crow"))
        s_nfst = sem("s_nfst")
        s_cxh, s_cs = sem("s_cxh"), sem("s_cs")
        s_ext, s_extr, s_zc, s_exps, s_ls = (sem(n) for n in ("s_ext", "s_extr", "s_zc", "s_exps", "s_ls"))
        s_xb, s_xd, s_xb2, s_fac = (sem(n) for n in ("s_xb", "s_xd", "s_xb2", "s_fac"))
        s_x2h, s_x2s, s_bm, s_stg = (sem(n) for n in ("s_x2h", "s_x2s", "s_bm", "s_stg"))
        s_h0s, s_h0x = sem("s_h0s"), sem("s_h0x")
        s_nmr, s_norm = sem("s_nmr"), sem("s_norm")
        s_csr, s_csp = sem("s_csr"), sem("s_csp")
        s_cl = [sem(f"s_cl{i}") for i in range(4)]
        s_cst2 = [sem(f"s_cst2{i}") for i in range(4)]
        s_nfl = [sem(f"s_nfl{i}") for i in range(2)]
        s_code = sem("s_code")
        s_mp = [sem(f"s_mp{U}") for U in range(2)]
        s_mm = [sem(f"s_mm{U}") for U in range(2)]
        s_mu = [sem(f"s_mu{U}") for U in range(2)]
        s_ev = [sem(f"s_ev{U}") for U in range(2)]
        s_post = [sem(f"s_post{U}") for U in range(2)]
        s_h0l = sem("s_h0l")
        s_fin, s_out = sem("s_fin"), [sem("s_out0"), sem("s_out1")]

        ACC, PM, PG, PT, PGT, PPX = B[0:2], B[2:4], B[4], B[5], B[6], B[7]

        block = ctx.enter_context(nc.Block())

        def store_tails(eng, L, half):
            eng.wait_ge(s_end[L], 1)
            ends = [eng.alloc_register(f"end{L}{half}{i}") for i in range(E // 2)]
            for i, r in enumerate(ends):
                e = half * (E // 2) + i
                eng.reg_load(r, endu[0:1, e:e + 1])
            for r in ends:
                row = eng.snap(r, min_val=0, max_val=E * CAP - P)
                eng.dma_start(sorted_d[L][bass.ds(row, P), :], fill[:]).then_inc(s_tail[L][half], 16)
            for r in ends:
                eng.free_register(r)

        @block.sync
        def _(sp):
            need = sp.alloc_register("need_sp")
            for dst, src, done in ((xs, x_v, s_x), (xh, x2_v, s_x2)):
                sp.dma_start(dst[:, 0:CT], src[:, 0:CT, :]).then_inc(done[0], 16)

            def load_adjacency(c, g):
                G = c * NG + g
                if not (isinstance(G, int) and G < 2):
                    wait_alone(sp, need, s_hi, CT * (G - 1))
                    wait_alone(sp, need, s_mk, G - 1)
                sp.dma_start(Abuf[:, g % 2], adjT[bass.ds(G, 1)].rearrange("a p n -> p (a n)")
                             .rearrange("p (t n) -> p t n", t=CT)).then_inc(s_ad[g % 2], 16)

            def store_mask(G, slot):
                wait_alone(sp, need, s_mk, G + 1)
                sp.dma_start(mask_d[bass.ds(G, 1)].rearrange("a p n -> p (a n)"), Mbuf[:, slot]).then_inc(s_mst[slot], 16)

            for g in range(NG):
                load_adjacency(0, g)
                if g == 0:
                    for dst, src, done in ((xs, x_v, s_x), (xh, x2_v, s_x2)):
                        sp.dma_start(dst[:, CT:], src[:, CT:, :]).then_inc(done[1], 16)
                if g == 1:
                    for dst, src in ((WTs[:], WT), (WmTs[:], WmT), (bTs[:], bT), (gws[:], gate_w), (a_s[:], a),
                                     (gbs[:], gate_b.partition_broadcast(P)),
                                     (gam[:], gamma.partition_broadcast(P)), (bet[:], beta.partition_broadcast(P)),
                                     (eps1[:], eps.partition_broadcast(P)), (ls[:], temp.partition_broadcast(P)),
                                     (b1c[:], eb1)):
                        sp.dma_start(dst, src).then_inc(s_cst, 16)
                    sp.dma_start(csr[:], bm.partition_broadcast(P)).then_inc(s_bmr, 16)
                if g == 3:
                    sp.dma_start(W12s[:], w12).then_inc(s_w, 16)
                    sp.dma_start(W3s[:], w3).then_inc(s_w, 16)
                    wait_alone(sp, need, s_const, 1)
                    for L in range(2):
                        sp.dma_start(sorted_d[L][E * CAP:E * CAP + P, :], fill[:]).then_inc(s_fillin, 16)
                if g:
                    store_mask(g - 1, (g - 1) % 2)
            with sp.Fori(1, NC) as c:
                for g in range(NG):
                    load_adjacency(c, g)
                    store_mask(c * NG + g - 1, (g - 1) % 2)
            store_mask(NC * NG - 1, 1)

            def moe_loads(L):
                store_tails(sp, L, 0)
                r = sp.alloc_register(f"row{L}")
                wait_alone(sp, need, s_tu[L], 1)
                for half in range(2):
                    sp.wait_ge(s_tail[L][half], 16 * E // 2)
                wait_alone(sp, need, s_sc[L], 16 * 2 * NT)
                wait_alone(sp, need, s_fillin, 32)
                with sp.Fori(0, ST // RS) as lap:
                    for u in range(RS):
                        k = lap * RS + u
                        sp.reg_load(r, tiles[0:1, 1, bass.ds(k, 1)])
                        row = sp.snap(r, min_val=0, max_val=E * CAP)
                        wait_alone(sp, need, s_efree[L], k + 1)
                        sp.dma_start(xin[:, u], sorted_d[L][bass.ds(row, P), :]).then_inc(s_ld[u], 16)
                wait_alone(sp, need, s_eall[L], 1)
                y_v = expert_d[L].rearrange("(k t p) d -> k p t d", k=2, p=P)
                for c in range(NC):
                    if c >= 4:
                        sp.wait_ge(s_cb[L], c // 2 - 1)
                    for k in range(2):
                        sp.dma_start(yb[:, c % 4, k], y_v[k, :, c * CT:(c + 1) * CT, :]).then_inc(s_yl[c % 4], 16)
                if L:
                    for c in range(NC):
                        store_out(c)

            def store_out(c):
                wait_alone(sp, need, s_fin, c + 1)
                sp.dma_start(out_v[:, c * CT:(c + 1) * CT, :], xs[:, c * CT:(c + 1) * CT, :]).then_inc(s_out[c % 2], 16)

            moe_loads(0)

            sp.wait_ge(s_crow, NC)
            sp.dma_start(nf1_d.rearrange("c n -> (c n)").unsqueeze(0), nfrow[:]).then_inc(s_nfst, 16)
            sp.wait_ge(s_nfst, 16)

            def load_codes(U, G, slot):
                src = (mask_d, code_d)[U]
                sp.dma_start(Cbuf[:, slot], src[bass.ds(G, 1)].rearrange("a p n -> p (a n)")).then_inc(s_cl[slot], 16)

            def load_nf1(c, slot):
                sp.dma_start(nf1[:, slot], nf1_d[bass.ds(c, 1), :].rearrange("a n -> (a n)").partition_broadcast(P)).then_inc(s_nfl[slot], 16)

            def codes_done(U, G):
                wait_alone(sp, need, s_mp[U], CT * (G + 1))
                wait_alone(sp, need, s_mm[U], CT * (G + 1))

            for i in range(2):
                wait_alone(sp, need, s_mst[i], 16 * NC * NG // 2)
            sp.wait_ge(s_cb[0], NC // 2)
            for i in range(4):
                load_codes(0, i, i)
            load_nf1(0, 0)

            def group_d(c, g, first=False, last=False):
                G = c * NG + g
                wait_alone(sp, need, s_code, CT * (G + 1))
                sp.dma_start(code_d[bass.ds(G, 1)].rearrange("a p n -> p (a n)"), Cbuf[:, g % 4]).then_inc(s_cst2[g % 4], 16)
                if not (first and g == 0 or last and g >= NG - 3):
                    codes_done(0, G - 1)
                    stores = c * (NG // 4) + ((g - 1) // 4 + 1)
                    wait_alone(sp, need, s_cst2[(g - 1) % 4], stores * 16)
                    load_codes(0, G + 3, (g + 3) % 4)

            load_nf1(1, 1)
            for g in range(NG):
                group_d(0, g, first=True)
            with sp.Fori(0, (NC - 2) // 2) as lap:
                for d in range(2):
                    c = lap * 2 + (d + 1)
                    load_nf1(c + 1, d)
                    for g in range(NG):
                        group_d(c, g)
            for g in range(NG):
                group_d(NC - 1, g, last=True)
            codes_done(0, NC * NG - 1)
            for i in range(4):
                sp.wait_ge(s_cst2[i], 16 * NC * NG // 4)
            for i in range(4):
                load_codes(1, i, i)
            wait_alone(sp, need, s_mu[0], NC * NT)
            for dst, src in ((V1s[:], ew1), (V2s[:], ew2), (C2s[:], eb2.partition_broadcast(P))):
                sp.dma_start(dst, src).then_inc(s_w1, 16)

            def group_e(c, g, last):
                codes_done(1, c * NG + g)
                if not (last and g >= NG - 4):
                    load_codes(1, c * NG + g + 4, g % 4)

            def chunk_e(c, first, last):
                for g in range(NG):
                    group_e(c, g, last)
                    if g == NG - 2:
                        if not first:
                            wait_alone(sp, need, s_post[1], c)
                        sp.dma_start(h0b[:], h0_v[:, bass.ds(c * CT, CT), :]).then_inc(s_h0l, 16)

            chunk_e(0, True, False)
            with sp.Fori(1, NC - 1) as c:
                chunk_e(c, False, False)
            chunk_e(NC - 1, False, True)
            moe_loads(1)
            for i in range(2):
                wait_alone(sp, need, s_out[i], 16 * NC // 2)

        @block.gpsimd
        def _(pool):
            need = pool.alloc_register("need_pool")
            S = Steps(pool, s_pool, need)
            S(pool.memset(ident[:], 0.0))
            S(pool.memset(ones[:], 1.0))
            S(pool.memset(fill[:, 0:P], 0.0))
            S(pool.memset(minus2[:], -2.0))
            S(pool.memset(zero4[:], 0.0))
            S(pool.memset(epsc[:, 0, :], EPS))
            S(pool.memset(epsc[:, 1, :], -0.5))
            S(pool.iota(fill[:, P:P + 1].bitcast(U32), pattern=[[1, 1]], base=2 * N, channel_multiplier=1))
            S(pool.iota(tok[:], pattern=[[N, 2], [P, NT]], base=0, channel_multiplier=1))
            S(pool.iota(iota_e[:], pattern=[[1, E]], base=0, channel_multiplier=0, allow_small_or_imprecise_dtypes=True))
            S(pool.iota(ecap[:], pattern=[[CAP, E]], base=0, channel_multiplier=0, allow_small_or_imprecise_dtypes=True))
            S(pool.iota(kcol[:], pattern=[[1, 1]], base=0, channel_multiplier=1, allow_small_or_imprecise_dtypes=True))
            S.wait()
            S(pool.affine_select(out=ident[:], in_=ident[:], compare_op=ALU.not_equal, fill=1.0, base=0,
                                 pattern=[[-1, P]], channel_multiplier=1))
            S(pool.affine_select(out=upper[:], in_=ones[:], compare_op=ALU.is_gt, fill=0.0, base=0,
                                 pattern=[[1, P]], channel_multiplier=-1))
            S.wait()
            pool.sem_inc(s_const, 1)

            def scatter_chunk(L, c):
                wait_alone(pool, need, s_p2[L], c + 1)
                pool.wait_ge(s_pos[L], c + 1)
                for q in range(CT):
                    for k in range(2):
                        pool.indirect_dma_start(
                            out=sorted_d[L], out_offset=bass.IndirectOffsetOnAxis(ap=pos[:, k, q:q + 1], axis=0),
                            in_=pay[L][:, k, q, :], in_offset=None,
                            bounds_check=E * CAP - 1, oob_is_err=False).then_inc(s_sc[L], 16)
                if L:
                    rows = xs[:, bass.ds(c * CT, CT), :]
                    S(pool.tensor_tensor(rows, rows, bet[:].unsqueeze(1).broadcast_to([P, CT, P]), ALU.add))
                pool.wait_ge(s_sc[L], c * (16 * 2 * CT) + 16 * 2 * CT)
                pool.sem_inc(s_pfree[L], 1)

            def scatter_results(L):
                def scattered(lap, u):
                    done = lap * (RS // RF) + (u // RF + 1) + L * (ST // RF)
                    pool.wait_ge(s_est[u % RF], done * 16)
                    pool.sem_inc(s_efree[L], 1)

                pool.sem_inc(s_efree[L], RS)
                with pool.Fori(0, ST // RS) as lap:
                    for u in range(RS):
                        wait_alone(pool, need, s_ey, lap * RS + u + 1 + L * ST)
                        pool.indirect_dma_start(
                            out=expert_d[L], out_offset=bass.IndirectOffsetOnAxis(ap=xin[:, u, P:P + 1].bitcast(U32), axis=0),
                            in_=ey[:, u], in_offset=None,
                            bounds_check=2 * N - 1, oob_is_err=False).then_inc(s_est[u % RF], 16)
                        if u:
                            scattered(lap, u - 1)
                    scattered(lap, RS - 1)
                pool.sem_inc(s_eall[L], 1)

            def root(n, slot=0):
                wait_alone(pool, need, s_var, n + 1)
                S(pool.tensor_tensor(varE[:, slot], mv[:, slot, :, 1], epsc[:, 0, :], ALU.add))
                S.wait()
                pool.tensor_tensor(rstd[:, slot], varE[:, slot], epsc[:, 1, :], ALU.pow).then_inc(s_root, 1)

            def add_h0(c):
                wait_alone(pool, need, s_h0s, c + 1)
                rows = xs[:, bass.ds(c * CT, CT), :]
                pool.tensor_tensor(rows, rows, h0s[:], ALU.add).then_inc(s_h0x, 1)

            def operands_of(g, X, src, factor, tmp):
                S(pool.tensor_tensor(tmp[:, :, 0:P], src, factor[:, 0, g].unsqueeze(2).broadcast_to([P, CT, P]), ALU.mult))
                width = tmp.shape[2]
                if width > P:
                    for k in range(2):
                        S(pool.tensor_copy(tmp[:, :, P + k], factor[:, k, g]))
                S.wait_alone()
                S(pool.tensor_copy(X[:, g, 0, :], tmp))
                S.wait_alone()
                return pool.tensor_tensor(X[:, g, 1, :], tmp, X[:, g, 0, :].bitcast(F32), ALU.subtract)

            for g in range(NG):
                t = slice(g * CT, (g + 1) * CT)
                root(g)
                pool.wait_ge(s_x2h, g + 1)
                pool.tensor_tensor(XLO[:, t, P:], xh[:, t], XHI[:, t, P:].bitcast(F32), ALU.subtract).then_inc(s_x2s, 1)
                if g == 0:
                    pool.wait_ge(s_bmr, 16)
                pool.wait_ge(s_xp, g + 1)
                pool.tensor_tensor(xs[:, t], xs[:, t], csr[:].unsqueeze(1).broadcast_to([P, CT, P]), ALU.add).then_inc(s_bm, 1)
            for L in range(2):
                pool.sem_inc(s_pfree[L], 1)
                with S.loop(NC, 1 + L) as c:
                    if L:
                        add_h0(c)
                    root(c + (NG + 2 * NC * L))
                    scatter_chunk(L, c)
                scatter_results(L)
                if L == 0:
                    with S.loop(NC // 2, 2) as lap:
                        for i in range(2):
                            root(lap * 2 + (i + NG + NC), i)
                    pool.wait_ge(s_ext, 1)
                    pool.partition_all_reduce(extr[:], ext[:], P, bass.bass_isa.ReduceOp.max).then_inc(s_extr, 1)
                    pool.wait_ge(s_fac, 1)
                    for g in range(NG):
                        t = slice(g * CT, (g + 1) * CT)
                        operands_of(t, XD, xh[:, t], fD, tmpx[:]).then_inc(s_xd, 1)
                        pool.wait_ge(s_xd, g + 1)
                    with S.loop(NC, 5) as c:
                        wait_alone(pool, need, s_post[0], c + 1)
                        t = bass.ds(c * CT, CT)
                        S(operands_of(t, XB2, xh[:, t, :], fB, tmpb[:, :, 0:P]))
                        S.wait_alone()
                        operands_of(t, XD2, xh[:, t, :], fD, tmpb[:, :, 0:P]).then_inc(s_xb2, 1)
                        wait_alone(pool, need, s_xb2, c + 1)

            def norm_factors(c, i):
                root(c + (NG + 3 * NC), i)
                wait_alone(pool, need, s_root, c + (NG + 3 * NC + 1))
                S(pool.tensor_tensor(varE[:, i], mv[:, i, :, 0], rstd[:, i], ALU.mult))
                S.wait_alone()
                pool.tensor_tensor(nmr[:, i], zero4[:], varE[:, i], ALU.subtract).then_inc(s_nmr, 1)

            def finish(c):
                y, r = (z[:, bass.ds(c * CT, CT), :] for z in (xh, xs))
                wait_alone(pool, need, s_norm, c * CT + CT)
                S(pool.tensor_tensor(y, y, gam[:].unsqueeze(1).broadcast_to([P, CT, P]), ALU.mult))
                S.wait_alone()
                pool.tensor_tensor(r, r, y, ALU.add).then_inc(s_fin, 1)

            pool.sem_inc(s_nmr, 1)
            norm_factors(0, 0)
            norm_factors(1, 1)
            with S.loop(NC // 2 - 1, 6) as lap:
                for i in range(2):
                    finish(lap * 2 + i)
                    norm_factors(lap * 2 + (i + 2), i)
            finish(NC - 2)
            finish(NC - 1)

        A_ACT = {2: "in", 5: "relu0", 8: "relu1", 11: "relu2", 20: "copy", 21: "xT"}
        A_DVE = {2: "in", 14: "add", 18: "norm", 23: "top", 29: "pos"}
        A_PE = {1: "mlp0", 4: "mlp1", 7: "mlp2", 10: "merge", 17: "turn", 19: "gate", 25: "prefix"}
        D_DVE = {2: "out", 5: "post"}
        E_ACT = {3: "h0", 24: "copy", 25: "xT"}
        E_DVE = {2: "out", 3: "post", 22: "norm", 26: "top", 31: "pos"}
        E_PE = {21: "turn", 23: "gate", 28: "prefix"}

        @block.scalar
        def _(act):
            def leading_part(c, jt, first):
                g, j = jt // CT, jt % CT
                if j == 0:
                    act.wait_ge(s_ad[g % 2], (c * (NG // 2) + g // 2) * 16 + 16)
                if not (first and jt < 4):
                    act.wait_ge(s_used, c * NT + jt - 3)
                act.activation(HI[:, jt % 4], Abuf[:, g % 2, j], ACT.Copy).then_inc(s_hi, 1)

            def mlp_in(c):
                act.wait_ge(s_used, c * NT + NT)
                act.activation(hT[:, 0], ACC[0][:], ACT.Identity, scale=eps1[:, 0:1]).then_inc(s_h0, 1)

            def relu(c, layer):
                act.wait_ge(s_m, c * 3 + layer + 1)
                for v in range(2):
                    bias = bTs[:, 3 * v + layer:3 * v + layer + 1]
                    act.activation(hT[:, v], PM[v][:], ACT.Relu, bias=bias).then_inc(s_r, 1)

            def second_copy(L, c):
                act.wait_ge(s_xn[L], c + 1)
                if L:
                    act.activation(xh[:, bass.ds(c * CT, CT), :], pay[L][:, 0, :, 0:P], ACT.Copy).then_inc(s_cxh, 1)
                act.activation(pay[L][:, 1, :, 0:P], pay[L][:, 0, :, 0:P], ACT.Copy).then_inc(s_p2[L], 1)

            def xT_out(L, c):
                act.wait_ge(s_tr[L], c + 1)
                act.activation(xTb[L][:], PT[:], ACT.Copy).then_inc(s_xT[L], 1)

            def tail_a(what, c):
                if what == "in":
                    mlp_in(c)
                elif what in ("relu0", "relu1", "relu2"):
                    relu(c, int(what[4]))
                elif what == "copy":
                    second_copy(0, c)
                elif what == "xT":
                    xT_out(0, c)

            act.wait_ge(s_const, 1)
            for jt in range(NT):
                g = jt // CT
                t = slice(g * CT, (g + 1) * CT)
                if jt % CT == 0:
                    if g < 2:
                        act.wait_ge(s_x2[g], 16)
                    act.activation(XHI[:, t, P:], xh[:, t], ACT.Copy).then_inc(s_x2h, 1)
                    act.wait_ge(s_stg, g + 1)
                    act.activation(XHI[:, t, 0:P], stg[:], ACT.Copy).then_inc(s_xh, 1)
                leading_part(0, jt, True)
            act.wait_ge(s_ls, 1)
            with act.Fori(0, NC - 1) as t:
                for jt in range(NT):
                    leading_part(t + 1, jt, False)
                    tail_a(A_ACT.get(jt), t)
            for what in A_ACT.values():
                tail_a(what, NC - 1)

            def experts(L):
                def x_out(k, u):
                    act.wait_ge(s_etx, k + 1 + L * ST)
                    act.activation(exT[:, u % 2], (B[2], B[5])[u % 2][:, 0:P], ACT.Copy).then_inc(s_exT, 1)

                def h_out(k, u):
                    act.wait_ge(s_eh, k + 1 + L * ST)
                    act.activation(eg[:, u % 2], B[u % 2][:, 0:H], (ACT.Silu, ACT.Copy)[L]).then_inc(s_eg, 1)

                for k in range(RS):
                    x_out(k, k)
                    if k:
                        h_out(k - 1, k - 1)
                with act.Fori(1, ST // RS) as lap:
                    for u in range(RS):
                        x_out(lap * RS + u, u)
                        h_out(lap * RS + (u - 1), (u - 1) % RS)
                h_out(ST - 1, RS - 1)

            def weights(L):
                act.wait_ge(s_wd[L], 1)
                act.activation(wt[:, 1], dl[:], ACT.Exp).then_inc(s_we[L], 1)

            store_tails(act, 0, 1)
            weights(0)
            experts(0)

            def row_out(c, i):
                act.wait_ge(s_cr, c + 1)
                act.activation(nfrow[:, bass.ds(c * CW, CW)], (PG, B[3])[i][0:1, :], ACT.Copy, scale=-1.0).then_inc(s_crow, 1)

            with act.Fori(0, NC // 2) as lap:
                for i in range(2):
                    act.wait_ge(s_ct, lap * 2 + i + 1)
                    act.activation((xTb[0], xTc)[i][:], (PT, B[2])[i][:], ACT.Copy).then_inc(s_cxT, 1)
                for i in range(2):
                    row_out(lap * 2 + i, i)
            act.wait_ge(s_zc, 1)
            act.activation(fB[:, 0], zc[:, 0], ACT.Exp).then_inc(s_exps, 1)
            act.activation(fD[:, 0], zc[:, 0], ACT.Exp, scale=SLOPE).then_inc(s_exps, 1)
            act.activation(fA[:], zc[:, 1], ACT.Exp).then_inc(s_exps, 1)
            act.activation(fC[:], zc[:, 2], ACT.Exp).then_inc(s_exps, 1)
            act.activation(lsc[:], ls[:], ACT.Exp, scale=-1.0).then_inc(s_exps, 1)

            def positive(U, c, jt, first):
                g, j = jt // CT, jt % CT
                if U == 0:
                    act.wait_ge(s_code, c * NT + jt + 1)
                elif j == 0:
                    act.wait_ge(s_cl[g % 4], (c * (NG // 4) + g // 4) * 16 + (16 + 4 * NC * NG))
                if not (first and jt < 4):
                    act.wait_ge(s_mu[U], c * NT + jt - 3)
                act.activation(MP[:, jt % 4], Cbuf[:, g % 4, j * CW:(j + 1) * CW], ACT.Relu, bias=minus2[:]).then_inc(s_mp[U], 1)

            def tail_e(what, c, first):
                if what == "h0":
                    act.wait_ge(s_h0l, c * 16 + 16)
                    if not first:
                        act.wait_ge(s_h0x, c)
                    act.activation(h0s[:], h0b[:], ACT.Copy, scale=k12[:, 1:2]).then_inc(s_h0s, 1)
                elif what == "copy":
                    second_copy(1, c)
                elif what == "xT":
                    xT_out(1, c)

            for U in range(2):
                if U:
                    act.wait_ge(s_mu[0], NC * NT)
                for jt in range(NT):
                    positive(U, 0, jt, True)
                for jt in range(NT):
                    positive(U, 1, jt, False)
                    if U:
                        tail_e(E_ACT.get(jt), 0, True)
                with act.Fori(1, NC - 1) as t:
                    for jt in range(NT):
                        positive(U, t + 1, jt, False)
                        if U:
                            tail_e(E_ACT.get(jt), t, False)
            for what in E_ACT.values():
                tail_e(what, NC - 1, False)
            store_tails(act, 1, 1)
            weights(1)
            experts(1)
            with act.Fori(0, NC // 2) as lap:
                for i in range(2):
                    c = lap * 2 + i
                    act.wait_ge(s_nmr, c + 2)
                    for q in range(CT):
                        row = xh[:, bass.ds(c * CT + q, 1), :].rearrange("p a d -> p (a d)")
                        last = act.activation(row, row, ACT.Identity, scale=rstd[:, i, q:q + 1], bias=nmr[:, i, q:q + 1])
                        if q < CT - 1:
                            last.then_inc(s_norm, 1)
                    last.then_inc(s_norm, 1)

        @block.tensor
        def _(pe):
            pe.wait_ge(s_const, 1)

            def aggregate(c, jt, first):
                if first and jt % CT == 0:
                    pe.wait_ge(s_xp, jt // CT + 1)
                    pe.wait_ge(s_x2s, jt // CT + 1)
                if jt == 0 and not first:
                    pe.wait_ge(s_h0, c)
                    pe.wait_ge(s_h1, c)
                pe.wait_ge(s_hi, c * NT + jt + 1)
                for X, start in ((XHI, jt == 0), (XLO, False)):
                    for v in range(2):
                        pe.matmul(ACC[v][:], X[:, jt, v * P:(v + 1) * P], HI[:, jt % 4], start=start, stop=False)
                pe.wait_ge(s_lo, c * NT + jt + 1)
                for v in range(2):
                    last = pe.matmul(ACC[v][:], XHI[:, jt, v * P:(v + 1) * P], LO[:, jt % 4], start=False, stop=jt == NT - 1)
                last.then_inc(s_used, 1)

            def mlp(c, layer):
                if layer == 0:
                    pe.wait_ge(s_h0, c + 1)
                    pe.wait_ge(s_h1, c + 1)
                else:
                    pe.wait_ge(s_r, c * 6 + 2 * layer)
                for v in range(2):
                    last = pe.matmul(PM[v][:], WTs[:, 3 * v + layer], hT[:, v], start=True, stop=True)
                last.then_inc(s_m, 1)

            def merge(c):
                pe.wait_ge(s_r, c * 6 + 6)
                for q in range(CT):
                    for v in range(2):
                        last = pe.matmul(PG[:, q * P:(q + 1) * P], hT[:, v, q * P:(q + 1) * P], WmTs[:, v],
                                         start=v == 0, stop=v == 1)
                last.then_inc(s_g, 1)

            def turn(L, c):
                pe.wait_ge(s_xn[L], c + 1)
                for q in range(CT):
                    last = pe.transpose(PT[:, q * P:(q + 1) * P], pay[L][:, 0, q, 0:P], ident[:])
                last.then_inc(s_tr[L], 1)

            def gate(L, c):
                pe.wait_ge(s_xT[L], c + 1)
                for q in range(CT):
                    last = pe.matmul(PGT[:, q * E:(q + 1) * E], xTb[L][:, q * P:(q + 1) * P], gws[:, L], start=True, stop=True)
                last.then_inc(s_gt[L], 1)

            def prefix(L, c):
                pe.wait_ge(s_oh[L], c + 1)
                pe.matmul(PPX[:, 0:CT * E], upper[:], oh[:, 2].rearrange("p q e -> p (q e)"), start=True, stop=False)
                for q in range(1, CT):
                    pe.matmul(PPX[:, q * E:CT * E], ones[:], oh[:, 2, 0:CT - q].rearrange("p q e -> p (q e)"), start=False, stop=False)
                for q in range(CT):
                    last = pe.matmul(PPX[:, q * E:(q + 1) * E], ones[:], run[:], start=False, stop=q == CT - 1)
                last.then_inc(s_pp[L], 1)

            def tail(L, what, c):
                if what in ("mlp0", "mlp1", "mlp2"):
                    mlp(c, int(what[3]))
                elif what == "merge":
                    merge(c)
                elif what == "turn":
                    turn(L, c)
                elif what == "gate":
                    gate(L, c)
                elif what == "prefix":
                    prefix(L, c)

            for jt in range(NT):
                aggregate(0, jt, True)
            pe.wait_ge(s_ls, 1)
            with pe.Fori(0, NC - 1) as t:
                for jt in range(NT):
                    aggregate(t + 1, jt, False)
                    tail(0, A_PE.get(jt), t)
            for what in A_PE.values():
                tail(0, what, NC - 1)

            def tile_table(L):
                pe.wait_ge(s_pos[L], NC)
                pe.matmul(PGT[:, 0:E], ones[:], run[:], start=True, stop=True).then_inc(s_cn[L], 1)
                pe.wait_ge(s_tl[L], 1)
                pe.matmul(PPX[0:1, 0:P], tcol[:, 0:1], ident[:], start=True, stop=True)
                pe.matmul(PPX[0:1, P:2 * P], tcol[:, 2:3], ident[:], start=True, stop=True).then_inc(s_tt[L], 1)

            def experts(L):
                W1, W2, width = ((W12s, W3s, 2 * H), (V1s, V2s, H))[L]
                r = [pe.alloc_register(f"expert{L}{u}") for u in range(RS)]

                def expert(u):
                    return pe.snap(r[u], min_val=0, max_val=E - 1)

                def x_in(k, lap, u):
                    pe.reg_load(r[u], tiles[0:1, 0, bass.ds(k, 1)])
                    pe.wait_ge(s_ld[u], lap * 16 + 16 + L * 16 * (ST // RS))
                    pe.transpose((B[2], B[5])[u % 2][:, 0:P], xin[:, u, 0:P], ident[:]).then_inc(s_etx, 1)

                def hidden(k, u):
                    e = expert(u)
                    pe.wait_ge(s_exT, k + 1 + L * ST)
                    pe.matmul(B[u % 2][:, 0:width], exT[:, u % 2], W1[:, bass.ds(e, 1), :].rearrange("p a n -> p (a n)"),
                              start=True, stop=True).then_inc(s_eh, 1)

                def result(k, u, first):
                    e = expert(u)
                    pe.wait_ge(s_ehT, k + 1 + L * ST)
                    if not first:
                        pe.wait_ge(s_ey, k - 1 + L * ST)
                    for h in range(2):
                        last = pe.matmul((B[4], B[6])[u % 2][:, 0:P], ehT[:, u % 2, h],
                                         W2[:, bass.ds(e, 1), h, :].rearrange("p a n -> p (a n)"), start=h == 0, stop=h == 1)
                    last.then_inc(s_eo, 1)

                def hidden_turn(k, u):
                    pe.wait_ge((s_ehid, s_eg)[L], k + 1 + L * ST)
                    for h in range(2):
                        src = (ehid, eg)[L][:, u % 2, h * P:(h + 1) * P]
                        last = pe.transpose((B[3], B[7])[u % 2][:, h * P:(h + 1) * P], src, ident[:])
                    last.then_inc(s_eth, 1)

                pe.wait_ge(s_tu[L], 1)
                pe.wait_ge((s_w, s_w1)[L], (32, 48)[L])
                for k in range(ST + 4):
                    if k == RS:
                        with pe.Fori(1, ST // RS) as lap:
                            for u in range(RS):
                                x_in(lap * RS + u, lap, u)
                                hidden(lap * RS + (u - 1), (u - 1) % RS)
                                result(lap * RS + (u - 4), (u - 4) % RS, False)
                                hidden_turn(lap * RS + (u - 2), (u - 2) % RS)
                    if RS <= k < ST:
                        continue
                    if k < ST:
                        x_in(k, 0, k % RS)
                    if 0 <= k - 1 < ST:
                        hidden(k - 1, (k - 1) % RS)
                    if 0 <= k - 4 < ST:
                        result(k - 4, (k - 4) % RS, k - 4 < 2)
                    if 0 <= k - 2 < ST:
                        hidden_turn(k - 2, (k - 2) % RS)

            tile_table(0)
            experts(0)

            for c in range(NC + 1):
                if c < NC:
                    pe.wait_ge(s_cx, c + 1)
                    for q in range(CT):
                        last = pe.transpose((PT, B[2])[c % 2][:, q * P:(q + 1) * P], xh[:, c * CT + q], ident[:])
                    last.then_inc(s_ct, 1)
                if c:
                    b = c - 1
                    xT = (xTb[0], xTc)[b % 2]
                    pe.wait_ge(s_cxT, b + 1)
                    if b >= 2:
                        pe.wait_ge(s_crow, b - 1)
                    pe.matmul((PG, B[3])[b % 2][0:1, :], a_s[:, 0:1], xT[:], start=True, stop=True).then_inc(s_cr, 1)
                    for q in range(CT):
                        t = b * CT + q
                        last = pe.matmul(PGT[:, 2 * t:2 * t + 2], xT[:, q * P:(q + 1) * P], a_s[:], start=True, stop=True)
                    last.then_inc(s_cf, 1)

            def column_sums(U):
                if U == 0:
                    pe.wait_ge(s_crow, NC)
                pe.wait_ge(s_csr, U + 1)
                pe.matmul(PG[:, 0:P], ones[:], csr[:], start=True, stop=True).then_inc(s_csp, 1)
                pe.wait_ge(s_cs, U + 1)

            def multiply(U, c, jt, first):
                operands = ((XB, XD), (XB2, XD2))[U]
                if U == 0 and first and jt % CT == 0:
                    pe.wait_ge(s_xb, jt // CT + 1)
                    pe.wait_ge(s_xd, jt // CT + 1)
                if U == 1 and first and jt % CT == 0:
                    pe.wait_ge(s_xb2, jt // CT + 1)
                for kind, (ring, made) in enumerate(((MP, s_mp[U]), (MM, s_mm[U]))):
                    pe.wait_ge(made, c * NT + jt + 1)
                    rhs = operands[kind][:, jt].rearrange("p h n -> p (h n)")
                    for q in range(CT):
                        if jt == 0 and not first:
                            if U == 0:
                                pe.wait_ge(s_ev[0], c * 8 + (kind * 4 + q - 7))
                            elif kind == 0:
                                pe.wait_ge(s_ev[1], c * 4 + (q - 3))
                        if U == 0:
                            dst = B[4 * kind + q][:, 0:260]
                        else:
                            dst = B[q][:, kind * 2 * P:(kind + 1) * 2 * P]
                        last = pe.matmul(dst, ring[:, jt % 4, q * P:(q + 1) * P], rhs,
                                         start=jt == 0 and (U == 0 or kind == 0), stop=jt == NT - 1,
                                         skip_group_check=U == 1)
                last.then_inc(s_mu[U], 1)

            for U in range(2):
                if U == 0:
                    column_sums(0)
                else:
                    pe.wait_ge(s_ev[0], 8 * NC)
                for jt in range(NT):
                    multiply(U, 0, jt, True)
                if U:
                    column_sums(1)
                with pe.Fori(0, NC - 1) as t:
                    for jt in range(NT):
                        multiply(U, t + 1, jt, False)
                        if U:
                            tail(1, E_PE.get(jt), t)
            for what in E_PE.values():
                tail(1, what, NC - 1)
            tile_table(1)
            experts(1)

        @block.vector
        def _(dve):
            need = dve.alloc_register("need_dve")
            D = Steps(dve, s_dve, need)

            def rest(c, jt, first):
                g, j = jt // CT, jt % CT
                dve.wait_ge(s_hi, c * NT + jt + 1)
                if not (first and jt < 4):
                    dve.wait_ge(s_used, c * NT + jt - 3)
                dve.tensor_tensor(LO[:, jt % 4], Abuf[:, g % 2, j], HI[:, jt % 4].bitcast(F32), ALU.subtract).then_inc(s_lo, 1)
                if j == CT - 1:
                    if not (first and g < 2):
                        dve.wait_ge(s_mst[g % 2], (c * (NG // 2) + g // 2) * 16)
                    dve.tensor_scalar(Mbuf[:, g % 2], Abuf[:, g % 2].rearrange("p t n -> p (t n)"), 0.0, 2.0,
                                      ALU.is_gt, ALU.mult).then_inc(s_mk, 1)

            def statistics(src, slot=0):
                for q in range(CT):
                    if q == 2:
                        yield
                    D(dve.bn_stats(stat[:, slot, q], src[:, q]))
                yield
                D.wait_alone()
                for q in range(CT):
                    last = dve.bn_aggr(mv[:, slot, q], stat[:, slot, q])
                    if q < CT - 1:
                        D(last)
                last.then_inc(s_var, 1)
                yield

            def normalize(dst, src, q, slot=0):
                return dve.tensor_scalar(dst, src, mv[:, slot, q, 0:1], rstd[:, slot, q:q + 1], ALU.subtract, ALU.mult)

            def chunk_of(c):
                return xs[:, bass.ds(c * CT, CT), :]

            def split(hi, lo, src):
                D(dve.tensor_copy(hi, src))
                D.wait()
                return dve.tensor_tensor(lo, src, hi.bitcast(F32), ALU.subtract)

            def operands_a(g):
                t = slice(g * CT, (g + 1) * CT)
                dve.wait_ge(s_root, g + 1)
                if g:
                    dve.wait_ge(s_xp, g)
                for q in range(CT):
                    last = normalize(stg[:, q], xs[:, g * CT + q], q)
                    if q < CT - 1:
                        D(last)
                last.then_inc(s_stg, 1)

            def rest_a(g):
                t = slice(g * CT, (g + 1) * CT)
                dve.wait_ge(s_xh, g + 1)
                dve.tensor_tensor(XLO[:, t, 0:P], stg[:], XHI[:, t, 0:P].bitcast(F32), ALU.subtract).then_inc(s_xp, 1)

            def mlp_in(c):
                dve.wait_ge(s_used, c * NT + NT)
                dve.tensor_scalar(hT[:, 1], ACC[1][:], eps1[:, 1:2], None, ALU.mult).then_inc(s_h1, 1)
                yield

            def add_gnn(c):
                dve.wait_ge(s_g, c + 1)
                D(dve.tensor_tensor(chunk_of(c), PG[:].rearrange("p (t n) -> p t n", t=CT), chunk_of(c), ALU.add))
                yield
                D.wait_alone()
                yield from statistics(chunk_of(c))

            def payload(L, c):
                dve.wait_ge(s_root, c + (NG + 2 * NC * L + 1))
                dve.wait_ge(s_pfree[L], c + 1)
                for k in range(2):
                    D(dve.tensor_copy(pay[L][:, k, :, P].bitcast(U32), tok[:, k, bass.ds(c * CT, CT)]))
                for q in range(CT):
                    last = normalize(pay[L][:, 0, q, 0:P], xs[:, bass.ds(c * CT + q, 1), :].rearrange("p a d -> p (a d)"), q)
                    if q < CT - 1:
                        D(last)
                last.then_inc(s_xn[L], 1)
                yield

            def top_two(L, c):
                dve.wait_ge(s_gt[L], c + 1)
                D(dve.tensor_tensor(lg[:], PGT[:, 0:CT * E].rearrange("p (q e) -> p q e", q=CT),
                                    gbs[:, L].unsqueeze(1).broadcast_to([P, CT, E]), ALU.add))
                yield
                D.wait_alone()
                for q in range(CT):
                    D(dve.max(top[:, q], lg[:, q]))
                yield
                D.wait_alone()
                for q in range(CT):
                    D(dve.max_index(topi[:, q], top[:, q], lg[:, q]))
                D(dve.tensor_tensor(dl[:, bass.ds(c * CT, CT)], top[:, :, 1], top[:, :, 0], ALU.subtract))
                yield
                D.wait()
                D(dve.tensor_copy(topf[:], topi[:]))
                yield
                D.wait()
                for k in range(2):
                    D(dve.tensor_tensor(oh[:, k], iota_e[:].unsqueeze(1).broadcast_to([P, CT, E]),
                                        topf[:, :, k:k + 1].broadcast_to([P, CT, E]), ALU.is_equal))
                yield
                D.wait()
                dve.tensor_tensor(oh[:, 2], oh[:, 0], oh[:, 1], ALU.add).then_inc(s_oh[L], 1)
                yield

            def positions(L, c):
                dve.wait_ge(s_pp[L], c + 1)
                free = PPX[:, 0:CT * E].rearrange("p (q e) -> p q e", q=CT)
                for k in range(2):
                    D(dve.tensor_tensor(posf[:, k], oh[:, k], free, ALU.mult))
                D(dve.tensor_reduce(cnt[:, 0], oh[:, 2].rearrange("p q e -> p e q"), AX.X, ALU.add))
                yield
                D.wait()
                D(dve.tensor_reduce(posr[:], posf[:], AX.X, ALU.add))
                D(dve.tensor_tensor(run[:], run[:], cnt[:, 0], ALU.add))
                yield
                D.wait()
                dve.tensor_copy(pos[:], posr[:]).then_inc(s_pos[L], 1)
                yield

            def first_rows():
                D(dve.memset(run[:], 0.0))
                D.wait()
                D(dve.tensor_copy(run[0:1, :], ecap[0:1, :]))
                D.wait()

            def now(steps):
                for _ in steps:
                    pass

            def part_a(what, c):
                return {"in": mlp_in, "add": add_gnn}[what](c) if what in ("in", "add") else routing(0, what, c)

            def routing(L, what, c):
                return {"norm": payload, "top": top_two, "pos": positions}[what](L, c)

            def between(places, part, c, tile, pace):
                steps = iter(())
                for jt in range(NT):
                    tile(jt)
                    if jt in places:
                        now(steps)
                        steps = part(places[jt], c)
                    for _ in range(pace(jt)):
                        next(steps, None)
                now(steps)

            def behind(places, part, c):
                for what in places.values():
                    now(part(what, c))

            dve.wait_ge(s_const, 1)
            first_rows()
            dve.wait_ge(s_x[0], 16)
            now(statistics(xs[:, 0:CT]))
            for jt in range(NT):
                g = jt // CT
                if jt % CT == 0:
                    operands_a(g)
                    rest_a(g)
                    if g == 0:
                        dve.wait_ge(s_x[1], 16)
                    if g < NG - 1:
                        D.wait()
                        dve.wait_ge(s_stg, g + 1)
                        now(statistics(xs[:, (g + 1) * CT:(g + 2) * CT]))
                rest(0, jt, True)
            dve.wait_ge(s_cst, 16 * 11)
            dve.tensor_scalar(eps1[:], eps1[:], 2.0, None, ALU.add).then_inc(s_ls, 1)
            dve.wait_ge(s_bm, NG)
            with D.loop(NC - 1, 31) as t:
                between(A_DVE, part_a, t, lambda jt: rest(t + 1, jt, False), lambda jt: 2)
            behind(A_DVE, part_a, NC - 1)

            def tile_table(L):
                end, need, upto, tmp = (cnt[:, i] for i in range(4))
                dve.wait_ge(s_cn[L], 1)
                D(dve.tensor_copy(end, PGT[:, 0:E]))
                D.wait()
                dve.tensor_copy(endu[:], end).then_inc(s_end[L], 1)
                D(dve.tensor_tensor(tmp, end, ecap[:], ALU.subtract))
                D.wait()
                D(dve.tensor_scalar(nuu[:], tmp, float(P - 1), None, ALU.add))
                D.wait()
                D(dve.tensor_scalar(nuu[:], nuu[:], 7, None, ALU.logical_shift_right))
                D.wait()
                D(dve.tensor_copy(need, nuu[:]))
                D.wait()
                D(dve.tensor_tensor_scan(upto, ones[:, 0:E], need, 0.0, ALU.mult, ALU.add))
                D.wait()
                D(dve.tensor_scalar(tmp, upto, kcol[:, 0:1], None, ALU.is_le))
                D.wait()
                D(dve.tensor_reduce(tcol[:, 0:1], tmp, AX.X, ALU.add))
                D(dve.tensor_tensor(need, need, tmp, ALU.mult))
                D.wait()
                D(dve.tensor_reduce(tcol[:, 1:2], need, AX.X, ALU.add))
                D.wait()
                D(dve.tensor_tensor(tcol[:, 2:3], kcol[:], tcol[:, 1:2], ALU.subtract))
                D(dve.tensor_scalar(tcol[:, 3:4], tcol[:, 0:1], float(CAP), None, ALU.mult))
                D.wait()
                D(dve.scalar_tensor_tensor(out=tcol[:, 2:3], in0=tcol[:, 2:3], scalar=float(P), in1=tcol[:, 3:4],
                                           op0=ALU.mult, op1=ALU.add))
                D.wait()
                D(dve.tensor_scalar(tcol[:, 2:3], tcol[:, 2:3], float(E * CAP), None, ALU.min))
                dve.tensor_scalar(tcol[:, 0:1], tcol[:, 0:1], float(E - 1), None, ALU.min).then_inc(s_tl[L], 1)
                dve.wait_ge(s_tt[L], 1)
                dve.tensor_copy(tiles[:], PPX[0:1, 0:2 * P].rearrange("p (a n) -> p a n", a=2)).then_inc(s_tu[L], 1)
                dve.wait_ge(s_tu[L], 1)
                if L == 0:
                    first_rows()
                dve.sem_inc(s_wd[L], 1)

            def weights(L):
                dve.wait_ge(s_we[L], 1)
                D(dve.tensor_scalar(wt[:, 0], wt[:, 1], 1.0, None, ALU.add))
                D.wait()
                D(dve.reciprocal(wt[:, 0], wt[:, 0]))
                D.wait()
                D(dve.tensor_tensor(wt[:, 1], wt[:, 1], wt[:, 0], ALU.mult))

            def experts(L):
                r = [dve.alloc_register(f"bias{u}") for u in range(RS)] if L else []

                def expert(u):
                    return dve.snap(r[u], min_val=0, max_val=E - 1)

                def gated(k, u):
                    if L:
                        dve.reg_load(r[u], tiles[0:1, 0, bass.ds(k, 1)])
                    if L == 0:
                        dve.wait_ge(s_eg, k + 1 + L * ST)
                        dve.tensor_tensor(ehid[:, u % 2], B[u % 2][:, H:2 * H], eg[:, u % 2], ALU.mult).then_inc(s_ehid, 1)

                def hidden_out(k, u):
                    src = (B[3], B[7])[u % 2][:, 0:H].rearrange("p (h n) -> p h n", h=2)
                    if L == 0:
                        dve.wait_ge(s_eth, k + 1 + L * ST)
                        dve.tensor_copy(ehT[:, u % 2], src).then_inc(s_ehT, 1)
                        return
                    e = expert(u)
                    dve.wait_ge(s_eth, k + 1 + L * ST)
                    for h in range(2):
                        last = dve.tensor_scalar(ehT[:, u % 2, h], src[:, h], b1c[:, bass.ds(e, 1), h], 0.0, ALU.add, ALU.max)
                        if h == 0:
                            D(last)
                    last.then_inc(s_ehT, 1)

                def result_out(k, u):
                    if L:
                        e = expert(u)
                    dve.wait_ge(s_eo, k + 1 + L * ST)
                    dve.wait_ge(s_efree[L], k + 1)
                    src = (B[4], B[6])[u % 2][:, 0:P]
                    if L == 0:
                        dve.tensor_copy(ey[:, u], src).then_inc(s_ey, 1)
                    else:
                        bias = C2s[:, bass.ds(e, 1), :].rearrange("p a n -> p (a n)")
                        dve.tensor_tensor(ey[:, u], src, bias, ALU.add).then_inc(s_ey, 1)

                if L:
                    dve.wait_ge(s_w1, 48)
                for k in range(ST + 4):
                    if k == RS:
                        with D.loop(ST // RS - 1, RS * L) as lap:
                            for u in range(RS):
                                gated(lap * RS + (u + RS - 1), (u - 1) % RS)
                                hidden_out(lap * RS + (u + RS - 2), (u - 2) % RS)
                                result_out(lap * RS + (u + RS - 4), (u - 4) % RS)
                    if RS <= k < ST:
                        continue
                    if 0 <= k - 1 < ST:
                        gated(k - 1, (k - 1) % RS)
                    if 0 <= k - 2 < ST:
                        hidden_out(k - 2, (k - 2) % RS)
                    if 0 <= k - 4 < ST:
                        result_out(k - 4, (k - 4) % RS)

            def combine(L, pair, lap, at4):
                dst = (xs, xh)[L]
                for i in range(2):
                    dve.wait_ge(s_yl[at4 + i], lap * 32 + (32 + L * 16 * NC // 2))
                for k in range(2):
                    for i, c in enumerate(pair):
                        for q in range(CT):
                            t = bass.ds(c * CT + q, 1)
                            row = dst[:, t, :].rearrange("p a d -> p (a d)")
                            D(dve.scalar_tensor_tensor(out=row, in0=yb[:, at4 + i, k, q], scalar=wt[:, k, t],
                                                       in1=row, op0=ALU.mult, op1=ALU.add))
                    D.wait_alone()
                dve.sem_inc(s_cb[L], 1)
                if L:
                    wait_alone(dve, need, s_nmr, lap * 4 + (at4 + 1))
                steps = [statistics(dst[:, bass.ds(c * CT, CT), :], i) for i, c in enumerate(pair)]
                for _ in range(4):
                    for s in steps:
                        next(s, None)

            tile_table(0)
            weights(0)
            experts(0)

            dve.wait_ge(s_p2[0], NC)
            with D.loop(NC // 4, 72) as lap:
                for at4 in (0, 2):
                    pair = [lap * 4 + (at4 + i) for i in range(2)]
                    combine(0, pair, lap, at4)
                    for i, c in enumerate(pair):
                        dve.wait_ge(s_root, c + (NG + NC + 1))
                        for q in range(CT):
                            t = bass.ds(c * CT + q, 1)
                            last = normalize(xh[:, t, :].rearrange("p a d -> p (a d)"), xs[:, t, :].rearrange("p a d -> p (a d)"), q, i)
                            if q < CT - 1:
                                D(last)
                        last.then_inc(s_cx, 1)
            dve.wait_ge(s_cx, NC)
            dve.wait_ge(s_cf, NC)
            D(dve.tensor_copy(f12[:], PGT[:, 0:2 * NT].rearrange("p (t n) -> p t n", t=NT)))
            D.wait()

            def column_sums(U):
                dve.tensor_reduce(csr[:], xh[:].rearrange("p t d -> p d t"), AX.X, ALU.add).then_inc(s_csr, 1)
                dve.wait_ge(s_csp, U + 1)
                dve.tensor_copy(cs[:], PG[:, 0:P]).then_inc(s_cs, 1)
                dve.wait_ge(s_cs, U + 1)

            D(dve.tensor_reduce(ext[:, 0:1], f12[:, :, 1], AX.X, ALU.max))
            D(dve.tensor_reduce(ext[:, 1:2], f12[:, :, 1], AX.X, ALU.min))
            D.wait()
            dve.tensor_scalar(ext[:, 1:2], ext[:, 1:2], -1.0, None, ALU.mult).then_inc(s_ext, 1)
            column_sums(0)
            dve.wait_ge(s_extr, 1)
            D(dve.tensor_tensor(mid[:], extr[:, 0:1], extr[:, 1:2], ALU.subtract))
            D.wait()
            D(dve.tensor_scalar(mid[:], mid[:], 0.5, None, ALU.mult))
            D.wait()
            D(dve.tensor_scalar(zc[:, 1], f12[:, :, 0], mid[:, 0:1], None, ALU.add))
            D(dve.tensor_scalar(zc[:, 0], f12[:, :, 1], mid[:, 0:1], None, ALU.subtract))
            D.wait()
            D(dve.scalar_tensor_tensor(out=al[:], in0=zc[:, 1], scalar=SLOPE, in1=zc[:, 1], op0=ALU.mult, op1=ALU.max))
            D.wait()
            D(dve.scalar_tensor_tensor(out=zc[:, 2], in0=zc[:, 1], scalar=SLOPE, in1=al[:], op0=ALU.mult, op1=ALU.subtract))
            dve.tensor_tensor(zc[:, 1], zc[:, 1], al[:], ALU.subtract).then_inc(s_zc, 1)
            dve.wait_ge(s_exps, 5)
            D(dve.tensor_tensor(fB[:, 1], fB[:, 0], fB[:, 0], ALU.mult))
            D(dve.tensor_tensor(fD[:, 1], fD[:, 0], fD[:, 0], ALU.mult))
            D(dve.tensor_scalar(ls[:], lsc[:], 1.0, None, ALU.add))
            D.wait()
            D(dve.reciprocal(ls[:], ls[:]))
            D.wait()
            D(dve.tensor_scalar(lsc[:], ls[:], -1.0, 1.0, ALU.mult, ALU.add))
            D.wait()
            dve.sem_inc(s_fac, 1)
            D(dve.tensor_scalar(k12[:, 0:1], lsc[:, 1:2], ls[:, 0:1], None, ALU.mult))
            D(dve.tensor_scalar(k12[:, 1:2], lsc[:, 1:2], lsc[:, 0:1], None, ALU.mult))
            D(dve.tensor_scalar(nc3[:], ls[:, 3:4], -1.0, None, ALU.mult))
            D.wait()

            def operands_d(g):
                t = slice(g * CT, (g + 1) * CT)
                if g:
                    dve.wait_ge(s_xb, g)
                D(dve.tensor_tensor(tmpb[:, :, 0:P], xh[:, t], fB[:, 0, t].unsqueeze(2).broadcast_to([P, CT, P]), ALU.mult))
                for k in range(2):
                    D(dve.tensor_copy(tmpb[:, :, P + k], fB[:, k, t]))
                D.wait()
                split(XB[:, t, 0], XB[:, t, 1], tmpb[:]).then_inc(s_xb, 1)

            def code_ahead(c, jt, slot, last):
                if jt + AHEAD < NT:
                    code(c, jt + AHEAD, slot)
                elif not last:
                    code(c + 1, jt + AHEAD - NT, 1 - slot)

            def code(c, jt, slot):
                g, j = jt // CT, jt % CT
                if j == 0:
                    dve.wait_ge(s_cl[g % 4], (c * (NG // 4) + g // 4) * 16 + 16)
                part = Cbuf[:, g % 4, j * CW:(j + 1) * CW]
                dve.scalar_tensor_tensor(out=part, in0=nf1[:, slot], scalar=f12[:, jt, 1:2], in1=part,
                                         op0=ALU.is_lt, op1=ALU.add).then_inc(s_code, 1)

            def other(U, c, jt, first):
                g, j = jt // CT, jt % CT
                if U == 0:
                    dve.wait_ge(s_code, c * NT + jt + 1)
                elif j == 0:
                    dve.wait_ge(s_cl[g % 4], (c * (NG // 4) + g // 4) * 16 + (16 + 4 * NC * NG))
                if not (first and jt < 4):
                    dve.wait_ge(s_mu[U], c * NT + jt - 3)
                dve.tensor_scalar(MM[:, jt % 4], Cbuf[:, g % 4, j * CW:(j + 1) * CW], 2.0, None, ALU.is_equal).then_inc(s_mm[U], 1)

            def products_out(U, c):
                dve.wait_ge(s_mu[U], c * NT + NT)
                if U == 0:
                    for kind in range(2):
                        for q in range(CT):
                            parts = B[4 * kind + q][:, 0:260].rearrange("p (h n) -> p n h", h=2)
                            dve.tensor_reduce(ev[:, q, kind], parts, AX.X, ALU.add).then_inc(s_ev[0], 1)
                else:
                    for q in range(CT):
                        parts = B[q][:].rearrange("p (s h n) -> p s n h", s=2, h=2)
                        dve.tensor_reduce(ev2[:, q], parts, AX.X, ALU.add).then_inc(s_ev[1], 1)
                yield
                dve.wait_ge(s_ev[U], c * (8, 4)[U] + (8, 4)[U])

            def scaled_rows(U, c):
                y = (ev, ev2)[U]
                for q in range(CT):
                    row = y[:, q, 0, 0:P]
                    D(dve.tensor_scalar(row, row, al[:, bass.ds(c * CT + q, 1)], None, ALU.mult))
                for other_part in (True, False):
                    for q in range(CT):
                        if q % 2 == 0:
                            yield
                            D.wait()
                        row = y[:, q, 0, 0:P]
                        part = y[:, q, 1, 0:P] if other_part else cs[:]
                        factor = (ga if other_part else ep)[:, bass.ds(c * CT + q, 1)]
                        D(dve.scalar_tensor_tensor(out=row, in0=part, scalar=factor, in1=row, op0=ALU.mult, op1=ALU.add))
                yield
                D.wait()

            def post_d(c):
                t = bass.ds(c * CT, CT)
                A4, C4, a4, g4, e4 = fA[:, t], fC[:, t], al[:, t], ga[:, t], ep[:, t]
                z = [q8[:, i] for i in range(8)]
                sp_, sm, qp, qm = (ev[:, :, k, P + n] for n in range(2) for k in range(2))
                D(dve.tensor_tensor(z[0], A4, sp_, ALU.mult))
                D(dve.tensor_tensor(z[1], C4, sm, ALU.mult))
                yield
                D.wait()
                D(dve.tensor_tensor(z[2], z[0], z[1], ALU.add))
                yield
                D.wait()
                D(dve.tensor_scalar(z[3], z[2], 0.0, None, ALU.is_equal))
                yield
                D.wait()
                D(dve.scalar_tensor_tensor(out=z[2], in0=z[3], scalar=float(N), in1=z[2], op0=ALU.mult, op1=ALU.add))
                yield
                D.wait()
                D(dve.reciprocal(z[4], z[2]))
                yield
                D.wait()
                D(dve.tensor_tensor(a4, A4, z[4], ALU.mult))
                D(dve.tensor_tensor(g4, C4, z[4], ALU.mult))
                D(dve.tensor_tensor(e4, z[3], z[4], ALU.mult))
                yield
                D.wait()
                D(dve.tensor_tensor(z[5], a4, a4, ALU.mult))
                D(dve.tensor_tensor(z[6], g4, g4, ALU.mult))
                yield
                D.wait()
                D(dve.tensor_tensor(z[5], z[5], qp, ALU.mult))
                D(dve.tensor_tensor(z[6], z[6], qm, ALU.mult))
                yield
                D.wait()
                D(dve.tensor_tensor(z[5], z[5], z[6], ALU.add))
                yield
                D.wait()
                D(dve.tensor_tensor(z[5], z[5], e4, ALU.add))
                yield
                D.wait()
                D(dve.tensor_scalar(rsu[:, t], z[5], 0.5, None, ALU.mult))
                yield
                D.wait()
                D(dve.tensor_scalar(z[7], rsu[:, t], -1.0, lsc[:, 2:3], ALU.mult, ALU.add))
                yield from scaled_rows(0, c)
                for q in range(CT):
                    row = ev[:, q, 0, 0:P]
                    xrow = xh[:, bass.ds(c * CT + q, 1), :].rearrange("p a d -> p (a d)")
                    D(dve.scalar_tensor_tensor(out=row, in0=xrow, scalar=z[7][:, q:q + 1], in1=row, op0=ALU.mult, op1=ALU.add))
                yield
                D.wait()
                rows, clip = ev[:, :, 0, 0:P], ev[:, :, 1, 0:P]
                D(dve.tensor_scalar(clip, rows, -THRESH, THRESH, ALU.max, ALU.min))
                yield
                D.wait()
                dve.tensor_tensor(xh[:, t, :], rows, clip, ALU.subtract).then_inc(s_post[0], 1)
                yield

            def post_e(c):
                t = bass.ds(c * CT, CT)
                yield from scaled_rows(1, c)
                pu, m = ev2[:, :, 0, :], ev2[:, :, 1, :]
                yield
                D(dve.scalar_tensor_tensor(out=odd[:], in0=pu, scalar=nc3[:, 0:1], in1=xh[:, t, :], op0=ALU.mult, op1=ALU.add))
                yield
                dve.wait_ge(s_h0x, c + 1)
                D.wait()
                D(dve.scalar_tensor_tensor(out=chunk_of(c), in0=odd[:], scalar=k12[:, 0:1], in1=chunk_of(c), op0=ALU.mult, op1=ALU.add))
                yield
                for q in range(CT):
                    D(dve.scalar_tensor_tensor(out=m[:, q], in0=odd[:, q], scalar=rsu[:, bass.ds(c * CT + q, 1)],
                                               in1=pu[:, q], op0=ALU.mult, op1=ALU.add))
                yield
                D.wait()
                dve.scalar_tensor_tensor(out=chunk_of(c), in0=m, scalar=ls[:, 1:2], in1=chunk_of(c), op0=ALU.mult,
                                         op1=ALU.add).then_inc(s_post[1], 1)
                yield
                wait_alone(dve, need, s_post[1], c + 1)
                yield from statistics(chunk_of(c))

            def part_d(what, c):
                return products_out(0, c) if what == "out" else post_d(c)

            def part_e(what, c):
                if what in ("out", "post"):
                    return products_out(1, c) if what == "out" else post_e(c)
                return routing(1, what, c)

            def chunk_d(c, slot, tail, next_nf1, first=False, last=False):
                def tile(jt):
                    if first and jt % CT == 0:
                        operands_d(jt // CT)
                    if jt == NT - AHEAD and not last:
                        dve.wait_ge(s_nfl[1 - slot], next_nf1)
                    code_ahead(c, jt, slot, last)
                    other(0, c, jt, first)

                if tail is None:
                    for jt in range(NT):
                        tile(jt)
                else:
                    between(D_DVE, part_d, tail, tile, lambda jt: 1)

            dve.wait_ge(s_nfl[0], 16)
            for jt in range(AHEAD):
                code(0, jt, 0)
            chunk_d(0, 0, None, 16, first=True)
            with D.loop((NC - 2) // 2, 68) as lap:
                chunk_d(lap * 2 + 1, 1, lap * 2, lap * 16 + 32)
                chunk_d(lap * 2 + 2, 0, lap * 2 + 1, lap * 16 + 32)
            chunk_d(NC - 1, 1, NC - 2, None, last=True)
            dve.wait_ge(s_mu[0], NC * NT)
            between(D_DVE, part_d, NC - 1, lambda jt: other(1, 0, jt, True), lambda jt: 1)
            dve.wait_ge(s_post[0], NC)
            column_sums(1)
            with D.loop(NC - 1, 48) as t:
                between(E_DVE, part_e, t, lambda jt: other(1, t + 1, jt, False),
                        lambda jt: 1 + (jt > 21))
            behind(E_DVE, part_e, NC - 1)
            tile_table(1)
            weights(1)
            experts(1)
            dve.wait_ge(s_cxh, NC)
            with D.loop(NC // 4, 60) as lap:
                for at4 in (0, 2):
                    pair = [lap * 4 + (at4 + i) for i in range(2)]
                    combine(1, pair, lap, at4)


def kernel(**inputs):
    import concourse.bacc as bacc
    from concourse.bass_utils import run_bass_kernel_spmd

    v = {k: np.asarray(w) for k, w in inputs.items()}

    def split_tiles(w):
        return w.reshape(E, 2, P, P).transpose(2, 0, 1, 3)

    adj = v["adj"].T.reshape(NG, CT, P, NC, CW).transpose(3, 0, 2, 1, 4).reshape(NC * NG, P, CT * CW)
    arrays = {
        "x": v["x"],
        "adjT": adj,
        "x2": v["L0_gnn_x2"],
        "eps": np.concatenate([v["L0_gnn_eps1"], v["L0_gnn_eps2"]]),
        "WT": np.concatenate([v["L0_gnn_W1"], v["L0_gnn_W2"]]).transpose(2, 0, 1),
        "bT": np.concatenate([v["L0_gnn_b1"], v["L0_gnn_b2"]]).T,
        "WmT": v["L0_gnn_Wm"].T.reshape(2, P, P).transpose(1, 0, 2),
        "bm": v["L0_gnn_bm"],
        "gate_w": np.stack([v["L0_ffn_gate_w"], v["L1_ffn_gate_w"]], axis=1),
        "gate_b": np.stack([v["L0_ffn_gate_b"], v["L1_ffn_gate_b"]]),
        "w12": np.concatenate([v["L0_ffn_w1"], v["L0_ffn_w2"]], axis=2).transpose(1, 0, 2),
        "w3": split_tiles(v["L0_ffn_w3"]),
        "h0": v["L1_gnn_h0"],
        "a": v["L1_gnn_a"].reshape(2, P).T,
        "temp": v["L1_gnn_temp"],
        "ew1": v["L1_ffn_w1"].transpose(1, 0, 2),
        "eb1": v["L1_ffn_b1"].reshape(E, 2, P).transpose(2, 0, 1),
        "ew2": split_tiles(v["L1_ffn_w2"]),
        "eb2": v["L1_ffn_b2"],
        "gamma": v["L1_ffn_gamma"],
        "beta": v["L1_ffn_beta"],
    }
    arrays = {f"in_{k}": np.ascontiguousarray(w) for k, w in arrays.items()}
    nc = bacc.Bacc("TRN2", target_bir_lowering=False, num_devices=1)
    args = [nc.dram_tensor(k, w.shape, mybir.dt.from_np(w.dtype), kind="ExternalInput").ap() for k, w in arrays.items()]
    out = nc.dram_tensor("out_dram", (N, P), F32, kind="ExternalOutput").ap()
    bass_gnn_moe_kernel(nc, *args, out)
    return run_bass_kernel_spmd(nc, [arrays], core_ids=[0]).results[0]["out_dram"]
```

```python
from contextlib import ExitStack, contextmanager

import numpy as np
import concourse.bass as bass
from concourse import mybir

ALU = mybir.AluOpType
ACT = mybir.ActivationFunctionType
AX = mybir.AxisListType
F32 = mybir.dt.float32
F32R = mybir.dt.float32r
U32 = mybir.dt.uint32
U8 = mybir.dt.uint8

P = 128
N = 4096
NT = N // P
CT = 4
CW = CT * P
NC = N // CW
NG = NT // CT
E = 16
H = 256
CAP = N + P
ROW = P + 1
ST = 80
RS = 16
AHEAD = 4
BY_ACT = (1, 4)
ONSET = 3
RF = 4
EPS = 1e-5
THRESH = 1e-6
SLOPE = 0.2


def wait_alone(eng, need, sem, value):
    if isinstance(value, int):
        eng.wait_ge(sem, value)
    else:
        eng.reg_mov(need, value)
        eng.wait_ge(sem, 1)
        eng.wait_ge(sem, need)


class Steps:

    def __init__(self, eng, sem, need):
        self.eng, self.sem, self.need, self.base, self.n = eng, sem, need, 0, 0

    def __call__(self, instruction):
        instruction.then_inc(self.sem, 1)
        self.n += 1

    def wait(self):
        self.eng.wait_ge(self.sem, self.base + self.n)

    def wait_alone(self):
        wait_alone(self.eng, self.need, self.sem, self.base + self.n)

    @contextmanager
    def loop(self, trips, each):
        start = self.base + self.n
        with self.eng.Fori(0, trips) as lap:
            self.base, self.n = lap * each + start, 0
            yield lap
            assert self.n == each, f"a lap counts {self.n}"
        self.base, self.n = start + trips * each, 0


def bass_gnn_moe_kernel(nc, x, adjT, x2, eps, WT, bT, WmT, bm, gate_w, gate_b, w12, w3, h0, a, temp,
                        ew1, eb1, ew2, eb2, gamma, beta, out):
    mask_d = nc.dram_tensor("mask_d", [NC * NG, P, CT * CW], U8).ap()
    code_d = nc.dram_tensor("code_d", [NC * NG, P, CT * CW], U8).ap()
    sorted_d = [nc.dram_tensor(f"sorted_d{L}", [E * CAP + P, ROW], F32).ap() for L in range(2)]
    expert_d = [nc.dram_tensor(f"expert_d{L}", [2 * N, P], F32).ap() for L in range(2)]
    nf1_d = nc.dram_tensor("nf1_d", [NC, CW], F32).ap()

    x_v = x.rearrange("(t p) d -> p t d", p=P)
    x2_v = x2.rearrange("(t p) d -> p t d", p=P)
    h0_v = h0.rearrange("(t p) d -> p t d", p=P)
    out_v = out.rearrange("(t p) d -> p t d", p=P)

    with ExitStack() as ctx:
        def sb(name, shape, dt=F32):
            return ctx.enter_context(nc.sbuf_tensor(name, shape, dt))

        def sem(name):
            return ctx.enter_context(nc.semaphore(name))

        xs = sb("xs", [P, NT, P])
        xh = sb("xh", [P, NT, P])
        ident = sb("ident", [P, P])
        ones = sb("ones", [P, P])
        upper = sb("upper", [P, P])
        bTs = sb("bTs", [P, 6])
        gws = sb("gws", [P, 2, E])
        gbs = sb("gbs", [P, 2, E])
        a_s = sb("a_s", [P, 2])
        gam = sb("gam", [P, P])
        bet = sb("bet", [P, P])
        eps1 = sb("eps1", [P, 2])
        ls = sb("ls", [P, 5])
        lsc = sb("lsc", [P, 5])
        k12 = sb("k12", [P, 2])
        nc3 = sb("nc3", [P, 1])
        iota_e = sb("iota_e", [P, E])
        ecap = sb("ecap", [P, E])
        kcol = sb("kcol", [P, 1])
        tok = sb("tok", [P, 2, NT], U32)
        fill = sb("fill", [P, ROW])
        away = sb("away", [P, CW], U8)
        minus2 = sb("minus2", [P, 1])
        run = sb("run", [P, E])
        cnt = sb("cnt", [P, 4, E])
        tcol = sb("tcol", [P, 4])
        endu = sb("endu", [P, E], U32)
        nuu = sb("nuu", [P, E], U32)
        tiles = sb("tiles", [1, 2, P], U32)
        stat = sb("stat", [P, 2, CT, 6])
        mv = sb("mv", [P, 2, CT, 2])
        zero4 = sb("zero4", [P, CT])
        nmr = sb("nmr", [P, 2, CT])
        varE = sb("varE", [P, 2, CT])
        epsc = sb("epsc", [P, 2, CT])
        rstd = sb("rstd", [P, 2, CT])
        lg = sb("lg", [P, CT, E])
        top = sb("top", [P, CT, 8])
        topi = sb("topi", [P, CT, 8], U32)
        topf = sb("topf", [P, CT, 8])
        oh = sb("oh", [P, 3, CT, E])
        posf = sb("posf", [P, 2, CT, E])
        posr = sb("posr", [P, 2, CT])
        pos = sb("pos", [P, 2, CT], U32)
        dl = sb("dl", [P, NT])
        wt = sb("wt", [P, 2, NT])
        f12 = sb("f12", [P, NT, 2])
        ext = sb("ext", [P, 2])
        bounds = sb("bounds", [2, 1])
        half = sb("half", [2, P])
        mid = sb("mid", [P, 1])
        zc = sb("zc", [P, 3, NT])
        fB = sb("fB", [P, 2, NT])
        fD = sb("fD", [P, 2, NT])
        fA = sb("fA", [P, NT])
        fC = sb("fC", [P, NT])
        al = sb("al", [P, NT])
        ga = sb("ga", [P, NT])
        ep = sb("ep", [P, NT])
        rsu = sb("rsu", [P, NT])
        q8 = sb("q8", [P, 8, CT])
        csr = sb("csr", [P, P])
        cs = sb("cs", [P, P])
        b1c = sb("b1c", [P, E, 2])

        R1_SIZE, R2_SIZE = NT * 4 * 130 * 4, 100544
        base1 = (nc.sbuf_base + 31) // 32 * 32
        assert base1 + R1_SIZE + R2_SIZE <= nc.sbuf_usable_end, (base1 + R1_SIZE + R2_SIZE, nc.sbuf_usable_end)
        base2 = base1 + R1_SIZE

        def at(region, offset, name, shape, dt=F32):
            size = int(np.prod(shape[1:])) * (1 if dt == U8 else 4)
            start, limit = (base1, R1_SIZE) if region == 1 else (base2, R2_SIZE)
            assert offset + size <= limit, (name, offset + size, limit)
            return nc.alloc_sbuf_tensor_at(name, shape, dt, offset=start + offset)

        XHI = at(1, 0, "XHI", [P, NT, 2 * P], F32R)
        XLO = at(1, 32768, "XLO", [P, NT, 2 * P], F32R)
        W12s = at(2, 0, "W12s", [P, E, 2 * H])
        W3s = at(2, 32768, "W3s", [P, E, 2, P])
        Abuf = at(2, 49152, "Abuf", [P, 2, CT, CW])
        HI = at(2, 65536, "HI", [P, 4, CW], F32R)
        LO = at(2, 73728, "LO", [P, 4, CW], F32R)
        Mbuf = at(2, 81920, "Mbuf", [P, 2, CT * CW], U8)
        hT = at(2, 86016, "hT", [P, 2, CW])
        stg = at(2, 86016, "stg", [P, CT, P])
        WTs = at(2, 96320, "WTs", [P, 6, P])
        WmTs = at(2, 99392, "WmTs", [P, 2, P])
        XB = at(1, 0, "XB", [P, NT, 2, 130], F32R)
        XD = at(1, 33280, "XD", [P, NT, 2, 130], F32R)
        XB2 = at(2, 0, "XB2", [P, NT, 2, P], F32R)
        XD2 = at(2, 32768, "XD2", [P, NT, 2, P], F32R)
        MP = at(2, 65536, "MP", [P, 4, CW], F32R)
        MM = at(2, 73728, "MM", [P, 4, CW], F32R)
        Cbuf = at(2, 81920, "Cbuf", [P, 4, CT * CW], U8)
        nfrow = at(2, 0, "nfrow", [1, N])
        nf1 = at(2, 90112, "nf1", [P, 2, CW])
        ev = at(2, 94208, "ev", [P, CT, 2, 130])
        ev2 = at(2, 94208, "ev2", [P, CT, 2, P])
        tmpx = at(2, 94208, "tmpx", [P, CT, 130])
        tmpb = at(2, 98400, "tmpb", [P, CT, 130])
        V1s = at(1, 0, "V1s", [P, E, H])
        V2s = at(1, 16384, "V2s", [P, E, 2, P])
        C2s = at(1, 32768, "C2s", [P, E, P])
        h0b = at(1, 58368, "h0b", [P, CT, P])
        odd = at(1, 60416, "odd", [P, CT, P])
        h0s = at(1, 62464, "h0s", [P, CT, P])
        pay = [at(r, o, f"pay{L}", [P, 2, CT, ROW]) for L, (r, o) in enumerate(((2, 90112), (1, 40960)))]
        xTb = [at(r, o + 4160, f"xT{L}", [P, CW]) for L, (r, o) in enumerate(((2, 90112), (1, 40960)))]
        xTc = at(2, 96320, "xTc", [P, CW])
        xin = at(2, 49152, "xin", [P, RS, ROW])
        ey = at(2, 57408, "ey", [P, RS, P])
        exT = at(2, 65600, "exT", [P, 2, P])
        eg = at(2, 66624, "eg", [P, 2, H])
        ehid = at(2, 68672, "ehid", [P, 2, H])
        ehT = at(2, 70720, "ehT", [P, 2, 2, P])
        W12h = at(1, 0, "W12h", [P, E, 2 * H], F32R)
        W12l = at(2, 0, "W12l", [P, E, 2 * H], F32R)
        exTh = at(2, 65600, "exTh", [P, 2, P], F32R)
        exTl = at(1, 49152, "exTl", [P, 2, P], F32R)
        yb = at(2, 73728, "yb", [P, 4, 2, CT, P])
        B = [ctx.enter_context(nc.psum_tensor(f"B{i}", [P, 512], F32)) for i in range(8)]

        s_x, s_x2 = [sem(f"s_x{i}") for i in range(2)], [sem(f"s_x2{i}") for i in range(2)]
        s_xh, s_cst, s_w, s_w1 = sem("s_xh"), sem("s_cst"), sem("s_w"), sem("s_w1")
        s_pool = sem("s_pool")
        s_const = sem("s_const")
        s_dve = sem("s_dve")
        s_fillin = sem("s_fillin")
        s_bmr = sem("s_bmr")
        s_ad = [sem(f"s_ad{i}") for i in range(2)]
        s_mst = [sem(f"s_mst{i}") for i in range(2)]
        s_acc = sem("s_acc")
        s_hi, s_lo, s_used, s_mk, s_xp = sem("s_hi"), sem("s_lo"), sem("s_used"), sem("s_mk"), sem("s_xp")
        s_h0, s_h1, s_m, s_r, s_g = sem("s_h0"), sem("s_h1"), sem("s_m"), sem("s_r"), sem("s_g")
        s_var, s_root = sem("s_var"), sem("s_root")
        s_xn = sem("s_xn")
        s_p2 = sem("s_p2")
        s_tr = sem("s_tr")
        s_xT = sem("s_xT")
        s_gt = sem("s_gt")
        s_oh = sem("s_oh")
        s_pp = sem("s_pp")
        s_pos = sem("s_pos")
        s_sc = [sem(f"s_sc{L}") for L in range(2)]
        s_pfree = [sem(f"s_pfree{L}") for L in range(2)]
        s_cn = sem("s_cn")
        s_end = sem("s_end")
        s_tl = sem("s_tl")
        s_tt = sem("s_tt")
        s_tu = [sem(f"s_tu{L}") for L in range(2)]
        s_tail = [[sem(f"s_tail{L}{i}") for i in range(2)] for L in range(2)]
        s_ld = [sem(f"s_ld{i}") for i in range(RS)]
        s_etx = sem("s_etx")
        s_exT = sem("s_exT")
        s_eh = sem("s_eh")
        s_eg = sem("s_eg")
        s_ehid = sem("s_ehid")
        s_eth = sem("s_eth")
        s_ehT = sem("s_ehT")
        s_eo = sem("s_eo")
        s_ey = sem("s_ey")
        s_est = [sem(f"s_est{i}") for i in range(RF)]
        s_efree = [sem(f"s_efree{L}") for L in range(2)]
        s_eall = [sem(f"s_eall{L}") for L in range(2)]
        s_yl = [sem(f"s_yl{i}") for i in range(4)]
        s_wd = [sem(f"s_wd{L}") for L in range(2)]
        s_we = sem("s_we")
        s_cb = [sem(f"s_cb{L}") for L in range(2)]
        s_cx, s_ct, s_cxT, s_cf, s_cr, s_crow = (sem(n) for n in ("s_cx", "s_ct", "s_cxT", "s_cf", "s_cr", "s_crow"))
        s_nfst = sem("s_nfst")
        s_cxh, s_cs = sem("s_cxh"), sem("s_cs")
        s_ext, s_extT, s_extr, s_zc, s_exps, s_ls = (sem(n) for n in ("s_ext", "s_extT", "s_extr", "s_zc", "s_exps", "s_ls"))
        s_xb, s_xd, s_xb2, s_fac = (sem(n) for n in ("s_xb", "s_xd", "s_xb2", "s_fac"))
        s_x2h, s_x2s, s_bm, s_stg = (sem(n) for n in ("s_x2h", "s_x2s", "s_bm", "s_stg"))
        s_h0s, s_h0x = sem("s_h0s"), sem("s_h0x")
        s_nmr, s_norm, s_gm = sem("s_nmr"), sem("s_norm"), sem("s_gm")
        s_wsp, s_exl, s_coef, s_evf = (sem(n) for n in ("s_wsp", "s_exl", "s_coef", "s_evf"))
        s_csr, s_csp = sem("s_csr"), sem("s_csp")
        s_cl = [sem(f"s_cl{i}") for i in range(4)]
        s_cst2 = [sem(f"s_cst2{i}") for i in range(4)]
        s_nfl = [sem(f"s_nfl{i}") for i in range(2)]
        s_code = sem("s_code")
        s_mp = [sem(f"s_mp{U}") for U in range(2)]
        s_mm = [sem(f"s_mm{U}") for U in range(2)]
        s_ma, s_abs = sem("s_ma"), sem("s_abs")
        s_mu = [sem(f"s_mu{U}") for U in range(2)]
        s_ev = [sem(f"s_ev{U}") for U in range(2)]
        s_post = [sem(f"s_post{U}") for U in range(2)]
        s_h0l = sem("s_h0l")
        s_fin, s_out = sem("s_fin"), [sem("s_out0"), sem("s_out1")]

        ACC, PM, PG, PT, PGT, PPX = B[0:2], B[2:4], B[4], B[5], B[6], B[7]

        block = ctx.enter_context(nc.Block())

        def store_tails(eng, L, half):
            eng.wait_ge(s_end, L + 1)
            ends = [eng.alloc_register(f"end{L}{half}{i}") for i in range(E // 2)]
            for i, r in enumerate(ends):
                e = half * (E // 2) + i
                eng.reg_load(r, endu[0:1, e:e + 1])
            for r in ends:
                row = eng.snap(r, min_val=0, max_val=E * CAP - P)
                eng.dma_start(sorted_d[L][bass.ds(row, P), :], fill[:]).then_inc(s_tail[L][half], 16)
            for r in ends:
                eng.free_register(r)

        @block.sync
        def _(sp):
            need = sp.alloc_register("need_sp")
            for dst, src, done in ((xs, x_v, s_x), (xh, x2_v, s_x2)):
                sp.dma_start(dst[:, 0:CT], src[:, 0:CT, :]).then_inc(done[0], 16)

            def load_adjacency(c, g):
                G = c * NG + g
                if not (isinstance(G, int) and G < 2):
                    wait_alone(sp, need, s_hi, CT * (G - 1))
                    wait_alone(sp, need, s_mk, G - 1)
                sp.dma_start(Abuf[:, g % 2], adjT[bass.ds(G, 1)].rearrange("a p n -> p (a n)")
                             .rearrange("p (t n) -> p t n", t=CT)).then_inc(s_ad[g % 2], 16)

            def store_mask(G, slot):
                wait_alone(sp, need, s_mk, G + 1)
                sp.dma_start(mask_d[bass.ds(G, 1)].rearrange("a p n -> p (a n)"), Mbuf[:, slot]).then_inc(s_mst[slot], 16)

            def load_weights(c):
                e = bass.ds(c * (E // NC), E // NC)
                sp.dma_start(W12s[:, e], w12[:, e, :]).then_inc(s_w, 16)
                sp.dma_start(W3s[:, e], w3[:, e, :, :]).then_inc(s_w, 16)

            for g in range(NG):
                load_adjacency(0, g)
                if g == 0:
                    for dst, src, done in ((xs, x_v, s_x), (xh, x2_v, s_x2)):
                        sp.dma_start(dst[:, CT:], src[:, CT:, :]).then_inc(done[1], 16)
                if g == 1:
                    for dst, src in ((WTs[:], WT), (WmTs[:], WmT), (bTs[:], bT), (gws[:], gate_w), (a_s[:], a),
                                     (gbs[:], gate_b.partition_broadcast(P)),
                                     (gam[:], gamma.partition_broadcast(P)), (bet[:], beta.partition_broadcast(P)),
                                     (eps1[:], eps.partition_broadcast(P)), (ls[:], temp.partition_broadcast(P)),
                                     (b1c[:], eb1)):
                        sp.dma_start(dst, src).then_inc(s_cst, 16)
                    sp.dma_start(csr[:], bm.partition_broadcast(P)).then_inc(s_bmr, 16)
                if g == 3:
                    load_weights(0)
                    wait_alone(sp, need, s_const, 1)
                    for L in range(2):
                        sp.dma_start(sorted_d[L][E * CAP:E * CAP + P, :], fill[:]).then_inc(s_fillin, 16)
                if g:
                    store_mask(g - 1, (g - 1) % 2)
            with sp.Fori(1, NC) as c:
                for g in range(NG):
                    load_adjacency(c, g)
                    store_mask(c * NG + g - 1, (g - 1) % 2)
                    if g == 3:
                        load_weights(c)
            store_mask(NC * NG - 1, 1)

            def moe_loads(L):
                store_tails(sp, L, 0)
                r = sp.alloc_register(f"row{L}")
                wait_alone(sp, need, s_tu[L], 1)
                for half in range(2):
                    sp.wait_ge(s_tail[L][half], 16 * E // 2)
                wait_alone(sp, need, s_sc[L], 16 * 2 * NT)
                wait_alone(sp, need, s_fillin, 32)
                with sp.Fori(0, ST // RS) as lap:
                    for u in range(RS):
                        k = lap * RS + u
                        sp.reg_load(r, tiles[0:1, 1, bass.ds(k, 1)])
                        row = sp.snap(r, min_val=0, max_val=E * CAP)
                        wait_alone(sp, need, s_efree[L], k + 1)
                        sp.dma_start(xin[:, u], sorted_d[L][bass.ds(row, P), :]).then_inc(s_ld[u], 16)
                wait_alone(sp, need, s_eall[L], 1)
                y_v = expert_d[L].rearrange("(k t p) d -> k p t d", k=2, p=P)
                for c in range(NC):
                    if c >= 4:
                        sp.wait_ge(s_cb[L], c // 2 - 1)
                    for k in range(2):
                        sp.dma_start(yb[:, c % 4, k], y_v[k, :, c * CT:(c + 1) * CT, :]).then_inc(s_yl[c % 4], 16)
                if L:
                    for c in range(NC):
                        store_out(c)

            def store_out(c):
                wait_alone(sp, need, s_fin, c + 1)
                sp.dma_start(out_v[:, c * CT:(c + 1) * CT, :], xs[:, c * CT:(c + 1) * CT, :]).then_inc(s_out[c % 2], 16)

            moe_loads(0)

            sp.wait_ge(s_crow, NC)
            sp.dma_start(nf1_d.rearrange("c n -> (c n)").unsqueeze(0), nfrow[:]).then_inc(s_nfst, 16)
            sp.wait_ge(s_nfst, 16)

            def load_codes(U, G, slot):
                src = (mask_d, code_d)[U]
                sp.dma_start(Cbuf[:, slot], src[bass.ds(G, 1)].rearrange("a p n -> p (a n)")).then_inc(s_cl[slot], 16)

            def load_nf1(c, slot):
                sp.dma_start(nf1[:, slot], nf1_d[bass.ds(c, 1), :].rearrange("a n -> (a n)").partition_broadcast(P)).then_inc(s_nfl[slot], 16)

            def codes_done(U, G, G_half=None):
                wait_alone(sp, need, s_mp[U], CT * (G + 1))
                if U:
                    wait_alone(sp, need, s_mm[1], CT * (G + 1))
                else:
                    half, odd_group = (G // 2, G % 2) if isinstance(G, int) else G_half
                    mine = [j for j in BY_ACT if j < CT * (odd_group + 1)]
                    wait_alone(sp, need, s_ma, half * len(BY_ACT) + len(mine))
                    wait_alone(sp, need, s_mm[0], half * (8 - len(BY_ACT)) + CT * (odd_group + 1) - len(mine))

            for i in range(2):
                wait_alone(sp, need, s_mst[i], 16 * NC * NG // 2)
            sp.wait_ge(s_cb[0], NC // 2)
            for i in range(4):
                load_codes(0, i, i)
            load_nf1(0, 0)

            def group_d(c, g, first=False, last=False):
                G = c * NG + g
                wait_alone(sp, need, s_code, CT * (G + 1))
                sp.dma_start(code_d[bass.ds(G, 1)].rearrange("a p n -> p (a n)"), Cbuf[:, g % 4]).then_inc(s_cst2[g % 4], 16)
                if not (first and g == 0 or last and g >= NG - 3):
                    codes_done(0, G - 1, (c * (NG // 2) + (g - 1) // 2, (g - 1) % 2))
                    stores = c * (NG // 4) + ((g - 1) // 4 + 1)
                    wait_alone(sp, need, s_cst2[(g - 1) % 4], stores * 16)
                    load_codes(0, G + 3, (g + 3) % 4)

            load_nf1(1, 1)
            for g in range(NG):
                group_d(0, g, first=True)
            with sp.Fori(0, (NC - 2) // 2) as lap:
                for d in range(2):
                    c = lap * 2 + (d + 1)
                    load_nf1(c + 1, d)
                    for g in range(NG):
                        group_d(c, g)
            for g in range(NG):
                group_d(NC - 1, g, last=True)
            for i in range(4):
                codes_done(0, NC * NG - 4 + i)
                sp.wait_ge(s_cst2[i], 16 * NC * NG // 4)
                load_codes(1, i, i)
            wait_alone(sp, need, s_mu[0], NC * NT)
            for dst, src in ((V1s[:], ew1), (V2s[:], ew2), (C2s[:], eb2.partition_broadcast(P))):
                sp.dma_start(dst, src).then_inc(s_w1, 16)

            def group_e(c, g, last):
                codes_done(1, c * NG + g)
                if not (last and g >= NG - 4):
                    load_codes(1, c * NG + g + 4, g % 4)

            def chunk_e(c, first, last):
                for g in range(NG):
                    group_e(c, g, last)
                    if g == NG - 2:
                        if not first:
                            wait_alone(sp, need, s_post[1], c)
                        sp.dma_start(h0b[:], h0_v[:, bass.ds(c * CT, CT), :]).then_inc(s_h0l, 16)

            chunk_e(0, True, False)
            with sp.Fori(1, NC - 1) as c:
                chunk_e(c, False, False)
            chunk_e(NC - 1, False, True)
            moe_loads(1)
            for i in range(2):
                wait_alone(sp, need, s_out[i], 16 * NC // 2)

        @block.gpsimd
        def _(pool):
            need = pool.alloc_register("need_pool")
            S = Steps(pool, s_pool, need)
            S(pool.memset(ident[:], 0.0))
            S(pool.memset(ones[:], 1.0))
            S(pool.memset(fill[:, 0:P], 0.0))
            S(pool.memset(minus2[:], -2.0))
            S(pool.memset(half[:], 0.5))
            S(pool.memset(zero4[:], 0.0))
            S(pool.memset(epsc[:, 0, :], EPS))
            S(pool.memset(epsc[:, 1, :], -0.5))
            S(pool.iota(fill[:, P:P + 1].bitcast(U32), pattern=[[1, 1]], base=2 * N, channel_multiplier=1))
            S(pool.iota(tok[:], pattern=[[N, 2], [P, NT]], base=0, channel_multiplier=1))
            S(pool.iota(iota_e[:], pattern=[[1, E]], base=0, channel_multiplier=0, allow_small_or_imprecise_dtypes=True))
            S(pool.iota(ecap[:], pattern=[[CAP, E]], base=0, channel_multiplier=0, allow_small_or_imprecise_dtypes=True))
            S(pool.iota(kcol[:], pattern=[[1, 1]], base=0, channel_multiplier=1, allow_small_or_imprecise_dtypes=True))
            S.wait()
            S(pool.affine_select(out=ident[:], in_=ident[:], compare_op=ALU.not_equal, fill=1.0, base=0,
                                 pattern=[[-1, P]], channel_multiplier=1))
            S(pool.affine_select(out=half[:], in_=half[:], compare_op=ALU.is_equal, fill=-0.5, base=0,
                                 pattern=[[0, P]], channel_multiplier=1))
            S(pool.affine_select(out=upper[:], in_=ones[:], compare_op=ALU.is_gt, fill=0.0, base=0,
                                 pattern=[[1, P]], channel_multiplier=-1))
            S.wait()
            pool.sem_inc(s_const, 1)

            def scatter_chunk(L, c):
                wait_alone(pool, need, s_p2, c + (1 + L * NC))
                pool.wait_ge(s_pos, c + (1 + L * NC))
                for q in range(CT):
                    for k in range(2):
                        pool.indirect_dma_start(
                            out=sorted_d[L], out_offset=bass.IndirectOffsetOnAxis(ap=pos[:, k, q:q + 1], axis=0),
                            in_=pay[L][:, k, q, :], in_offset=None,
                            bounds_check=E * CAP - 1, oob_is_err=False).then_inc(s_sc[L], 16)
                if L:
                    rows = xs[:, bass.ds(c * CT, CT), :]
                    S(pool.tensor_tensor(rows, rows, bet[:].unsqueeze(1).broadcast_to([P, CT, P]), ALU.add))
                pool.wait_ge(s_sc[L], c * (16 * 2 * CT) + 16 * 2 * CT)
                pool.sem_inc(s_pfree[L], 1)

            def scatter_results(L):
                def scattered(lap, u):
                    done = lap * (RS // RF) + (u // RF + 1) + L * (ST // RF)
                    pool.wait_ge(s_est[u % RF], done * 16)
                    pool.sem_inc(s_efree[L], 1)

                pool.sem_inc(s_efree[L], RS)
                with pool.Fori(0, ST // RS) as lap:
                    for u in range(RS):
                        wait_alone(pool, need, s_ey, lap * RS + u + 1 + L * ST)
                        pool.indirect_dma_start(
                            out=expert_d[L], out_offset=bass.IndirectOffsetOnAxis(ap=xin[:, u, P:P + 1].bitcast(U32), axis=0),
                            in_=ey[:, u], in_offset=None,
                            bounds_check=2 * N - 1, oob_is_err=False).then_inc(s_est[u % RF], 16)
                        if u >= 2:
                            scattered(lap, u - 2)
                    for u in (RS - 2, RS - 1):
                        scattered(lap, u)
                pool.sem_inc(s_eall[L], 1)

            def root(n, slot=0):
                wait_alone(pool, need, s_var, n + 1)
                S(pool.tensor_tensor(varE[:, slot], mv[:, slot, :, 1], epsc[:, 0, :], ALU.add))
                S.wait()
                pool.tensor_tensor(rstd[:, slot], varE[:, slot], epsc[:, 1, :], ALU.pow).then_inc(s_root, 1)

            def norm_factors(L, c, i):
                n = c + (NG + NC + 2 * NC * L)
                root(n, i)
                wait_alone(pool, need, s_root, n + 1)
                S(pool.tensor_tensor(varE[:, i], mv[:, i, :, 0], rstd[:, i], ALU.mult))
                S.wait_alone()
                pool.tensor_tensor(nmr[:, i], zero4[:], varE[:, i], ALU.subtract).then_inc(s_nmr, 1)

            def add_h0(c):
                wait_alone(pool, need, s_h0s, c + 1)
                rows = xs[:, bass.ds(c * CT, CT), :]
                pool.tensor_tensor(rows, rows, h0s[:], ALU.add).then_inc(s_h0x, 1)

            def operands_of(g, X, src, factor, tmp):
                S(pool.tensor_tensor(tmp[:, :, 0:P], src, factor[:, 0, g].unsqueeze(2).broadcast_to([P, CT, P]), ALU.mult))
                width = tmp.shape[2]
                if width > P:
                    for k in range(2):
                        S(pool.tensor_copy(tmp[:, :, P + k], factor[:, k, g]))
                S.wait_alone()
                S(pool.tensor_copy(X[:, g, 0, :], tmp))
                S.wait_alone()
                return pool.tensor_tensor(X[:, g, 1, :], tmp, X[:, g, 0, :].bitcast(F32), ALU.subtract)

            def features(c):
                wait_alone(pool, need, s_coef, c + 1)
                t = bass.ds(c * CT, CT)
                rows, others, tmp, x_rows = ev[:, :, 0, 0:P], ev[:, :, 1, 0:P], tmpb[:, :, 0:P], xh[:, t, :]

                def spread(f):
                    return f.unsqueeze(2).broadcast_to([P, CT, P])

                S(pool.tensor_tensor(rows, rows, spread(al[:, t]), ALU.mult))
                S(pool.tensor_tensor(others, others, spread(ga[:, t]), ALU.mult))
                S(pool.tensor_tensor(tmp, cs[:].unsqueeze(1).broadcast_to([P, CT, P]), spread(ep[:, t]), ALU.mult))
                S.wait_alone()
                S(pool.tensor_tensor(rows, rows, others, ALU.add))
                S.wait_alone()
                S(pool.tensor_tensor(rows, rows, tmp, ALU.add))
                S(pool.tensor_tensor(others, x_rows, spread(q8[:, 7]), ALU.mult))
                S.wait_alone()
                S(pool.tensor_tensor(rows, rows, others, ALU.add))
                S.wait_alone()
                S(pool.tensor_scalar(others, rows, -THRESH, THRESH, ALU.max, ALU.min))
                S.wait_alone()
                pool.tensor_tensor(x_rows, rows, others, ALU.subtract).then_inc(s_post[0], 1)

            for g in range(NG):
                t = slice(g * CT, (g + 1) * CT)
                root(g)
                pool.wait_ge(s_x2h, g + 1)
                pool.tensor_tensor(XLO[:, t, P:], xh[:, t], XHI[:, t, P:].bitcast(F32), ALU.subtract).then_inc(s_x2s, 1)
                if g == 0:
                    pool.wait_ge(s_bmr, 16)
                pool.wait_ge(s_xp, g + 1)
                pool.tensor_tensor(xs[:, t], xs[:, t], csr[:].unsqueeze(1).broadcast_to([P, CT, P]), ALU.add).then_inc(s_bm, 1)
            for L in range(2):
                pool.sem_inc(s_pfree[L], 1)
                with S.loop(NC, 1 + L) as c:
                    if L:
                        add_h0(c)
                    root(c + (NG + 2 * NC * L))
                    scatter_chunk(L, c)
                scatter_results(L)
                if L == 0:
                    pool.sem_inc(s_nmr, 1)
                    norm_factors(0, 0, 0)
                    norm_factors(0, 1, 1)
                    with S.loop(NC // 2 - 1, 4) as lap:
                        for i in range(2):
                            wait_alone(pool, need, s_cx, lap * (2 * CT) + (i + 1) * CT)
                            norm_factors(0, lap * 2 + (i + 2), i)
                    pool.wait_ge(s_fac, 1)
                    for g in range(NG):
                        t = slice(g * CT, (g + 1) * CT)
                        operands_of(t, XD, xh[:, t], fD, tmpx[:]).then_inc(s_xd, 1)
                        pool.wait_ge(s_xd, g + 1)
                    S(pool.memset(csr[:], 0.0))
                    pool.sem_inc(s_evf, 1)
                    with S.loop(NC, 17) as c:
                        features(c)
                        wait_alone(pool, need, s_post[0], c + 1)
                        pool.sem_inc(s_evf, 1)
                        t = bass.ds(c * CT, CT)
                        S(operands_of(t, XB2, xh[:, t, :], fB, tmpb[:, :, 0:P]))
                        S.wait_alone()
                        operands_of(t, XD2, xh[:, t, :], fD, tmpb[:, :, 0:P]).then_inc(s_xb2, 1)
                        wait_alone(pool, need, s_xb2, c + 1)
                        for q in range(CT):
                            S.wait_alone()
                            S(pool.tensor_tensor(csr[:], csr[:], xh[:, bass.ds(c * CT + q, 1), :].rearrange("p a d -> p (a d)"), ALU.add))
                    S.wait()
                    pool.sem_inc(s_csr, 1)

            def finish(c):
                y, r = (z[:, bass.ds(c * CT, CT), :] for z in (xh, xs))
                wait_alone(pool, need, s_gm, c + 1)
                pool.tensor_tensor(r, r, y, ALU.add).then_inc(s_fin, 1)

            norm_factors(1, 0, 0)
            norm_factors(1, 1, 1)
            with S.loop(NC // 2 - 1, 4) as lap:
                for i in range(2):
                    wait_alone(pool, need, s_norm, lap * (2 * CT) + (i + 1) * CT)
                    norm_factors(1, lap * 2 + (i + 2), i)
                for i in range(2):
                    finish(lap * 2 + i)
            finish(NC - 2)
            finish(NC - 1)

        TILES_A = [(0, 1), *((jt,) for jt in range(2, NT - 2)), (NT - 2, NT - 1)]
        A_ACT = {1: "in", 5: "relu0", 8: "relu1", 11: "relu2", 20: "copy", 21: "xT"}
        A_DVE = {1: "in", 14: "add", 18: "norm", 23: "top", 29: "pos"}
        A_PE = {1: "mlp0", 4: "mlp1", 7: "mlp2", 10: "merge", 17: "turn", 19: "gate", 25: "prefix"}
        D_DVE = {2: "out", 5: "post"}
        E_ACT = {3: "h0", 24: "copy", 25: "xT"}
        E_DVE = {2: "out", 3: "post", 22: "norm", 26: "top", 31: "pos"}
        E_PE = {21: "turn", 23: "gate", 28: "prefix"}

        @block.scalar
        def _(act):
            def leading_part(c, jt, first):
                g, j = jt // CT, jt % CT
                if j == 0:
                    act.wait_ge(s_ad[g % 2], (c * (NG // 2) + g // 2) * 16 + 16)
                if not (first and jt < 4):
                    act.wait_ge(s_used, c * NT + jt - 3)
                act.activation(HI[:, jt % 4], Abuf[:, g % 2, j], ACT.Copy).then_inc(s_hi, 1)

            def mlp_in(c):
                act.wait_ge(s_acc, c + 1)
                act.activation(hT[:, 0], ACC[0][:], ACT.Identity, scale=eps1[:, 0:1]).then_inc(s_h0, 1)

            def relu(c, layer):
                for v in range(2):
                    act.wait_ge(s_m, c * 6 + (2 * layer + v + 1))
                    bias = bTs[:, 3 * v + layer:3 * v + layer + 1]
                    act.activation(hT[:, v], PM[v][:], ACT.Relu, bias=bias).then_inc(s_r, 1)

            def second_copy(L, c):
                act.wait_ge(s_xn, c + (1 + L * NC))
                if L:
                    act.activation(xh[:, bass.ds(c * CT, CT), :], pay[L][:, 0, :, 0:P], ACT.Copy).then_inc(s_cxh, 1)
                act.activation(pay[L][:, 1, :, 0:P], pay[L][:, 0, :, 0:P], ACT.Copy).then_inc(s_p2, 1)

            def xT_out(L, c):
                act.wait_ge(s_tr, c + (1 + L * NC))
                act.activation(xTb[L][:], PT[:], ACT.Copy).then_inc(s_xT, 1)

            def tail_a(what, c):
                if what == "in":
                    mlp_in(c)
                elif what in ("relu0", "relu1", "relu2"):
                    relu(c, int(what[4]))
                elif what == "copy":
                    second_copy(0, c)
                elif what == "xT":
                    xT_out(0, c)

            act.wait_ge(s_const, 1)
            for jt in range(NT):
                g = jt // CT
                t = slice(g * CT, (g + 1) * CT)
                if jt % CT == 0:
                    if g < 2:
                        act.wait_ge(s_x2[g], 16)
                    act.activation(XHI[:, t, P:], xh[:, t], ACT.Copy).then_inc(s_x2h, 1)
                    act.wait_ge(s_stg, g + 1)
                    act.activation(XHI[:, t, 0:P], stg[:], ACT.Copy).then_inc(s_xh, 1)
                leading_part(0, jt, True)
            act.wait_ge(s_ls, 1)
            with act.Fori(0, NC - 1) as t:
                for jt in range(NT):
                    leading_part(t + 1, jt, False)
                    tail_a(A_ACT.get(jt), t)
            for what in A_ACT.values():
                tail_a(what, NC - 1)

            def experts(L):
                def x_out(k, u):
                    act.wait_ge(s_etx, k + 1 + L * ST)
                    act.activation((exTh, exT)[L][:, u % 2], (B[2], B[5])[u % 2][:, 0:P], ACT.Copy).then_inc(s_exT, 1)

                def h_out(k, u):
                    act.wait_ge(s_eh, k + 1 + L * ST)
                    act.activation(eg[:, u % 2], B[u % 2][:, 0:H], (ACT.Silu, ACT.Copy)[L]).then_inc(s_eg, 1)

                for k in range(ST + 1):
                    if k == RS:
                        with act.Fori(1, ST // RS) as lap:
                            for u in range(RS):
                                x_out(lap * RS + u, u)
                                h_out(lap * RS + (u - 1), (u - 1) % RS)
                    if RS <= k < ST:
                        continue
                    if k < ST:
                        x_out(k, k % RS)
                    if 0 <= k - 1 < ST:
                        h_out(k - 1, (k - 1) % RS)

            def weights(L):
                act.wait_ge(s_wd[L], 1)
                act.activation(wt[:, 1], dl[:], ACT.Exp).then_inc(s_we, 1)

            store_tails(act, 0, 1)
            weights(0)
            experts(0)

            def row_out(c, i):
                act.wait_ge(s_cr, c + 1)
                act.activation(nfrow[:, bass.ds(c * CW, CW)], (PG, B[3])[i][0:1, :], ACT.Copy, scale=-1.0).then_inc(s_crow, 1)

            def normalize_chunk(dst, src, c, i, nth, done):
                act.wait_ge(s_nmr, nth + 2)
                for q in range(CT):
                    t = bass.ds(c * CT + q, 1)
                    act.activation(dst[:, t, :].rearrange("p a d -> p (a d)"), src[:, t, :].rearrange("p a d -> p (a d)"),
                                   ACT.Identity, scale=rstd[:, i, q:q + 1], bias=nmr[:, i, q:q + 1]).then_inc(done, 1)

            def pair_out(lap):
                for i in range(2):
                    normalize_chunk(xh, xs, lap * 2 + i, i, lap * 2 + i, s_cx)
                for i in range(2):
                    act.wait_ge(s_ct, lap * 2 + i + 1)
                    act.activation((xTb[0], xTc)[i][:], (PT, B[2])[i][:], ACT.Copy).then_inc(s_cxT, 1)

            pair_out(0)
            with act.Fori(1, NC // 2) as lap:
                pair_out(lap)
                for i in range(2):
                    row_out(lap * 2 + (i - 2), i)
            for i in range(2):
                row_out(NC - 2 + i, i)
            act.wait_ge(s_zc, 1)
            act.activation(fB[:, 0], zc[:, 0], ACT.Exp).then_inc(s_exps, 1)
            act.activation(fD[:, 0], zc[:, 0], ACT.Exp, scale=SLOPE).then_inc(s_exps, 1)
            act.activation(fA[:], zc[:, 1], ACT.Exp).then_inc(s_exps, 1)
            act.activation(fC[:], zc[:, 2], ACT.Exp).then_inc(s_exps, 1)
            act.activation(lsc[:], ls[:], ACT.Exp, scale=-1.0).then_inc(s_exps, 1)

            def positive(U, c, jt, first):
                g, j = jt // CT, jt % CT
                if U == 0:
                    act.wait_ge(s_code, c * NT + jt + 1)
                elif j == 0:
                    act.wait_ge(s_cl[g % 4], (c * (NG // 4) + g // 4) * 16 + (16 + 4 * NC * NG))
                if not (first and jt < 4):
                    act.wait_ge(s_mu[U], c * NT + jt - 3)
                part = Cbuf[:, g % 4, j * CW:(j + 1) * CW]
                shared = U == 0 and jt % 8 in BY_ACT
                n = c * (NT // 8 * len(BY_ACT)) + (jt // 8 * len(BY_ACT) + sum(b < jt % 8 for b in BY_ACT))
                if shared:
                    if not (first and n == 0):
                        act.wait_ge(s_ma, n)
                    act.activation(away[:], part, ACT.Abs, bias=minus2[:]).then_inc(s_abs, 1)
                act.activation(MP[:, jt % 4], part, ACT.Relu, bias=minus2[:]).then_inc(s_mp[U], 1)
                if shared:
                    act.wait_ge(s_abs, n + 1)
                    act.activation(MM[:, jt % 4], away[:], ACT.Relu, scale=-1.0, bias=ones[:, 0:1]).then_inc(s_ma, 1)

            def tail_e(what, c, first):
                if what == "h0":
                    act.wait_ge(s_h0l, c * 16 + 16)
                    if not first:
                        act.wait_ge(s_h0x, c)
                    act.activation(h0s[:], h0b[:], ACT.Copy, scale=k12[:, 1:2]).then_inc(s_h0s, 1)
                elif what == "copy":
                    second_copy(1, c)
                elif what == "xT":
                    xT_out(1, c)

            for U in range(2):
                if U:
                    act.wait_ge(s_mu[0], NC * NT)
                for jt in range(NT):
                    positive(U, 0, jt, True)
                for jt in range(NT):
                    positive(U, 1, jt, False)
                    if U:
                        tail_e(E_ACT.get(jt), 0, True)
                with act.Fori(1, NC - 1) as t:
                    for jt in range(NT):
                        positive(U, t + 1, jt, False)
                        if U:
                            tail_e(E_ACT.get(jt), t, False)
            for what in E_ACT.values():
                tail_e(what, NC - 1, False)
            store_tails(act, 1, 1)
            weights(1)
            experts(1)
            with act.Fori(0, NC // 2) as lap:
                for i in range(2):
                    c = lap * 2 + i
                    normalize_chunk(xh, xh, c, i, c + NC, s_norm)

        @block.tensor
        def _(pe):
            pe.wait_ge(s_const, 1)

            def aggregate(c, some, first):
                jt = some[-1]
                if first and some[0] % CT == 0:
                    pe.wait_ge(s_xp, jt // CT + 1)
                    pe.wait_ge(s_x2s, jt // CT + 1)
                for v in range(2):
                    if some[0] == 0 and not first:
                        pe.wait_ge((s_h0, s_h1)[v], c)
                    for j in some:
                        if v == 0:
                            pe.wait_ge(s_hi, c * NT + j + 1)
                        for X, start in ((XHI, j == 0), (XLO, False)):
                            pe.matmul(ACC[v][:], X[:, j, v * P:(v + 1) * P], HI[:, j % 4], start=start, stop=False)
                        if v == 0:
                            pe.wait_ge(s_lo, c * NT + j + 1)
                        last = pe.matmul(ACC[v][:], XHI[:, j, v * P:(v + 1) * P], LO[:, j % 4], start=False, stop=j == NT - 1)
                        if v == 1:
                            last.then_inc(s_used, 1)
                        elif j == NT - 1:
                            last.then_inc(s_acc, 1)

            def mlp(c, layer):
                for v in range(2):
                    if layer == 0:
                        pe.wait_ge((s_h0, s_h1)[v], c + 1)
                    else:
                        pe.wait_ge(s_r, c * 6 + (2 * layer - 1 + v))
                    pe.matmul(PM[v][:], WTs[:, 3 * v + layer], hT[:, v], start=True, stop=True).then_inc(s_m, 1)

            def merge(c):
                pe.wait_ge(s_r, c * 6 + 6)
                for q in range(CT):
                    for v in range(2):
                        last = pe.matmul(PG[:, q * P:(q + 1) * P], hT[:, v, q * P:(q + 1) * P], WmTs[:, v],
                                         start=v == 0, stop=v == 1)
                last.then_inc(s_g, 1)

            def turn(L, c):
                pe.wait_ge(s_xn, c + (1 + L * NC))
                for q in range(CT):
                    last = pe.transpose(PT[:, q * P:(q + 1) * P], pay[L][:, 0, q, 0:P], ident[:])
                last.then_inc(s_tr, 1)

            def gate(L, c):
                pe.wait_ge(s_xT, c + (1 + L * NC))
                for q in range(CT):
                    last = pe.matmul(PGT[:, q * E:(q + 1) * E], xTb[L][:, q * P:(q + 1) * P], gws[:, L], start=True, stop=True)
                last.then_inc(s_gt, 1)

            def prefix(L, c):
                pe.wait_ge(s_oh, c + (1 + L * NC))
                pe.matmul(PPX[:, 0:CT * E], upper[:], oh[:, 2].rearrange("p q e -> p (q e)"), start=True, stop=False)
                for q in range(1, CT):
                    pe.matmul(PPX[:, q * E:CT * E], ones[:], oh[:, 2, 0:CT - q].rearrange("p q e -> p (q e)"), start=False, stop=False)
                for q in range(CT):
                    last = pe.matmul(PPX[:, q * E:(q + 1) * E], ones[:], run[:], start=False, stop=q == CT - 1)
                last.then_inc(s_pp, 1)

            def tail(L, what, c):
                if what in ("mlp0", "mlp1", "mlp2"):
                    mlp(c, int(what[3]))
                elif what == "merge":
                    merge(c)
                elif what == "turn":
                    turn(L, c)
                elif what == "gate":
                    gate(L, c)
                elif what == "prefix":
                    prefix(L, c)

            for some in TILES_A:
                aggregate(0, some, True)
            pe.wait_ge(s_ls, 1)
            with pe.Fori(0, NC - 1) as t:
                for some in TILES_A:
                    aggregate(t + 1, some, False)
                    tail(0, A_PE.get(some[-1]), t)
            for what in A_PE.values():
                tail(0, what, NC - 1)

            def tile_table(L):
                pe.wait_ge(s_pos, NC * (1 + L))
                pe.matmul(PGT[:, 0:E], ones[:], run[:], start=True, stop=True).then_inc(s_cn, 1)
                pe.wait_ge(s_tl, L + 1)
                pe.matmul(PPX[0:1, 0:P], tcol[:, 0:1], ident[:], start=True, stop=True)
                pe.matmul(PPX[0:1, P:2 * P], tcol[:, 2:3], ident[:], start=True, stop=True).then_inc(s_tt, 1)

            def experts(L):
                width = (2 * H, H)[L]
                r = [pe.alloc_register(f"expert{L}{u}") for u in range(RS)]

                def expert(u):
                    return pe.snap(r[u], min_val=0, max_val=E - 1)

                def x_in(k, lap, u):
                    pe.reg_load(r[u], tiles[0:1, 0, bass.ds(k, 1)])
                    pe.wait_ge(s_ld[u], lap * 16 + 16 + L * 16 * (ST // RS))
                    pe.transpose((B[2], B[5])[u % 2][:, 0:P], xin[:, u, 0:P], ident[:]).then_inc(s_etx, 1)

                def hidden(k, u):
                    e = expert(u)
                    pe.wait_ge(s_exT, k + 1 + L * ST)
                    dst = B[u % 2][:, 0:width]
                    if L:
                        pe.matmul(dst, exT[:, u % 2], V1s[:, bass.ds(e, 1), :].rearrange("p a n -> p (a n)"),
                                  start=True, stop=True).then_inc(s_eh, 1)
                        return
                    for X, W in ((exTh, W12h), (exTh, W12l), (exTl, W12h)):
                        if X is exTl:
                            pe.wait_ge(s_exl, k + 1)
                        last = pe.matmul(dst, X[:, u % 2], W[:, bass.ds(e, 1), :].rearrange("p a n -> p (a n)"),
                                         start=W is W12h and X is exTh, stop=X is exTl)
                    last.then_inc(s_eh, 1)

                def result(k, u, first):
                    e = expert(u)
                    pe.wait_ge(s_ehT, k + 1 + L * ST)
                    if not first:
                        pe.wait_ge(s_ey, k - 1 + L * ST)
                    for h in range(2):
                        last = pe.matmul((B[4], B[6])[u % 2][:, 0:P], ehT[:, u % 2, h],
                                         (W3s, V2s)[L][:, bass.ds(e, 1), h, :].rearrange("p a n -> p (a n)"),
                                         start=h == 0, stop=h == 1)
                    last.then_inc(s_eo, 1)

                def hidden_turn(k, u):
                    pe.wait_ge((s_ehid, s_eg)[L], k + 1 + L * ST)
                    for h in range(2):
                        src = (ehid, eg)[L][:, u % 2, h * P:(h + 1) * P]
                        last = pe.transpose((B[3], B[7])[u % 2][:, h * P:(h + 1) * P], src, ident[:])
                    last.then_inc(s_eth, 1)

                pe.wait_ge(s_tu[L], 1)
                pe.wait_ge((s_wsp, s_w1)[L], (8, 48)[L])
                for k in range(ST + 4):
                    if k == RS:
                        with pe.Fori(1, ST // RS) as lap:
                            for u in range(RS):
                                x_in(lap * RS + u, lap, u)
                                hidden(lap * RS + (u - 1), (u - 1) % RS)
                                result(lap * RS + (u - 4), (u - 4) % RS, False)
                                hidden_turn(lap * RS + (u - 2), (u - 2) % RS)
                    if RS <= k < ST:
                        continue
                    if k < ST:
                        x_in(k, 0, k % RS)
                    if 0 <= k - 1 < ST:
                        hidden(k - 1, (k - 1) % RS)
                    if 0 <= k - 4 < ST:
                        result(k - 4, (k - 4) % RS, k - 4 < 2)
                    if 0 <= k - 2 < ST:
                        hidden_turn(k - 2, (k - 2) % RS)

            tile_table(0)
            experts(0)

            for pair in range(0, NC, 2):
                for c in (pair, pair + 1):
                    pe.wait_ge(s_cx, CT * (c + 1))
                    for q in range(CT):
                        last = pe.transpose((PT, B[2])[c % 2][:, q * P:(q + 1) * P], xh[:, c * CT + q], ident[:])
                    last.then_inc(s_ct, 1)
                for c in (pair, pair + 1):
                    xT = (xTb[0], xTc)[c % 2]
                    pe.wait_ge(s_cxT, c + 1)
                    for q in range(CT):
                        t = c * CT + q
                        last = pe.matmul(PGT[:, 2 * t:2 * t + 2], xT[:, q * P:(q + 1) * P], a_s[:], start=True, stop=True)
                    last.then_inc(s_cf, 1)
                    if c >= 2:
                        pe.wait_ge(s_crow, c - 1)
                    pe.matmul((PG, B[3])[c % 2][0:1, :], a_s[:, 0:1], xT[:], start=True, stop=True).then_inc(s_cr, 1)
                for t in range(pair * CT, (pair + 2) * CT):
                    last = pe.matmul(B[7][:, 0:P], ones[:], xh[:, t], start=t == 0, stop=t == NT - 1)
            last.then_inc(s_csp, 1)
            pe.wait_ge(s_ext, 1)
            pe.transpose(B[0][0:2, 0:P], ext[:], ident[:]).then_inc(s_extT, 1)
            pe.wait_ge(s_ext, 2)
            pe.matmul(B[1][:, 0:1], half[:], bounds[:], start=True, stop=True).then_inc(s_extr, 1)

            def column_sums():
                pe.wait_ge(s_csr, 1)
                pe.matmul(PG[:, 0:P], ones[:], csr[:], start=True, stop=True).then_inc(s_csp, 1)

            def multiply(U, c, some, first):
                operands = ((XB, XD), (XB2, XD2))[U]
                jt = some[-1]
                if U == 0 and first and jt % CT == 0:
                    pe.wait_ge(s_xb, jt // CT + 1)
                    pe.wait_ge(s_xd, jt // CT + 1)
                if U == 1 and first and jt % CT == 0:
                    pe.wait_ge(s_xb2, jt // CT + 1)

                def made(kind):
                    if kind == 0:
                        pe.wait_ge(s_mp[U], c * NT + jt + 1)
                    elif U == 1:
                        pe.wait_ge(s_mm[1], c * NT + jt + 1)
                    else:
                        acts = jt // 8 * len(BY_ACT) + sum(b <= jt % 8 for b in BY_ACT)
                        if len(some) > 1 or jt % 8 in BY_ACT:
                            pe.wait_ge(s_ma, c * (NT // 8 * len(BY_ACT)) + acts)
                        if len(some) > 1 or jt % 8 not in BY_ACT:
                            pe.wait_ge(s_mm[0], c * (NT // 8 * (8 - len(BY_ACT))) + (jt + 1 - acts))

                def product(kind, q, j):
                    if U == 0:
                        dst = B[4 * kind + q][:, 0:260]
                    else:
                        dst = B[q][:, kind * 2 * P:(kind + 1) * 2 * P]
                    return pe.matmul(dst, (MP, MM)[kind][:, j % 4, q * P:(q + 1) * P],
                                     operands[kind][:, j].rearrange("p h n -> p (h n)"),
                                     start=j == 0 and (U == 0 or kind == 0), stop=j == NT - 1,
                                     skip_group_check=U == 1)

                if len(some) == 1:
                    for kind in range(2):
                        made(kind)
                        for q in range(CT):
                            last = product(kind, q, jt)
                    last.then_inc(s_mu[U], 1)
                elif U == 0:
                    for kind in range(2):
                        made(kind)
                        for q in range(CT):
                            pe.wait_ge(s_ev[0], c * 8 + (kind * 4 + q - 7))
                            for j in some:
                                last = product(kind, q, j)
                                if kind and q == CT - 1:
                                    last.then_inc(s_mu[0], 1)
                else:
                    made(0)
                    made(1)
                    for q in range(CT):
                        pe.wait_ge(s_ev[1], c * 4 + (q - 3))
                        for j in some:
                            product(0, q, j)
                            last = product(1, q, j)
                            if q == CT - 1:
                                last.then_inc(s_mu[1], 1)

            for U in range(2):
                if U == 0:
                    pe.wait_ge(s_crow, NC)
                    pe.wait_ge(s_cs, 2)
                else:
                    pe.wait_ge(s_ev[0], 8 * NC)
                for jt in range(NT):
                    multiply(U, 0, (jt,), True)
                if U:
                    column_sums()
                with pe.Fori(0, NC - 1) as t:
                    multiply(U, t + 1, range(ONSET), False)
                    for jt in range(ONSET, NT):
                        multiply(U, t + 1, (jt,), False)
                        if U:
                            tail(1, E_PE.get(jt), t)
            for what in E_PE.values():
                tail(1, what, NC - 1)
            tile_table(1)
            experts(1)

        @block.vector
        def _(dve):
            need = dve.alloc_register("need_dve")
            D = Steps(dve, s_dve, need)

            def rest(c, jt, first):
                g, j = jt // CT, jt % CT
                dve.wait_ge(s_hi, c * NT + jt + 1)
                if not (first and jt < 4):
                    dve.wait_ge(s_used, c * NT + jt - 3)
                dve.tensor_tensor(LO[:, jt % 4], Abuf[:, g % 2, j], HI[:, jt % 4].bitcast(F32), ALU.subtract).then_inc(s_lo, 1)
                if j == CT - 1:
                    if not (first and g < 2):
                        dve.wait_ge(s_mst[g % 2], (c * (NG // 2) + g // 2) * 16)
                    dve.tensor_scalar(Mbuf[:, g % 2], Abuf[:, g % 2].rearrange("p t n -> p (t n)"), 0.0, 2.0,
                                      ALU.is_gt, ALU.mult).then_inc(s_mk, 1)

            def statistics(src, slot=0):
                for q in range(CT):
                    if q == 2:
                        yield
                    D(dve.bn_stats(stat[:, slot, q], src[:, q]))
                yield
                D.wait_alone()
                for q in range(CT):
                    last = dve.bn_aggr(mv[:, slot, q], stat[:, slot, q])
                    if q < CT - 1:
                        D(last)
                last.then_inc(s_var, 1)
                yield

            def normalize(dst, src, q, slot=0):
                return dve.tensor_scalar(dst, src, mv[:, slot, q, 0:1], rstd[:, slot, q:q + 1], ALU.subtract, ALU.mult)

            def chunk_of(c):
                return xs[:, bass.ds(c * CT, CT), :]

            def split(hi, lo, src):
                D(dve.tensor_copy(hi, src))
                D.wait()
                return dve.tensor_tensor(lo, src, hi.bitcast(F32), ALU.subtract)

            def operands_a(g):
                t = slice(g * CT, (g + 1) * CT)
                dve.wait_ge(s_root, g + 1)
                if g:
                    dve.wait_ge(s_xp, g)
                for q in range(CT):
                    last = normalize(stg[:, q], xs[:, g * CT + q], q)
                    if q < CT - 1:
                        D(last)
                last.then_inc(s_stg, 1)

            def rest_a(g):
                t = slice(g * CT, (g + 1) * CT)
                dve.wait_ge(s_xh, g + 1)
                dve.tensor_tensor(XLO[:, t, 0:P], stg[:], XHI[:, t, 0:P].bitcast(F32), ALU.subtract).then_inc(s_xp, 1)

            def mlp_in(c):
                dve.wait_ge(s_used, c * NT + NT)
                dve.tensor_scalar(hT[:, 1], ACC[1][:], eps1[:, 1:2], None, ALU.mult).then_inc(s_h1, 1)
                yield

            def add_gnn(c):
                dve.wait_ge(s_g, c + 1)
                D(dve.tensor_tensor(chunk_of(c), PG[:].rearrange("p (t n) -> p t n", t=CT), chunk_of(c), ALU.add))
                yield
                D.wait_alone()
                yield from statistics(chunk_of(c))

            def payload(L, c):
                dve.wait_ge(s_root, c + (NG + 2 * NC * L + 1))
                dve.wait_ge(s_pfree[L], c + 1)
                for k in range(2):
                    D(dve.tensor_copy(pay[L][:, k, :, P].bitcast(U32), tok[:, k, bass.ds(c * CT, CT)]))
                for q in range(CT):
                    last = normalize(pay[L][:, 0, q, 0:P], xs[:, bass.ds(c * CT + q, 1), :].rearrange("p a d -> p (a d)"), q)
                    if q < CT - 1:
                        D(last)
                last.then_inc(s_xn, 1)
                yield

            def top_two(L, c):
                dve.wait_ge(s_gt, c + (1 + L * NC))
                D(dve.tensor_tensor(lg[:], PGT[:, 0:CT * E].rearrange("p (q e) -> p q e", q=CT),
                                    gbs[:, L].unsqueeze(1).broadcast_to([P, CT, E]), ALU.add))
                yield
                D.wait_alone()
                for q in range(CT):
                    D(dve.max(top[:, q], lg[:, q]))
                yield
                D.wait_alone()
                for q in range(CT):
                    D(dve.max_index(topi[:, q], top[:, q], lg[:, q]))
                D(dve.tensor_tensor(dl[:, bass.ds(c * CT, CT)], top[:, :, 1], top[:, :, 0], ALU.subtract))
                yield
                D.wait()
                D(dve.tensor_copy(topf[:], topi[:]))
                yield
                D.wait()
                for k in range(2):
                    D(dve.tensor_tensor(oh[:, k], iota_e[:].unsqueeze(1).broadcast_to([P, CT, E]),
                                        topf[:, :, k:k + 1].broadcast_to([P, CT, E]), ALU.is_equal))
                yield
                D.wait()
                dve.tensor_tensor(oh[:, 2], oh[:, 0], oh[:, 1], ALU.add).then_inc(s_oh, 1)
                yield

            def positions(L, c):
                dve.wait_ge(s_pp, c + (1 + L * NC))
                free = PPX[:, 0:CT * E].rearrange("p (q e) -> p q e", q=CT)
                for k in range(2):
                    D(dve.tensor_tensor(posf[:, k], oh[:, k], free, ALU.mult))
                D(dve.tensor_reduce(cnt[:, 0], oh[:, 2].rearrange("p q e -> p e q"), AX.X, ALU.add))
                yield
                D.wait()
                D(dve.tensor_reduce(posr[:], posf[:], AX.X, ALU.add))
                D(dve.tensor_tensor(run[:], run[:], cnt[:, 0], ALU.add))
                yield
                D.wait()
                dve.tensor_copy(pos[:], posr[:]).then_inc(s_pos, 1)
                yield

            def first_rows():
                D(dve.memset(run[:], 0.0))
                D.wait()
                D(dve.tensor_copy(run[0:1, :], ecap[0:1, :]))
                D.wait()

            def now(steps):
                for _ in steps:
                    pass

            def part_a(what, c):
                return {"in": mlp_in, "add": add_gnn}[what](c) if what in ("in", "add") else routing(0, what, c)

            def routing(L, what, c):
                return {"norm": payload, "top": top_two, "pos": positions}[what](L, c)

            def between(places, part, c, tile, pace):
                steps = iter(())
                for jt in range(NT):
                    tile(jt)
                    if jt in places:
                        now(steps)
                        steps = part(places[jt], c)
                    for _ in range(pace(jt)):
                        next(steps, None)
                now(steps)

            def behind(places, part, c):
                for what in places.values():
                    now(part(what, c))

            dve.wait_ge(s_const, 1)
            first_rows()
            dve.wait_ge(s_x[0], 16)
            now(statistics(xs[:, 0:CT]))
            for jt in range(NT):
                g = jt // CT
                if jt % CT == 0:
                    operands_a(g)
                    rest_a(g)
                    if g == 0:
                        dve.wait_ge(s_x[1], 16)
                    if g < NG - 1:
                        D.wait()
                        dve.wait_ge(s_stg, g + 1)
                        now(statistics(xs[:, (g + 1) * CT:(g + 2) * CT]))
                rest(0, jt, True)
            dve.wait_ge(s_cst, 16 * 11)
            dve.tensor_scalar(eps1[:], eps1[:], 2.0, None, ALU.add).then_inc(s_ls, 1)
            dve.wait_ge(s_bm, NG)
            with D.loop(NC - 1, 31) as t:
                between(A_DVE, part_a, t, lambda jt: rest(t + 1, jt, False), lambda jt: 2)
            def split_weights(pieces):
                for n in pieces:
                    part = slice(n % 4 * E // 4, (n % 4 + 1) * E // 4)
                    if n < 4:
                        dve.tensor_copy(W12h[:, part], W12s[:, part]).then_inc(s_wsp, 1)
                    else:
                        dve.wait_ge(s_wsp, n - 3)
                        dve.tensor_tensor(W12l[:, part], W12s[:, part], W12h[:, part].bitcast(F32), ALU.subtract).then_inc(s_wsp, 1)

            for what in A_DVE.values():
                if what == "add":
                    dve.wait_ge(s_w, 32 * NC)
                    split_weights(range(6))
                if what == "top":
                    split_weights((6,))
                now(part_a(what, NC - 1))

            def tile_table(L):
                end, need, upto, tmp = (cnt[:, i] for i in range(4))
                dve.wait_ge(s_cn, L + 1)
                D(dve.tensor_copy(end, PGT[:, 0:E]))
                D.wait()
                dve.tensor_copy(endu[:], end).then_inc(s_end, 1)
                D(dve.tensor_tensor(tmp, end, ecap[:], ALU.subtract))
                D.wait()
                D(dve.tensor_scalar(nuu[:], tmp, float(P - 1), None, ALU.add))
                D.wait()
                D(dve.tensor_scalar(nuu[:], nuu[:], 7, None, ALU.logical_shift_right))
                D.wait()
                D(dve.tensor_copy(need, nuu[:]))
                D.wait()
                D(dve.tensor_tensor_scan(upto, ones[:, 0:E], need, 0.0, ALU.mult, ALU.add))
                D.wait()
                D(dve.tensor_scalar(tmp, upto, kcol[:, 0:1], None, ALU.is_le))
                D.wait()
                D(dve.tensor_reduce(tcol[:, 0:1], tmp, AX.X, ALU.add))
                D(dve.tensor_tensor(need, need, tmp, ALU.mult))
                D.wait()
                D(dve.tensor_reduce(tcol[:, 1:2], need, AX.X, ALU.add))
                D.wait()
                D(dve.tensor_tensor(tcol[:, 2:3], kcol[:], tcol[:, 1:2], ALU.subtract))
                D(dve.tensor_scalar(tcol[:, 3:4], tcol[:, 0:1], float(CAP), None, ALU.mult))
                D.wait()
                D(dve.scalar_tensor_tensor(out=tcol[:, 2:3], in0=tcol[:, 2:3], scalar=float(P), in1=tcol[:, 3:4],
                                           op0=ALU.mult, op1=ALU.add))
                D.wait()
                D(dve.tensor_scalar(tcol[:, 2:3], tcol[:, 2:3], float(E * CAP), None, ALU.min))
                dve.tensor_scalar(tcol[:, 0:1], tcol[:, 0:1], float(E - 1), None, ALU.min).then_inc(s_tl, 1)
                dve.wait_ge(s_tt, L + 1)
                dve.tensor_copy(tiles[:], PPX[0:1, 0:2 * P].rearrange("p (a n) -> p a n", a=2)).then_inc(s_tu[L], 1)
                dve.wait_ge(s_tu[L], 1)
                if L == 0:
                    first_rows()
                dve.sem_inc(s_wd[L], 1)

            def weights(L):
                dve.wait_ge(s_we, L + 1)
                D(dve.tensor_scalar(wt[:, 0], wt[:, 1], 1.0, None, ALU.add))
                D.wait()
                D(dve.reciprocal(wt[:, 0], wt[:, 0]))
                D.wait()
                D(dve.tensor_tensor(wt[:, 1], wt[:, 1], wt[:, 0], ALU.mult))

            def experts(L):
                r = [dve.alloc_register(f"bias{u}") for u in range(RS)] if L else []

                def expert(u):
                    return dve.snap(r[u], min_val=0, max_val=E - 1)

                def x_rest(k, u):
                    if L == 0:
                        dve.wait_ge(s_exT, k + 1)
                        dve.tensor_tensor(exTl[:, u % 2], (B[2], B[5])[u % 2][:, 0:P], exTh[:, u % 2].bitcast(F32),
                                          ALU.subtract).then_inc(s_exl, 1)

                def gated(k, u):
                    if L:
                        dve.reg_load(r[u], tiles[0:1, 0, bass.ds(k, 1)])
                    if L == 0:
                        dve.wait_ge(s_eg, k + 1 + L * ST)
                        dve.tensor_tensor(ehid[:, u % 2], B[u % 2][:, H:2 * H], eg[:, u % 2], ALU.mult).then_inc(s_ehid, 1)

                def hidden_out(k, u):
                    src = (B[3], B[7])[u % 2][:, 0:H].rearrange("p (h n) -> p h n", h=2)
                    if L == 0:
                        dve.wait_ge(s_eth, k + 1 + L * ST)
                        dve.tensor_copy(ehT[:, u % 2], src).then_inc(s_ehT, 1)
                        return
                    e = expert(u)
                    dve.wait_ge(s_eth, k + 1 + L * ST)
                    for h in range(2):
                        last = dve.tensor_scalar(ehT[:, u % 2, h], src[:, h], b1c[:, bass.ds(e, 1), h], 0.0, ALU.add, ALU.max)
                        if h == 0:
                            D(last)
                    last.then_inc(s_ehT, 1)

                def result_out(k, u):
                    if L:
                        e = expert(u)
                    dve.wait_ge(s_eo, k + 1 + L * ST)
                    dve.wait_ge(s_efree[L], k + 1)
                    src = (B[4], B[6])[u % 2][:, 0:P]
                    if L == 0:
                        dve.tensor_copy(ey[:, u], src).then_inc(s_ey, 1)
                    else:
                        bias = C2s[:, bass.ds(e, 1), :].rearrange("p a n -> p (a n)")
                        dve.tensor_tensor(ey[:, u], src, bias, ALU.add).then_inc(s_ey, 1)

                if L:
                    dve.wait_ge(s_w1, 48)
                for k in range(ST + 4):
                    if k == RS:
                        with D.loop(ST // RS - 1, RS * L) as lap:
                            for u in range(RS):
                                x_rest(lap * RS + (u + RS), u)
                                gated(lap * RS + (u + RS - 1), (u - 1) % RS)
                                hidden_out(lap * RS + (u + RS - 2), (u - 2) % RS)
                                result_out(lap * RS + (u + RS - 4), (u - 4) % RS)
                    if RS <= k < ST:
                        continue
                    if k < ST:
                        x_rest(k, k % RS)
                    if 0 <= k - 1 < ST:
                        gated(k - 1, (k - 1) % RS)
                    if 0 <= k - 2 < ST:
                        hidden_out(k - 2, (k - 2) % RS)
                    if 0 <= k - 4 < ST:
                        result_out(k - 4, (k - 4) % RS)

            def combine(L, pair, lap, at4):
                dst = (xs, xh)[L]
                for i in range(2):
                    dve.wait_ge(s_yl[at4 + i], lap * 32 + (32 + L * 16 * NC // 2))
                for k in range(2):
                    for i, c in enumerate(pair):
                        for q in range(CT):
                            t = bass.ds(c * CT + q, 1)
                            row = dst[:, t, :].rearrange("p a d -> p (a d)")
                            D(dve.scalar_tensor_tensor(out=row, in0=yb[:, at4 + i, k, q], scalar=wt[:, k, t],
                                                       in1=row, op0=ALU.mult, op1=ALU.add))
                    D.wait_alone()
                dve.sem_inc(s_cb[L], 1)
                wait_alone(dve, need, s_nmr, lap * 4 + (at4 + 1 + NC * L))
                steps = [statistics(dst[:, bass.ds(c * CT, CT), :], i) for i, c in enumerate(pair)]
                for _ in range(4):
                    for s in steps:
                        next(s, None)

            tile_table(0)
            split_weights((7,))
            weights(0)
            experts(0)

            with D.loop(NC // 4, 60) as lap:
                for at4 in (0, 2):
                    pair = [lap * 4 + (at4 + i) for i in range(2)]
                    combine(0, pair, lap, at4)
            dve.wait_ge(s_cf, NC)
            D(dve.tensor_copy(f12[:], PGT[:, 0:2 * NT].rearrange("p (t n) -> p t n", t=NT)))
            D.wait()
            D(dve.tensor_reduce(ext[:, 0:1], f12[:, :, 1], AX.X, ALU.max))
            D(dve.tensor_reduce(ext[:, 1:2], f12[:, :, 1], AX.X, ALU.min))
            D.wait()
            dve.tensor_scalar(ext[:, 1:2], ext[:, 1:2], -1.0, None, ALU.mult).then_inc(s_ext, 1)
            dve.wait_ge(s_extT, 1)
            dve.tensor_reduce(bounds[:], B[0][0:2, 0:P], AX.X, ALU.max).then_inc(s_ext, 1)
            dve.wait_ge(s_csp, 1)
            dve.tensor_copy(cs[:], B[7][:, 0:P]).then_inc(s_cs, 1)
            dve.wait_ge(s_extr, 1)
            dve.tensor_copy(mid[:], B[1][:, 0:1]).then_inc(s_cs, 1)
            dve.wait_ge(s_cs, 2)
            D(dve.tensor_scalar(zc[:, 1], f12[:, :, 0], mid[:, 0:1], None, ALU.add))
            D(dve.tensor_scalar(zc[:, 0], f12[:, :, 1], mid[:, 0:1], None, ALU.subtract))
            D.wait()
            D(dve.scalar_tensor_tensor(out=al[:], in0=zc[:, 1], scalar=SLOPE, in1=zc[:, 1], op0=ALU.mult, op1=ALU.max))
            D.wait()
            D(dve.scalar_tensor_tensor(out=zc[:, 2], in0=zc[:, 1], scalar=SLOPE, in1=al[:], op0=ALU.mult, op1=ALU.subtract))
            dve.tensor_tensor(zc[:, 1], zc[:, 1], al[:], ALU.subtract).then_inc(s_zc, 1)
            dve.wait_ge(s_exps, 5)
            D(dve.tensor_tensor(fB[:, 1], fB[:, 0], fB[:, 0], ALU.mult))
            D(dve.tensor_tensor(fD[:, 1], fD[:, 0], fD[:, 0], ALU.mult))
            D(dve.tensor_scalar(ls[:], lsc[:], 1.0, None, ALU.add))
            D.wait()
            D(dve.reciprocal(ls[:], ls[:]))
            D.wait()
            D(dve.tensor_scalar(lsc[:], ls[:], -1.0, 1.0, ALU.mult, ALU.add))
            D.wait()
            dve.sem_inc(s_fac, 1)
            D(dve.tensor_scalar(k12[:, 0:1], lsc[:, 1:2], ls[:, 0:1], None, ALU.mult))
            D(dve.tensor_scalar(k12[:, 1:2], lsc[:, 1:2], lsc[:, 0:1], None, ALU.mult))
            D(dve.tensor_scalar(nc3[:], ls[:, 3:4], -1.0, None, ALU.mult))
            D.wait()

            def operands_d(g):
                t = slice(g * CT, (g + 1) * CT)
                if g:
                    dve.wait_ge(s_xb, g)
                D(dve.tensor_tensor(tmpb[:, :, 0:P], xh[:, t], fB[:, 0, t].unsqueeze(2).broadcast_to([P, CT, P]), ALU.mult))
                for k in range(2):
                    D(dve.tensor_copy(tmpb[:, :, P + k], fB[:, k, t]))
                D.wait()
                split(XB[:, t, 0], XB[:, t, 1], tmpb[:]).then_inc(s_xb, 1)

            def code_ahead(c, jt, slot, last):
                if jt + AHEAD < NT:
                    code(c, jt + AHEAD, slot)
                elif not last:
                    code(c + 1, jt + AHEAD - NT, 1 - slot)

            def code(c, jt, slot):
                g, j = jt // CT, jt % CT
                if j == 0:
                    dve.wait_ge(s_cl[g % 4], (c * (NG // 4) + g // 4) * 16 + 16)
                part = Cbuf[:, g % 4, j * CW:(j + 1) * CW]
                dve.scalar_tensor_tensor(out=part, in0=nf1[:, slot], scalar=f12[:, jt, 1:2], in1=part,
                                         op0=ALU.is_lt, op1=ALU.add).then_inc(s_code, 1)

            def other(U, c, jt, first):
                g, j = jt // CT, jt % CT
                if U == 0:
                    dve.wait_ge(s_code, c * NT + jt + 1)
                elif j == 0:
                    dve.wait_ge(s_cl[g % 4], (c * (NG // 4) + g // 4) * 16 + (16 + 4 * NC * NG))
                if not (first and jt < 4):
                    dve.wait_ge(s_mu[U], c * NT + jt - 3)
                dve.tensor_scalar(MM[:, jt % 4], Cbuf[:, g % 4, j * CW:(j + 1) * CW], 2.0, None, ALU.is_equal).then_inc(s_mm[U], 1)

            def products_out(U, c):
                dve.wait_ge(s_mu[U], c * NT + NT)
                if U == 0:
                    dve.wait_ge(s_evf, c + 1)
                    for kind in range(2):
                        for q in range(CT):
                            parts = B[4 * kind + q][:, 0:260].rearrange("p (h n) -> p n h", h=2)
                            dve.tensor_reduce(ev[:, q, kind], parts, AX.X, ALU.add).then_inc(s_ev[0], 1)
                else:
                    for q in range(CT):
                        parts = B[q][:].rearrange("p (s h n) -> p s n h", s=2, h=2)
                        dve.tensor_reduce(ev2[:, q], parts, AX.X, ALU.add).then_inc(s_ev[1], 1)
                yield
                dve.wait_ge(s_ev[U], c * (8, 4)[U] + (8, 4)[U])

            def scaled_rows(c):
                for q in range(CT):
                    row = ev2[:, q, 0]
                    D(dve.tensor_scalar(row, row, al[:, bass.ds(c * CT + q, 1)], None, ALU.mult))
                for other_part in (True, False):
                    for q in range(CT):
                        if q % 2 == 0:
                            yield
                            D.wait()
                        row = ev2[:, q, 0]
                        part = ev2[:, q, 1] if other_part else cs[:]
                        factor = (ga if other_part else ep)[:, bass.ds(c * CT + q, 1)]
                        D(dve.scalar_tensor_tensor(out=row, in0=part, scalar=factor, in1=row, op0=ALU.mult, op1=ALU.add))
                yield
                D.wait()

            def post_d(c):
                t = bass.ds(c * CT, CT)
                A4, C4, a4, g4, e4 = fA[:, t], fC[:, t], al[:, t], ga[:, t], ep[:, t]
                z = [q8[:, i] for i in range(8)]
                sp_, sm, qp, qm = (ev[:, :, k, P + n] for n in range(2) for k in range(2))
                D(dve.tensor_tensor(z[0], A4, sp_, ALU.mult))
                D(dve.tensor_tensor(z[1], C4, sm, ALU.mult))
                yield
                D.wait()
                D(dve.tensor_tensor(z[2], z[0], z[1], ALU.add))
                yield
                D.wait()
                D(dve.tensor_scalar(z[3], z[2], 0.0, None, ALU.is_equal))
                yield
                D.wait()
                D(dve.scalar_tensor_tensor(out=z[2], in0=z[3], scalar=float(N), in1=z[2], op0=ALU.mult, op1=ALU.add))
                yield
                D.wait()
                D(dve.reciprocal(z[4], z[2]))
                yield
                D.wait()
                D(dve.tensor_tensor(a4, A4, z[4], ALU.mult))
                D(dve.tensor_tensor(g4, C4, z[4], ALU.mult))
                D(dve.tensor_tensor(e4, z[3], z[4], ALU.mult))
                yield
                D.wait()
                D(dve.tensor_tensor(z[5], a4, a4, ALU.mult))
                D(dve.tensor_tensor(z[6], g4, g4, ALU.mult))
                yield
                D.wait()
                D(dve.tensor_tensor(z[5], z[5], qp, ALU.mult))
                D(dve.tensor_tensor(z[6], z[6], qm, ALU.mult))
                yield
                D.wait()
                D(dve.tensor_tensor(z[5], z[5], z[6], ALU.add))
                yield
                D.wait()
                D(dve.tensor_tensor(z[5], z[5], e4, ALU.add))
                yield
                D.wait()
                D(dve.tensor_scalar(rsu[:, t], z[5], 0.5, None, ALU.mult))
                yield
                D.wait()
                dve.tensor_scalar(z[7], rsu[:, t], -1.0, lsc[:, 2:3], ALU.mult, ALU.add).then_inc(s_coef, 1)
                yield

            def post_e(c):
                t = bass.ds(c * CT, CT)
                yield from scaled_rows(c)
                pu, m = ev2[:, :, 0, :], ev2[:, :, 1, :]
                yield
                D(dve.scalar_tensor_tensor(out=odd[:], in0=pu, scalar=nc3[:, 0:1], in1=xh[:, t, :], op0=ALU.mult, op1=ALU.add))
                yield
                D.wait()
                for q in range(CT):
                    if q == 2:
                        yield
                    D(dve.scalar_tensor_tensor(out=m[:, q], in0=odd[:, q], scalar=rsu[:, bass.ds(c * CT + q, 1)],
                                               in1=pu[:, q], op0=ALU.mult, op1=ALU.add))
                yield
                dve.wait_ge(s_h0x, c + 1)
                D(dve.scalar_tensor_tensor(out=chunk_of(c), in0=odd[:], scalar=k12[:, 0:1], in1=chunk_of(c), op0=ALU.mult, op1=ALU.add))
                yield
                D.wait()
                dve.scalar_tensor_tensor(out=chunk_of(c), in0=m, scalar=ls[:, 1:2], in1=chunk_of(c), op0=ALU.mult,
                                         op1=ALU.add).then_inc(s_post[1], 1)
                yield
                wait_alone(dve, need, s_post[1], c + 1)
                yield from statistics(chunk_of(c))

            def part_d(what, c):
                return products_out(0, c) if what == "out" else post_d(c)

            def part_e(what, c):
                if what in ("out", "post"):
                    return products_out(1, c) if what == "out" else post_e(c)
                return routing(1, what, c)

            def chunk_d(c, slot, tail, next_nf1, first=False, last=False):
                def tile(jt):
                    if first and jt and jt % CT == 0:
                        operands_d(jt // CT)
                    if jt == NT - AHEAD and not last:
                        dve.wait_ge(s_nfl[1 - slot], next_nf1)
                    code_ahead(c, jt, slot, last)
                    if jt % 8 not in BY_ACT:
                        other(0, c, jt, first)

                if tail is None:
                    for jt in range(NT):
                        tile(jt)
                else:
                    between(D_DVE, part_d, tail, tile, lambda jt: 1)

            operands_d(0)
            dve.wait_ge(s_nfl[0], 16)
            for jt in range(AHEAD):
                code(0, jt, 0)
            chunk_d(0, 0, None, 16, first=True)
            with D.loop((NC - 2) // 2, 32) as lap:
                chunk_d(lap * 2 + 1, 1, lap * 2, lap * 16 + 32)
                chunk_d(lap * 2 + 2, 0, lap * 2 + 1, lap * 16 + 32)
            chunk_d(NC - 1, 1, NC - 2, None, last=True)
            dve.wait_ge(s_mu[0], NC * NT)
            between({0: "out", 1: "post"}, part_d, NC - 1, lambda jt: other(1, 0, jt, True), lambda jt: 2)
            dve.wait_ge(s_csp, 2)
            D(dve.tensor_copy(cs[:], PG[:, 0:P]))
            with D.loop(NC - 1, 48) as t:
                between(E_DVE, part_e, t, lambda jt: other(1, t + 1, jt, False),
                        lambda jt: 1 + (jt > 21))
            behind(E_DVE, part_e, NC - 1)
            tile_table(1)
            weights(1)
            experts(1)
            dve.wait_ge(s_cxh, NC)
            for p in range(NC // 2 + 1):
                if p < NC // 2:
                    combine(1, (2 * p, 2 * p + 1), p // 2, p % 2 * 2)
                if p:
                    for c in (2 * p - 2, 2 * p - 1):
                        dve.wait_ge(s_norm, CT * (c + 1))
                        y = xh[:, c * CT:(c + 1) * CT]
                        dve.tensor_tensor(y, y, gam[:].unsqueeze(1).broadcast_to([P, CT, P]), ALU.mult).then_inc(s_gm, 1)


def kernel(**inputs):
    import concourse.bacc as bacc
    from concourse.bass_utils import run_bass_kernel_spmd

    v = {k: np.asarray(w) for k, w in inputs.items()}

    def split_tiles(w):
        return w.reshape(E, 2, P, P).transpose(2, 0, 1, 3)

    adj = v["adj"].T.reshape(NG, CT, P, NC, CW).transpose(3, 0, 2, 1, 4).reshape(NC * NG, P, CT * CW)
    arrays = {
        "x": v["x"],
        "adjT": adj,
        "x2": v["L0_gnn_x2"],
        "eps": np.concatenate([v["L0_gnn_eps1"], v["L0_gnn_eps2"]]),
        "WT": np.concatenate([v["L0_gnn_W1"], v["L0_gnn_W2"]]).transpose(2, 0, 1),
        "bT": np.concatenate([v["L0_gnn_b1"], v["L0_gnn_b2"]]).T,
        "WmT": v["L0_gnn_Wm"].T.reshape(2, P, P).transpose(1, 0, 2),
        "bm": v["L0_gnn_bm"],
        "gate_w": np.stack([v["L0_ffn_gate_w"], v["L1_ffn_gate_w"]], axis=1),
        "gate_b": np.stack([v["L0_ffn_gate_b"], v["L1_ffn_gate_b"]]),
        "w12": np.concatenate([v["L0_ffn_w1"], v["L0_ffn_w2"]], axis=2).transpose(1, 0, 2),
        "w3": split_tiles(v["L0_ffn_w3"]),
        "h0": v["L1_gnn_h0"],
        "a": v["L1_gnn_a"].reshape(2, P).T,
        "temp": v["L1_gnn_temp"],
        "ew1": v["L1_ffn_w1"].transpose(1, 0, 2),
        "eb1": v["L1_ffn_b1"].reshape(E, 2, P).transpose(2, 0, 1),
        "ew2": split_tiles(v["L1_ffn_w2"]),
        "eb2": v["L1_ffn_b2"],
        "gamma": v["L1_ffn_gamma"],
        "beta": v["L1_ffn_beta"],
    }
    arrays = {f"in_{k}": np.ascontiguousarray(w) for k, w in arrays.items()}
    nc = bacc.Bacc("TRN2", target_bir_lowering=False, num_devices=1)
    args = [nc.dram_tensor(k, w.shape, mybir.dt.from_np(w.dtype), kind="ExternalInput").ap() for k, w in arrays.items()]
    out = nc.dram_tensor("out_dram", (N, P), F32, kind="ExternalOutput").ap()
    bass_gnn_moe_kernel(nc, *args, out)
    return run_bass_kernel_spmd(nc, [arrays], core_ids=[0]).results[0]["out_dram"]
```
